# Optimizing a Trainium2 kernel written in Bass

```python
import numpy as np
import jax
import jax.numpy as jnp

def _softmax(x, axis=-1):
    return jax.nn.softmax(x, axis=axis)

def _gelu(x):
    return jax.nn.gelu(x, approximate=True)

def _silu(x):
    return jax.nn.silu(x)

def _sigmoid(x):
    return jax.nn.sigmoid(x)

def _layernorm(x, axis=-1, eps=1e-05):
    m = jnp.mean(x, axis=axis, keepdims=True)
    v = jnp.var(x, axis=axis, keepdims=True)
    return (x - m) / jnp.sqrt(v + eps)

def _scatter_add(tgt, idx, src, axis=0):
    return tgt.at[idx].add(src)

def _segment_sum(src, seg, n):
    return jax.ops.segment_sum(src, seg, n)
kernel_name = 'mk_sandwich_d2_jaxref_r8_636d6a'

def setup_inputs(seed: int=0):
    np.random.seed(seed)
    _w = jnp.asarray

    def _L0_attn_setup():
        import jax, jax.numpy as jnp
        import numpy as np
        key = jax.random.key(seed)
        kx, kf = jax.random.split(key)
        x = jax.random.normal(kx, (4, 1024, 128), dtype=jnp.float32)
        filt = jax.random.normal(kf, (256,), dtype=jnp.float32)
        return {'x': x, 'filt': filt}
    _L0_attn_in = _L0_attn_setup()

    def _L0_ffn_setup():
        import jax, jax.numpy as jnp
        import numpy as np
        DIM = 128
        DEPTH = 2
        HEADS = 8
        DIM_HEAD = 64
        WINDOW = 64
        INNER = HEADS * DIM_HEAD
        HID = int(DIM * 4 * 2 / 3)
        B, N = (2, 1024)
        QK_SCALE = 8.0

        def shift_token(t):
            t1, t2 = jnp.split(t, 2, axis=-1)
            t2 = jnp.pad(t2, ((0, 0), (1, 0), (0, 0)))[:, :-1]
            return jnp.concatenate([t1, t2], axis=-1)

        def l2norm(t):
            return t / jnp.clip(jnp.linalg.norm(t, axis=-1, keepdims=True), 1e-12)

        def rotate_half(x):
            x1, x2 = jnp.split(x, 2, axis=-1)
            return jnp.concatenate([-x2, x1], axis=-1)

        def rotary_xpos(q, k):
            n = q.shape[-2]
            half_idx = jnp.arange(0, DIM_HEAD, 2, dtype=jnp.float32)
            inv_freq = 1.0 / 10000.0 ** (half_idx / DIM_HEAD)
            t = jnp.arange(n, dtype=jnp.float32)
            freqs = t[:, None] * inv_freq[None, :]
            freqs = jnp.concatenate([freqs, freqs], axis=-1)
            base = (half_idx + 0.4 * DIM_HEAD) / (1.4 * DIM_HEAD)
            power = (t - n // 2) / float(WINDOW // 2)
            scale = base[None, :] ** power[:, None]
            scale = jnp.concatenate([scale, scale], axis=-1)
            cos, sin = (jnp.cos(freqs), jnp.sin(freqs))
            q = q * cos * scale + rotate_half(q) * sin * scale
            k = k * cos / scale + rotate_half(k) * sin / scale
            return (q, k)

        def local_attention(q, k, v):
            b, h, n, d = q.shape
            w = n // WINDOW
            bq = q.reshape(b, h, w, WINDOW, d) * QK_SCALE
            bk = k.reshape(b, h, w, WINDOW, d)
            bv = v.reshape(b, h, w, WINDOW, d)

            def look_around(t):
                p = jnp.pad(t, ((0, 0), (0, 0), (1, 0), (0, 0), (0, 0)))
                return jnp.concatenate([p[:, :, :w], p[:, :, 1:]], axis=3)
            bk, bv = (look_around(bk), look_around(bv))
            bt = jnp.arange(n).reshape(w, WINDOW)
            btp = jnp.pad(bt, ((1, 0), (0, 0)), constant_values=-1)
            btk = jnp.concatenate([btp[:w], btp[1:]], axis=1)
            sim = jnp.einsum('bhwid,bhwjd->bhwij', bq, bk)
            i = bt[:, :, None]
            j = btk[:, None, :]
            mask = (i < j) | (i > j + WINDOW) | (j == -1)
            sim = jnp.where(mask, -jnp.finfo(sim.dtype).max, sim)
            attn = jax.nn.softmax(sim, axis=-1)
            out = jnp.einsum('bhwij,bhwjd->bhwid', attn, bv)
            return out.reshape(b, h, n, d)

        def _layer(x, wqkv, qs, ksc, wo, lg, lb, w1, b1, w2, b2):
            b, n, _ = x.shape
            h = shift_token(x)
            qkv = h @ wqkv
            q, k, v = jnp.split(qkv, 3, axis=-1)
            to_heads = lambda t: t.reshape(b, n, HEADS, DIM_HEAD).transpose(0, 2, 1, 3)
            q, k, v = (to_heads(q), to_heads(k), to_heads(v))
            q = l2norm(q) * qs
            k = l2norm(k) * ksc
            q, k = rotary_xpos(q, k)
            o = local_attention(q, k, v)
            o = o.transpose(0, 2, 1, 3).reshape(b, n, INNER)
            x = x + o @ wo
            h = shift_token(x)
            mu = h.mean(-1, keepdims=True)
            var = h.var(-1, keepdims=True)
            h = (h - mu) / jnp.sqrt(var + 1e-05) * lg + lb
            h = h @ w1 + b1
            a, g = jnp.split(h, 2, axis=-1)
            h = a * jax.nn.gelu(g, approximate=False)
            x = x + h @ w2 + b2
            return x
        key = jax.random.key(seed)
        ks = jax.random.split(key, 6)
        return {'x': jax.random.normal(ks[0], (B, N, DIM), jnp.float32), 'wqkv': jax.random.normal(ks[1], (DEPTH, DIM, 3 * INNER), jnp.float32) * 0.02, 'q_scale': jnp.ones((DEPTH, DIM_HEAD), jnp.float32), 'k_scale': jnp.ones((DEPTH, DIM_HEAD), jnp.float32), 'wo': jax.random.normal(ks[2], (DEPTH, INNER, DIM), jnp.float32) * 0.02, 'ln_g': jnp.ones((DEPTH, DIM), jnp.float32), 'ln_b': jnp.zeros((DEPTH, DIM), jnp.float32), 'w1': jax.random.normal(ks[3], (DEPTH, DIM, 2 * HID), jnp.float32) * 0.02, 'b1': jnp.zeros((DEPTH, 2 * HID), jnp.float32), 'w2': jax.random.normal(ks[4], (DEPTH, HID, DIM), jnp.float32) * 0.02, 'b2': jnp.zeros((DEPTH, DIM), jnp.float32)}
    _L0_ffn_in = _L0_ffn_setup()

    def _L1_attn_setup():
        import jax, jax.numpy as jnp
        import numpy as np
        N_EMBD = 128
        N_HEAD = 16
        B, T = (4, 256)
        key = jax.random.key(seed)
        ks = jax.random.split(key, 4)
        s = 1.0 / np.sqrt(N_EMBD)
        return {'x': jax.random.normal(ks[0], (B, T, N_EMBD), dtype=jnp.float32), 'w_attn': jax.random.normal(ks[1], (N_EMBD, 3 * N_EMBD), dtype=jnp.float32) * s, 'b_attn': jnp.zeros((3 * N_EMBD,), dtype=jnp.float32), 'w_proj': jax.random.normal(ks[2], (N_EMBD, N_EMBD), dtype=jnp.float32) * s, 'b_proj': jnp.zeros((N_EMBD,), dtype=jnp.float32)}
    _L1_attn_in = _L1_attn_setup()

    def _L1_ffn_setup():
        import jax, jax.numpy as jnp
        import numpy as np
        TOP_K = 2
        key = jax.random.key(seed)
        ks = jax.random.split(key, 8)
        B, S, D = (2, 256, 128)
        N_r, N_s = (16, 2)
        u = jax.random.normal(ks[0], (B, S, D), dtype=jnp.float32)
        centroids = jax.random.normal(ks[1], (N_r, D), dtype=jnp.float32)
        expert_biases = jnp.zeros((N_r,), dtype=jnp.float32)
        Wr = jax.random.normal(ks[2], (N_r, D, D), dtype=jnp.float32) * (1.0 / np.sqrt(D))
        br = jax.random.normal(ks[3], (N_r, D), dtype=jnp.float32) * 0.01
        Ws = jax.random.normal(ks[4], (N_s, D, D), dtype=jnp.float32) * (1.0 / np.sqrt(D))
        bs = jax.random.normal(ks[5], (N_s, D), dtype=jnp.float32) * 0.01
        return {'u': u, 'centroids': centroids, 'expert_biases': expert_biases, 'Wr': Wr, 'br': br, 'Ws': Ws, 'bs': bs}
    _L1_ffn_in = _L1_ffn_setup()
    _d = {'L0_attn_x': _L0_attn_in['x'], 'L0_attn_filt': _L0_attn_in['filt'], 'L0_ffn_wqkv': _L0_ffn_in['wqkv'], 'L0_ffn_q_scale': _L0_ffn_in['q_scale'], 'L0_ffn_k_scale': _L0_ffn_in['k_scale'], 'L0_ffn_wo': _L0_ffn_in['wo'], 'L0_ffn_ln_g': _L0_ffn_in['ln_g'], 'L0_ffn_ln_b': _L0_ffn_in['ln_b'], 'L0_ffn_w1': _L0_ffn_in['w1'], 'L0_ffn_b1': _L0_ffn_in['b1'], 'L0_ffn_w2': _L0_ffn_in['w2'], 'L0_ffn_b2': _L0_ffn_in['b2'], 'L1_attn_w_attn': _L1_attn_in['w_attn'], 'L1_attn_b_attn': _L1_attn_in['b_attn'], 'L1_attn_w_proj': _L1_attn_in['w_proj'], 'L1_attn_b_proj': _L1_attn_in['b_proj'], 'L1_ffn_centroids': _L1_ffn_in['centroids'], 'L1_ffn_expert_biases': _L1_ffn_in['expert_biases'], 'L1_ffn_Wr': _L1_ffn_in['Wr'], 'L1_ffn_br': _L1_ffn_in['br'], 'L1_ffn_Ws': _L1_ffn_in['Ws'], 'L1_ffn_bs': _L1_ffn_in['bs']}
    _x0 = _d['L0_attn_x']
    _d['L0_attn_x'] = jax.random.normal(jax.random.fold_in(jax.random.key(seed), 1), (16, 512, 128), dtype=_x0.dtype)
    del _x0
    return _d

def reference(L0_attn_x, L0_attn_filt, L0_ffn_wqkv, L0_ffn_q_scale, L0_ffn_k_scale, L0_ffn_wo, L0_ffn_ln_g, L0_ffn_ln_b, L0_ffn_w1, L0_ffn_b1, L0_ffn_w2, L0_ffn_b2, L1_attn_w_attn, L1_attn_b_attn, L1_attn_w_proj, L1_attn_b_proj, L1_ffn_centroids, L1_ffn_expert_biases, L1_ffn_Wr, L1_ffn_br, L1_ffn_Ws, L1_ffn_bs):

    def _L0_attn_ref(x, filt):
        import jax, jax.numpy as jnp
        import numpy as np
        batch, seq, dim = x.shape
        L = filt.shape[0]
        pad = seq + L - 1
        xt = jnp.swapaxes(x, 1, 2)
        fx = jnp.fft.rfft(xt, n=pad, axis=-1)
        ff = jnp.fft.rfft(filt[::-1], n=pad)
        conv = jnp.fft.irfft(fx * ff, n=pad, axis=-1)
        conv = conv[:, :, L - 1:L - 1 + seq]
        return jnp.swapaxes(conv, 1, 2)

    def _L0_ffn_ref(x, wqkv, q_scale, k_scale, wo, ln_g, ln_b, w1, b1, w2, b2):
        import jax, jax.numpy as jnp
        import numpy as np
        DIM = 128
        DEPTH = 2
        HEADS = 8
        DIM_HEAD = 64
        WINDOW = 64
        INNER = HEADS * DIM_HEAD
        HID = int(DIM * 4 * 2 / 3)
        B, N = (2, 1024)
        QK_SCALE = 8.0

        def shift_token(t):
            t1, t2 = jnp.split(t, 2, axis=-1)
            t2 = jnp.pad(t2, ((0, 0), (1, 0), (0, 0)))[:, :-1]
            return jnp.concatenate([t1, t2], axis=-1)

        def l2norm(t):
            return t / jnp.clip(jnp.linalg.norm(t, axis=-1, keepdims=True), 1e-12)

        def rotate_half(x):
            x1, x2 = jnp.split(x, 2, axis=-1)
            return jnp.concatenate([-x2, x1], axis=-1)

        def rotary_xpos(q, k):
            n = q.shape[-2]
            half_idx = jnp.arange(0, DIM_HEAD, 2, dtype=jnp.float32)
            inv_freq = 1.0 / 10000.0 ** (half_idx / DIM_HEAD)
            t = jnp.arange(n, dtype=jnp.float32)
            freqs = t[:, None] * inv_freq[None, :]
            freqs = jnp.concatenate([freqs, freqs], axis=-1)
            base = (half_idx + 0.4 * DIM_HEAD) / (1.4 * DIM_HEAD)
            power = (t - n // 2) / float(WINDOW // 2)
            scale = base[None, :] ** power[:, None]
            scale = jnp.concatenate([scale, scale], axis=-1)
            cos, sin = (jnp.cos(freqs), jnp.sin(freqs))
            q = q * cos * scale + rotate_half(q) * sin * scale
            k = k * cos / scale + rotate_half(k) * sin / scale
            return (q, k)

        def local_attention(q, k, v):
            b, h, n, d = q.shape
            w = n // WINDOW
            bq = q.reshape(b, h, w, WINDOW, d) * QK_SCALE
            bk = k.reshape(b, h, w, WINDOW, d)
            bv = v.reshape(b, h, w, WINDOW, d)

            def look_around(t):
                p = jnp.pad(t, ((0, 0), (0, 0), (1, 0), (0, 0), (0, 0)))
                return jnp.concatenate([p[:, :, :w], p[:, :, 1:]], axis=3)
            bk, bv = (look_around(bk), look_around(bv))
            bt = jnp.arange(n).reshape(w, WINDOW)
            btp = jnp.pad(bt, ((1, 0), (0, 0)), constant_values=-1)
            btk = jnp.concatenate([btp[:w], btp[1:]], axis=1)
            sim = jnp.einsum('bhwid,bhwjd->bhwij', bq, bk)
            i = bt[:, :, None]
            j = btk[:, None, :]
            mask = (i < j) | (i > j + WINDOW) | (j == -1)
            sim = jnp.where(mask, -jnp.finfo(sim.dtype).max, sim)
            attn = jax.nn.softmax(sim, axis=-1)
            out = jnp.einsum('bhwij,bhwjd->bhwid', attn, bv)
            return out.reshape(b, h, n, d)

        def _layer(x, wqkv, qs, ksc, wo, lg, lb, w1, b1, w2, b2):
            b, n, _ = x.shape
            h = shift_token(x)
            qkv = h @ wqkv
            q, k, v = jnp.split(qkv, 3, axis=-1)
            to_heads = lambda t: t.reshape(b, n, HEADS, DIM_HEAD).transpose(0, 2, 1, 3)
            q, k, v = (to_heads(q), to_heads(k), to_heads(v))
            q = l2norm(q) * qs
            k = l2norm(k) * ksc
            q, k = rotary_xpos(q, k)
            o = local_attention(q, k, v)
            o = o.transpose(0, 2, 1, 3).reshape(b, n, INNER)
            x = x + o @ wo
            h = shift_token(x)
            mu = h.mean(-1, keepdims=True)
            var = h.var(-1, keepdims=True)
            h = (h - mu) / jnp.sqrt(var + 1e-05) * lg + lb
            h = h @ w1 + b1
            a, g = jnp.split(h, 2, axis=-1)
            h = a * jax.nn.gelu(g, approximate=False)
            x = x + h @ w2 + b2
            return x
        for l in range(DEPTH):
            x = _layer(x, wqkv[l], q_scale[l], k_scale[l], wo[l], ln_g[l], ln_b[l], w1[l], b1[l], w2[l], b2[l])
        return x

    def _L1_attn_ref(x, w_attn, b_attn, w_proj, b_proj):
        import jax, jax.numpy as jnp
        import numpy as np
        N_EMBD = 128
        N_HEAD = 16
        B, T = (4, 256)
        Bb, Tt, C = x.shape
        H = N_HEAD
        D = C // H
        qkv = x @ w_attn + b_attn
        q, k, v = jnp.split(qkv, 3, axis=2)
        q = q.reshape(Bb, Tt, H, D).transpose(0, 2, 1, 3)
        k = k.reshape(Bb, Tt, H, D).transpose(0, 2, 1, 3)
        v = v.reshape(Bb, Tt, H, D).transpose(0, 2, 1, 3)
        scale = 1.0 / np.sqrt(D).astype(np.float32)
        attn = jnp.einsum('bhqd,bhkd->bhqk', q, k) * scale
        mask = jnp.tril(jnp.ones((Tt, Tt), dtype=bool))
        attn = jnp.where(mask, attn, jnp.float32(-jnp.inf))
        probs = jax.nn.softmax(attn, axis=-1)
        out = jnp.einsum('bhqk,bhkd->bhqd', probs, v)
        out = out.transpose(0, 2, 1, 3).reshape(Bb, Tt, C)
        return out @ w_proj + b_proj

    def _L1_ffn_ref(u, centroids, expert_biases, Wr, br, Ws, bs):
        import jax, jax.numpy as jnp
        import numpy as np
        TOP_K = 2
        N_r = centroids.shape[0]
        N_s = Ws.shape[0]
        raw_scores = jnp.einsum('bsd,ed->bse', u, centroids)
        s = jax.nn.softmax(raw_scores + expert_biases, axis=-1)
        topk_vals, topk_idx = jax.lax.top_k(s, TOP_K)
        g_topk = jnp.sum(jax.nn.one_hot(topk_idx, N_r, dtype=s.dtype) * topk_vals[..., None], axis=-2)
        xe = jnp.einsum('bsd,eod->bseo', u, Wr) + br
        routed = jnp.einsum('bse,bseo->bso', g_topk, xe)
        shared = (jnp.einsum('bsd,eod->bso', u, Ws) + jnp.sum(bs, axis=0)) / N_s
        return u + routed + shared
    x = L0_attn_x
    x = x + _layernorm(_L0_attn_ref(_layernorm(x, axis=-1), L0_attn_filt), axis=-1)
    x = x + _layernorm(_L0_ffn_ref(_layernorm(x, axis=-1), L0_ffn_wqkv, L0_ffn_q_scale, L0_ffn_k_scale, L0_ffn_wo, L0_ffn_ln_g, L0_ffn_ln_b, L0_ffn_w1, L0_ffn_b1, L0_ffn_w2, L0_ffn_b2), axis=-1)
    x = x + _layernorm(_L1_attn_ref(_layernorm(x, axis=-1), L1_attn_w_attn, L1_attn_b_attn, L1_attn_w_proj, L1_attn_b_proj), axis=-1)
    x = x + _layernorm(_L1_ffn_ref(_layernorm(x, axis=-1), L1_ffn_centroids, L1_ffn_expert_biases, L1_ffn_Wr, L1_ffn_br, L1_ffn_Ws, L1_ffn_bs), axis=-1)
    return x

_drawn_inputs = setup_inputs


def setup_inputs(seed=0):
    import zlib

    import numpy as np

    out = dict(_drawn_inputs(seed))
    spreads = {'L0_ffn_q_scale': (1.0, 0.6),
     'L0_ffn_k_scale': (1.0, 0.6),
     'L0_ffn_ln_g': (1.0, 0.6),
     'L0_ffn_ln_b': (0.0, 0.8),
     'L0_ffn_b1': (0.0, 0.8),
     'L0_ffn_b2': (0.0, 0.318),
     'L1_attn_b_attn': (0.0, 0.1),
     'L1_attn_b_proj': (0.0, 0.1),
     'L1_ffn_expert_biases': (0.0, 0.8)}
    factors = {'L0_ffn_wqkv': 2.808,
     'L0_ffn_wo': 2.813,
     'L0_ffn_w1': 5.662,
     'L0_ffn_w2': 5.481,
     'L1_ffn_br': 25.947,
     'L1_ffn_bs': 30.478}
    for name, (base, spread) in spreads.items():
        noise = np.random.default_rng([zlib.crc32(name.encode()), seed]).standard_normal(out[name].shape)
        drawn = base * np.exp(spread * noise) if base else spread * noise
        out[name] = jnp.asarray(drawn.astype(out[name].dtype))
    for name, factor in factors.items():
        out[name] = (out[name] * factor).astype(out[name].dtype)
    return out
```

```python
from contextlib import ExitStack

import numpy as np

import concourse.bass as bass
from concourse import mybir

F32 = mybir.dt.float32
BF16 = mybir.dt.bfloat16
ALU = mybir.AluOpType
ACT = mybir.ActivationFunctionType
AX = mybir.AxisListType.X

P = 128
D = 128
TB = 4
SEQ = TB * P
EPS = 1e-5
MASKED = -1e30


class Steps:

    def __init__(self, sem, per=1):
        self.sem, self.per = sem, per

    def at(self, n, k=None):
        return n * self.per + (self.per if k is None else k)


def settle(eng, ready):
    eng.sem_inc(ready.sem, 1)


def back(b, t, k, unroll):
    return (b, t - k) if t >= k else (b - 1, t - k + unroll)


def program(nc, x, filt, wqkv, qsc, ksc, wo, lng, lnb, w1, b1, w2, b2, wat, bat, wpr, bpr, cenT, ebias,
            wrT, br, wsT, bs, rot, masks, out, stop=99):
    NB = x.shape[0]
    DEPTH = wqkv.shape[0]
    NT = NB * TB
    HEADS, DH = 8, 64
    WIN = 64
    HID = w2.shape[1]
    CH = [min(P, HID - P * c) for c in range(-(-HID // P))]
    NC_ = len(CH)
    TAPS = filt.shape[0]
    H2, D2 = 16, 8
    NE = wrT.shape[1]
    assert x.shape[1:] == (SEQ, D) and TAPS == 2 * P and NB % 4 == 0 and NC_ == 3

    pad = nc.dram_tensor("filter_padded", [4 * P], F32, kind="Internal").ap()
    split_dram = nc.dram_tensor("qk_split", [NB, 2, 3, D, SEQ], BF16, kind="Internal").ap()

    with ExitStack() as whole:
        def sb(name, shape, dt=F32, ctx=whole):
            return ctx.enter_context(nc.sbuf_tensor(name, shape, dt))

        def ps(name, shape, ctx, dt=F32):
            return ctx.enter_context(nc.psum_tensor(name, shape, dt))

        def steps(name, per=1):
            return Steps(whole.enter_context(nc.semaphore(name)), per)

        X = sb("X", [P, NT, D])
        S = sb("S", [P, NT, D])
        ident = sb("ident", [P, P])
        mk = sb("mk", [P, 5, P], BF16)
        mhalf = sb("mhalf", [P, 16])
        ready = steps("marks")

        class Norm:

            def __init__(self, name, ctx, pieces=1):
                self.pieces = pieces
                self.st = sb(name + "_st", [P, TB, pieces, 6], ctx=ctx)
                self.mv = sb(name + "_mv", [P, TB, 2], ctx=ctx)
                self.ve = sb(name + "_ve", [P, TB], ctx=ctx)
                self.rs = sb(name + "_rs", [P, TB], ctx=ctx)
                self.done = steps(name + "_var", 3)
                self.rstd = steps(name + "_rstd")

            def stats(self, dve, n, pieces):
                settle(dve, ready)
                for t in range(TB):
                    for k, piece in enumerate(pieces(t)):
                        last = dve.bn_stats(self.st[:, t, k, :], piece)
                last.then_inc(self.done.sem, 1)
                dve.wait_ge(self.done.sem, self.done.at(n, 1))
                settle(dve, ready)
                for t in range(TB):
                    last = dve.bn_aggr(self.mv[:, t, :], self.st[:, t, :, :].rearrange("p k s -> p (k s)"))
                last.then_inc(self.done.sem, 1)
                dve.wait_ge(self.done.sem, self.done.at(n, 2))
                dve.tensor_scalar(self.ve[:, :], self.mv[:, :, 1], EPS, None, ALU.add).then_inc(self.done.sem, 1)

            def power(self, pool, n):
                pool.wait_ge(self.done.sem, self.done.at(n))
                pool.tensor_tensor(self.rs[:, :], self.ve[:, :], mhalf[:, 0:TB], ALU.pow).then_inc(self.rstd.sem, 1)

            def apply(self, dve, n, outs, pieces):
                dve.wait_ge(self.rstd.sem, self.rstd.at(n))
                for t in range(TB):
                    for o, i in zip(outs(t), pieces(t)):
                        last = dve.tensor_scalar(o, i, self.mv[:, t, 0:1], self.rs[:, t:t + 1],
                                                 ALU.subtract, ALU.mult)
                return last

        with ExitStack() as ctx:
            hank = sb("hankel", [P, 3 * P], ctx=ctx)
            toep = sb("toeplitz", [P, 3, P], ctx=ctx)
            zero = sb("zero_row", [1, P], ctx=ctx)
            mkf = sb("masks_f32", [P, 5, P], ctx=ctx)
            Y = [sb(f"conv_in{u}", [P, SEQ], ctx=ctx) for u in range(2)]
            T = sb("conv_normed", [P, TB, D], ctx=ctx)
            C = [ps(f"conv_out{u}", [P, SEQ], ctx) for u in range(2)]
            lnA, lnB, lnC = (Norm(f"ln{c}", ctx) for c in "abc")
            consts = steps("constants")
            x_in = [steps(f"x_in{j}") for j in range(4)]
            zeroed = steps("zeroed")
            padded = steps("padded")
            hank_in = steps("hankel_in")
            toep_ok = steps("toeplitz_built")
            half_ok = steps("half_set")
            y_ok = steps("conv_in_ready")
            conv = steps("conv_done")
            t_ok = steps("conv_normed_ready")
            x_ok = steps("x_updated")
            s_ok = steps("stream_ready")
            XV = x.rearrange("b (t p) d -> b p t d", p=P)

            with nc.Block() as block:
                @block.sync
                def _(sp):
                    sp.wait_ge(zeroed.sem, 1)
                    for o in (0, 3 * P):
                        sp.dma_start(pad[o:o + P].rearrange("(a n) -> a n", a=1), zero[:, :]).then_inc(padded.sem, 16)
                    sp.dma_start(pad[P:3 * P].rearrange("(a n) -> a n", a=1),
                                 filt.rearrange("(a n) -> a n", a=1)).then_inc(padded.sem, 16)
                    sp.wait_ge(padded.sem, 48)
                    rows = bass.AP(pad.tensor, 1, [[1, P], [1, 3 * P]])
                    sp.dma_start(hank[:, :], rows).then_inc(hank_in.sem, 16)

                @block.scalar
                def _(act):
                    act.dma_start(ident[:, :], masks[1]).then_inc(consts.sem, 16)
                    act.dma_start(mkf[:, :, :], masks[0]).then_inc(consts.sem, 16)

                    def load(b, j):
                        act.dma_start(X[:, bass.ds(b * TB, TB), :], XV[b]).then_inc(x_in[j].sem, 16)
                    for j in range(4):
                        load(j, j)
                    with act.Fori(1, NB // 4) as g:
                        for j in range(4):
                            act.wait_ge(lnA.done.sem, lnA.done.at(g * 4 + j - 4))
                            load(g * 4 + j, j)
                    act.wait_ge(consts.sem, 32)
                    act.activation(mk[:, :, :], mkf[:, :, :], ACT.Copy)

                @block.gpsimd
                def _(pool):
                    pool.memset(mhalf[:, :], -0.5).then_inc(half_ok.sem, 1)
                    pool.wait_ge(half_ok.sem, 1)

                    def slot(b, first):
                        lnA.power(pool, b)
                        if not first:
                            lnC.power(pool, b - 1)
                        lnB.power(pool, b)
                    slot(0, True)
                    with pool.Fori(1, NB) as b:
                        slot(b, False)
                    lnC.power(pool, NB - 1)

                @block.vector
                def _(dve):
                    dve.memset(zero[:, :], 0.0).then_inc(zeroed.sem, 1)
                    dve.wait_ge(hank_in.sem, 16)
                    for j in range(3):
                        last = dve.tensor_copy(toep[:, j, :], hank[:, j * P:(j + 1) * P][:, ::-1])
                    last.then_inc(toep_ok.sem, 1)

                    def first_norm(b, j, fresh):
                        xt = lambda t: [X[:, b * TB + t, :]]
                        if fresh is not None:
                            dve.wait_ge(x_in[j].sem, fresh)
                        lnA.stats(dve, b, xt)

                    def residual(b, u):
                        lnB.apply(dve, b, lambda t: [T[:, t, :]], lambda t: [C[u][:, t * P:(t + 1) * P]])\
                            .then_inc(t_ok.sem, 1)
                        dve.wait_ge(t_ok.sem, t_ok.at(b))
                        dve.tensor_tensor(X[:, bass.ds(b * TB, TB), :], X[:, bass.ds(b * TB, TB), :], T[:, :, :],
                                          ALU.add).then_inc(x_ok.sem, 1)
                        dve.wait_ge(x_ok.sem, x_ok.at(b))
                        lnC.stats(dve, b, lambda t: [X[:, b * TB + t, :]])

                    def stream(b):
                        lnC.apply(dve, b, lambda t: [S[:, b * TB + t, :]], lambda t: [X[:, b * TB + t, :]])\
                            .then_inc(s_ok.sem, 1)

                    def slot(b, j, loads, first, warm):
                        u = j % 2
                        first_norm(b, j, loads)
                        if not first:
                            residual(b - 1, 1 - u)
                        if warm:
                            dve.wait_ge(conv.sem, conv.at(b - 2))
                        lnA.apply(dve, b, lambda t: [Y[u][:, t * P:(t + 1) * P]], lambda t: [X[:, b * TB + t, :]])\
                            .then_inc(y_ok.sem, 1)
                        if not first:
                            stream(b - 1)
                        dve.wait_ge(conv.sem, conv.at(b))
                        lnB.stats(dve, b, lambda t: [C[u][:, t * P:(t + 1) * P]])

                    for j in range(4):
                        slot(j, j, 16, j == 0, j >= 2)
                    with dve.Fori(1, NB // 4) as g:
                        for j in range(4):
                            slot(g * 4 + j, j, g * 16 + 16, False, True)
                    residual(NB - 1, 1)
                    stream(NB - 1)

                @block.tensor
                def _(pe):
                    pe.wait_ge(toep_ok.sem, 1)

                    def slot(b, u, warm):
                        pe.wait_ge(y_ok.sem, y_ok.at(b))
                        if warm:
                            pe.wait_ge(t_ok.sem, t_ok.at(b - 2))
                        for j in range(3):
                            last = pe.matmul(C[u][:, 0:(TB - j) * P], toep[:, j, :], Y[u][:, j * P:SEQ],
                                             start=(j == 0), stop=(j == 2), skip_group_check=True)
                        last.then_inc(conv.sem, 1)
                    slot(0, 0, False)
                    slot(1, 1, False)
                    with pe.Fori(1, NB // 2) as g:
                        for u in range(2):
                            slot(g * 2 + u, u, True)

        if stop <= 1:
            return dump(nc, out, S if stop else X, NB)

        with ExitStack() as layers:
            rotc = sb("rot_const", [P, TB, 4, DH], ctx=layers)
            rot_in = steps("rot_in")
            shiftm = sb("shift", [P, 2, P], ctx=layers)
            shift_in = steps("shift_in")
            VN = [sb(f"v{t}", [P, HEADS, DH + 1], ctx=layers) for t in range(TB)]
            KZ = [sb(f"kz{u}", [P, HEADS, P], ctx=layers) for u in range(2)]
            HT = [sb(f"ht{t}", [P, P], ctx=layers) for t in range(TB)]
            zcol = sb("zero_col", [P, 1], ctx=layers)
            init = steps("layers_init")
            with nc.Block() as block:
                @block.sync
                def _(sp):
                    sp.dma_start(rotc[:, :, :, :], rot).then_inc(rot_in.sem, 16)
                    for k in range(2):
                        sp.dma_start(shiftm[:, k, :], masks[2 + k]).then_inc(shift_in.sem, 16)
                    sp.wait_ge(rot_in.sem, 16)
                    sp.wait_ge(shift_in.sem, 32)

                @block.vector
                def _(dve):
                    for v in VN:
                        dve.memset(v[:, :, :], 1.0)
                    for k in KZ:
                        dve.memset(k[:, :, :], 0.0)
                    dve.memset(zcol[:, :], 0.0)
                    dve.memset(HT[0][:, 0:1], 0.0).then_inc(init.sem, 1)
                    dve.wait_ge(init.sem, 1)
            env = dict(locals())
            sems_a, sems_f = attention_sems(steps), ffn_sems(steps, Norm, layers)
            with nc.Fori(0, DEPTH) as L:
                local_attention(nc, L, sb, ps, steps, sems_a, env)
                if stop > 2:
                    feed_forward(nc, L, sb, ps, steps, sems_f, env)
        if stop <= 3:
            return dump(nc, out, S, NB)
        env = dict(locals())
        causal_attention(nc, sb, ps, steps, Norm, env)
        if stop <= 4:
            return dump(nc, out, S, NB)
        experts(nc, sb, ps, steps, Norm, env)


def dump(nc, out, S, NB):
    with nc.semaphore("dumped") as dumped, nc.Block() as block:
        @block.sync
        def _(sp):
            for b in range(NB):
                sp.dma_start(out[b].rearrange("(t p) d -> p t d", p=P), S[:, b * TB:(b + 1) * TB, :]).then_inc(dumped, 16)
            sp.wait_ge(dumped, 16 * NB)


def attention_sems(steps):
    per = dict(w_in=1, tab=2, xst=1, hps=1, ht=1, qkps=1, vps=1, sq=1, rn=1, d1=5, tq=1, tk=1, eq=1, ek=1, ev=1, sc=1,
               d2=2, ex=1, pt=2, ept=2, pv=1, d3=2, ot=1, eot=1, wo=1, xadd=1)
    made = {k: steps("att_" + k, v) for k, v in per.items()}
    made["vx"] = [steps(f"att_vx{t}") for t in range(TB)]
    return made


def local_attention(nc, L, sb, ps, steps, q, env):
    NB, NT, S, ident, mk, mhalf = (env[k] for k in ("NB", "NT", "S", "ident", "mk", "mhalf"))
    HEADS, DH, WIN, ready = env["HEADS"], env["DH"], env["WIN"], env["ready"]
    VN, KZ, HT, zcol, rotc = (env[k] for k in ("VN", "KZ", "HT", "zcol", "rotc"))
    wqkv, qsc, ksc, wo = (env[k] for k in ("wqkv", "qsc", "ksc", "wo"))
    INNER = HEADS * DH
    NG = INNER // P
    LAST = 4
    with ExitStack() as ctx:
        wq = sb("wq", [P, 3 * INNER], ctx=ctx)
        wot = sb("wo", [P, NG, D], ctx=ctx)
        scb = sb("qk_scales", [P, 4, DH], ctx=ctx)
        tab = sb("rot_scaled", [P, TB, 4, DH], ctx=ctx)
        xst = [sb(f"xst{u}", [P, P], ctx=ctx) for u in range(2)]
        SQ = sb("squares", [P, 2 * INNER], ctx=ctx)
        ss = sb("sumsq", [P, 16], ctx=ctx)
        rn = sb("rnorm", [P, 16], ctx=ctx)
        A1 = sb("rot_a", [P, 2 * INNER], ctx=ctx)
        A2 = sb("rot_b", [P, 2 * INNER], ctx=ctx)
        QKN = sb("qk_normed", [P, 2 * INNER], ctx=ctx)
        QT = sb("qt", [P, NG, P], ctx=ctx)
        VX = [sb(f"vx{t}", [P, HEADS, DH + 1], ctx=ctx) for t in range(TB)]
        mx = sb("score_max", [P, HEADS], ctx=ctx)
        SS = sb("scores_less_max", [P, HEADS, P], ctx=ctx)
        PP = sb("probs", [P, HEADS, P], ctx=ctx)
        PT = sb("probs_t", [P, HEADS, P], ctx=ctx)
        rec = sb("rec", [P, HEADS], ctx=ctx)
        ON = sb("o_normed", [P, HEADS, DH], ctx=ctx)
        OT = sb("o_t", [P, NG, P], ctx=ctx)
        QK = ps("qk_ps", [P, 2 * INNER], ctx)
        R = [ps(f"ring{k}", [P, 512], ctx) for k in range(2)]
        SC = ps("scores_ps", [P, HEADS, P], ctx)
        OP = ps("o_ps", [P, 2, 512], ctx)
        OH = OP[:, :, 0:4 * (DH + 1)].rearrange("p b (h d) -> p b h d", d=DH + 1)
        base = L * NT

        def num(b, t):
            return base + b * TB + t

        def run(eng, slot):
            def one(b, t, n=None):
                has = lambda k: n is None or 0 <= n - k < NT
                slot(b, t, lambda k: num(*back(b, t, k, TB)) if k <= TB else num(*back(b - 1, t, k - TB, TB)), has)
            for t in range(TB):
                one(0, t, t)
            with eng.Fori(1, NB) as b:
                for t in range(TB):
                    one(b, t)
            for t in range(LAST):
                one(NB, t, NT + t)

        USES = [("h", 0, 0, "ht", 1), ("q", 2, 1, "eq", 1), ("k", 2, 0, "ek", 1), ("v", 1, 1, "ev", 1),
                ("p0", 3, 0, "ept", 1), ("p1", 3, 1, "ept", 2), ("o", 4, 0, "eot", 1), ("w", 4, 1, "xadd", 1)]
        HP, WP = R[0][:, 0:P], R[1][:, 0:P]

        def ring_wait(pe, use, item, has):
            at = [u[0] for u in USES].index(use)
            bank = USES[at][2]
            earlier = [(u, 0) for u in USES[:at][::-1]] + [(u, 1) for u in USES[::-1]] + [(u, 2) for u in USES[::-1]]
            for (name, lag, bk, sem, step), slots in earlier:
                if bk == bank and has(lag + slots):
                    pe.wait_ge(q[sem].sem, q[sem].at(item(lag + slots), step))
                    return

        with nc.Block() as block:
            @block.sync
            def _(sp):
                sp.dma_start(wq[:, :], wqkv[L]).then_inc(q["w_in"].sem, 16)
                sp.dma_start(wot[:, :, :], wo[L].rearrange("(c p) d -> p c d", p=P)).then_inc(q["w_in"].sem, 16)
                for k, src in enumerate((qsc, ksc)):
                    row = src[L].rearrange("(a n) -> a n", a=1)
                    half = DH // 2
                    sp.dma_start(scb[:, k, :], row.to_broadcast([P, DH]))\
                      .then_inc(q["w_in"].sem, 16)
                    for h in range(2):
                        sp.dma_start(scb[:, 2 + k, h * half:(h + 1) * half],
                                     row[:, (1 - h) * half:(2 - h) * half].to_broadcast([P, half]))\
                          .then_inc(q["w_in"].sem, 16)

                def slot(b, t, item, has):
                    if has(1):
                        bb, t1 = back(b, t, 1, TB)
                        sp.wait_ge(q["ev"].sem, q["ev"].at(item(1)))
                        settle(sp, ready)
                        if has(5):
                            sp.wait_ge(q["pv"].sem, q["pv"].at(item(5)))
                        settle(sp, ready)
                        for lo, src in ((0, VN[t1]), (WIN, VN[(t1 - 1) % TB])):
                            sp.dma_start(VX[t1][lo:lo + WIN, :, :], src[lo:lo + WIN, :, :]).then_inc(q["vx"][t1].sem, 16)
                run(sp, slot)

            @block.gpsimd
            def _(pool):
                def slot(b, t, item, has):
                    if has(0):
                        if has(2):
                            pool.wait_ge(q["hps"].sem, q["hps"].at(item(2)))
                        settle(pool, ready)
                        pool.tensor_copy(xst[t % 2][:, :], S[:, b * TB + t, :]).then_inc(q["xst"].sem, 1)
                    if has(1):
                        pool.wait_ge(q["d1"].sem, q["d1"].at(item(1), 2))
                        pool.tensor_tensor(rn[:, :], ss[:, :], mhalf[:, :], ALU.pow).then_inc(q["rn"].sem, 1)
                run(pool, slot)

            @block.tensor
            def _(pe):
                pe.wait_ge(q["w_in"].sem, (L + 1) * (16 * 8))

                def slot(b, t, item, has):
                    if has(0):
                        pe.wait_ge(q["xst"].sem, q["xst"].at(item(0)))
                        ring_wait(pe, "h", item, has)
                        pe.transpose(HP, xst[t % 2][:, :], ident[:, :]).then_inc(q["hps"].sem, 1)
                    if has(2):
                        pe.wait_ge(q["d1"].sem, q["d1"].at(item(2)))
                        for k, (use, done) in enumerate((("q", "tq"), ("k", "tk"))):
                            ring_wait(pe, use, item, has)
                            for p in range(NG):
                                last = pe.transpose(R[1 - k][:, p * P:(p + 1) * P],
                                                    QKN[:, k * INNER + p * P:k * INNER + (p + 1) * P], ident[:, :])
                            last.then_inc(q[done].sem, 1)
                    if has(1):
                        t1 = (t - 1) % TB
                        pe.wait_ge(q["ht"].sem, q["ht"].at(item(1)))
                        if has(2):
                            pe.wait_ge(q["d1"].sem, q["d1"].at(item(2), 3))
                            pe.wait_ge(q["sq"].sem, q["sq"].at(item(2)))
                        for k in range(2):
                            last = pe.matmul(QK[:, k * INNER:(k + 1) * INNER], HT[t1][:, :],
                                             wq[:, k * INNER:(k + 1) * INNER], start=True, stop=True)
                        last.then_inc(q["qkps"].sem, 1)
                        ring_wait(pe, "v", item, has)
                        pe.matmul(R[1][:, :], HT[t1][:, :], wq[:, 2 * INNER:], start=True, stop=True)\
                            .then_inc(q["vps"].sem, 1)
                    if has(2):
                        t2 = (t - 2) % TB
                        u = t2 % 2
                        if has(3):
                            pe.wait_ge(q["d2"].sem, q["d2"].at(item(3)))
                        for h4 in (0, 4):
                            pe.matmul(SC[:, h4:h4 + 4, :], mk[:, 4, :],
                                      mk[:, 1 if t2 == 0 else 0, :].unsqueeze(1).to_broadcast([P, 4, P]),
                                      start=True, stop=False, skip_group_check=True)
                        pe.wait_ge(q["eq"].sem, q["eq"].at(item(2)))
                        pe.wait_ge(q["ek"].sem, q["ek"].at(item(2)))
                        for h in range(HEADS):
                            qt = QT[:, h // 2, :]
                            pe.matmul(SC[:, h, 0:WIN], qt, KZ[u][:, h, 0:WIN],
                                      start=False, stop=False, skip_group_check=True)
                            last = pe.matmul(SC[WIN:P, h, WIN:P], qt[:, WIN:P], KZ[u][:, h, WIN:P],
                                             start=False, stop=True, skip_group_check=True)
                            if t2 > 0:
                                last = pe.matmul(SC[0:WIN, h, WIN:P], qt[:, 0:WIN], KZ[1 - u][:, h, WIN:P],
                                                 start=False, stop=True, skip_group_check=True)
                        last.then_inc(q["sc"].sem, 1)
                    if has(3):
                        pe.wait_ge(q["ex"].sem, q["ex"].at(item(3)))
                        for k in range(2):
                            ring_wait(pe, f"p{k}", item, has)
                            for p in range(4):
                                last = pe.transpose(R[k][:, p * P:(p + 1) * P], PP[:, 4 * k + p, :], ident[:, :])
                            last.then_inc(q["pt"].sem, 1)
                    if has(4):
                        pe.wait_ge(q["d3"].sem, q["d3"].at(item(4)))
                        ring_wait(pe, "o", item, has)
                        for p in range(NG):
                            last = pe.transpose(R[0][:, p * P:(p + 1) * P],
                                                ON[:, 2 * p:2 * p + 2, :].rearrange("p a b -> p (a b)"), ident[:, :])
                        last.then_inc(q["ot"].sem, 1)
                    if has(3):
                        bb, t3 = back(b, t, 3, TB)
                        pe.wait_ge(q["vx"][t3].sem, (L * NB + bb) * 32 + 32)
                        if has(4):
                            pe.wait_ge(q["d3"].sem, q["d3"].at(item(4)))
                        for h in range(HEADS):
                            if h % 4 == 0:
                                pe.wait_ge(q["ept"].sem, q["ept"].at(item(3), 1 + h // 4))
                            o = OH[:, h // 4, h % 4, :]
                            pe.matmul(o[WIN:P, :], PT[:, h, WIN:P], VN[t3][:, h, :], start=True, stop=True)
                            last = pe.matmul(o[0:WIN, :], PT[:, h, 0:WIN], VX[t3][:, h, :], start=True, stop=True)
                        last.then_inc(q["pv"].sem, 1)
                    if has(4):
                        pe.wait_ge(q["eot"].sem, q["eot"].at(item(4)))
                        ring_wait(pe, "w", item, has)
                        for c in range(NG):
                            last = pe.matmul(WP, OT[:, c, :], wot[:, c, :], start=(c == 0), stop=(c == NG - 1))
                        last.then_inc(q["wo"].sem, 1)
                run(pe, slot)

            @block.scalar
            def _(act):
                def slot(b, t, item, has):
                    if has(0):
                        act.wait_ge(q["hps"].sem, q["hps"].at(item(0)))
                        nxt = HT[(t + 1) % TB]
                        act.activation(HT[t][0:64, :], HP[0:64, :], ACT.Copy)
                        act.activation(HT[t][64:P, 1:P], HP[64:P, 0:P - 1], ACT.Copy)
                        act.activation(nxt[64:P, 0:1], HP[64:P, P - 1:P] if t < TB - 1 else zcol[64:P, :], ACT.Copy)\
                            .then_inc(q["ht"].sem, 1)
                    if has(2):
                        u = t % 2
                        act.wait_ge(q["tq"].sem, q["tq"].at(item(2)))
                        if has(3):
                            act.wait_ge(q["sc"].sem, q["sc"].at(item(3)))
                        act.activation(QT[:, :, :].rearrange("p a b -> p (a b)"), R[1][:, :], ACT.Copy)\
                            .then_inc(q["eq"].sem, 1)
                        act.wait_ge(q["tk"].sem, q["tk"].at(item(2)))
                        for half in range(2):
                            r = slice(64 * half, 64 * half + 64)
                            last = act.activation(
                                KZ[u][r, :, :].rearrange("p (a two) k -> p a two k", two=2)[:, :, half, :],
                                R[0][r, :].rearrange("p (a k) -> p a k", k=P), ACT.Copy)
                        last.then_inc(q["ek"].sem, 1)
                    if has(1):
                        t1 = (t - 1) % TB
                        act.wait_ge(q["qkps"].sem, q["qkps"].at(item(1)))
                        if has(2):
                            act.wait_ge(q["d1"].sem, q["d1"].at(item(2), 1))
                        act.activation(SQ[:, :], QK[:, :], ACT.Square).then_inc(q["sq"].sem, 1)
                        act.wait_ge(q["vps"].sem, q["vps"].at(item(1)))
                        act.activation(VN[t1][:, :, 0:DH], R[1][:, :].rearrange("p (h d) -> p h d", d=DH), ACT.Copy)\
                            .then_inc(q["ev"].sem, 1)
                    if has(3):
                        for k in range(2):
                            act.wait_ge(q["pt"].sem, q["pt"].at(item(3), k + 1))
                            if has(4) and k == 0:
                                act.wait_ge(q["pv"].sem, q["pv"].at(item(4)))
                            act.activation(PT[:, 4 * k:4 * k + 4, :].rearrange("p a b -> p (a b)"), R[k][:, :],
                                           ACT.Copy).then_inc(q["ept"].sem, 1)
                    if has(4):
                        act.wait_ge(q["ot"].sem, q["ot"].at(item(4)))
                        if has(5):
                            act.wait_ge(q["wo"].sem, q["wo"].at(item(5)))
                        act.activation(OT[:, :, :].rearrange("p a b -> p (a b)"), R[0][:, :], ACT.Copy)\
                            .then_inc(q["eot"].sem, 1)
                    if has(2):
                        act.wait_ge(q["d2"].sem, q["d2"].at(item(2)))
                        if has(3):
                            act.wait_ge(q["pt"].sem, q["pt"].at(item(3)))
                        act.activation(PP[:, :, :], SS[:, :, :], ACT.Exp).then_inc(q["ex"].sem, 1)
                run(act, slot)

            @block.vector
            def _(dve):
                dve.wait_ge(q["w_in"].sem, (L + 1) * (16 * 8))
                for t in range(TB):
                    last = dve.tensor_tensor(tab[:, t, :, :], rotc[:, t, :, :], scb[:, :, :], ALU.mult)
                last.then_inc(q["tab"].sem, 2)
                dve.wait_ge(q["tab"].sem, L * 2 + 2)
                qk4 = lambda a: a.rearrange("p (k h d) -> p k h d", k=2, d=DH)

                def slot(b, t, item, has):
                    if has(1):
                        t1 = (t - 1) % TB
                        d1 = q["d1"]
                        half = DH // 2
                        dve.wait_ge(q["sq"].sem, q["sq"].at(item(1)))
                        if has(2):
                            dve.wait_ge(q["rn"].sem, q["rn"].at(item(2)))
                        dve.tensor_reduce(ss[:, :], SQ[:, :].rearrange("p (h d) -> p h d", d=DH), AX, ALU.add)\
                            .then_inc(d1.sem, 1)
                        dve.wait_ge(d1.sem, d1.at(item(1), 1))
                        dve.tensor_scalar(ss[:, :], ss[:, :], 1e-24, None, ALU.max).then_inc(d1.sem, 1)
                        for k in range(2):
                            io = slice(k * INNER, (k + 1) * INNER)
                            hd = lambda a: a[:, io].rearrange("p (h d) -> p h d", d=DH)
                            bc = lambda c, lo, hi: tab[:, t1, c, lo:hi].unsqueeze(1).to_broadcast([P, HEADS, hi - lo])
                            dve.tensor_tensor(hd(A1), hd(QK), bc(k, 0, DH), ALU.mult)
                            for h in range(2):
                                lo, sw = h * half, (1 - h) * half
                                last = dve.tensor_tensor(hd(A2)[:, :, lo:lo + half], hd(QK)[:, :, sw:sw + half],
                                                         bc(2 + k, lo, lo + half), ALU.mult)
                        last.then_inc(d1.sem, 1)
                        dve.wait_ge(d1.sem, d1.at(item(1), 3))
                        dve.tensor_tensor(A1[:, :], A1[:, :], A2[:, :], ALU.add).then_inc(d1.sem, 1)
                        dve.wait_ge(d1.sem, d1.at(item(1), 4))
                        dve.wait_ge(q["rn"].sem, q["rn"].at(item(1)))
                        if has(2):
                            dve.wait_ge(q["tk"].sem, q["tk"].at(item(2)))
                        dve.tensor_tensor(QKN[:, :].rearrange("p (h d) -> p h d", d=DH),
                                          A1[:, :].rearrange("p (h d) -> p h d", d=DH),
                                          rn[:, :].unsqueeze(2).to_broadcast([P, 16, DH]), ALU.mult)\
                            .then_inc(d1.sem, 1)
                    if has(2):
                        d2 = q["d2"]
                        dve.wait_ge(q["sc"].sem, q["sc"].at(item(2)))
                        dve.tensor_reduce(mx[:, :], SC[:, :, :], AX, ALU.max).then_inc(d2.sem, 1)
                        dve.wait_ge(d2.sem, d2.at(item(2), 1))
                        if has(3):
                            dve.wait_ge(q["ex"].sem, q["ex"].at(item(3)))
                        dve.tensor_tensor(SS[:, :, :], SC[:, :, :], mx[:, :].unsqueeze(2).to_broadcast([P, HEADS, P]),
                                          ALU.subtract).then_inc(d2.sem, 1)
                    if has(3):
                        d3 = q["d3"]
                        dve.wait_ge(q["pv"].sem, q["pv"].at(item(3)))
                        rech = rec[:, :].rearrange("p (b h) -> p b h", b=2)
                        dve.reciprocal(rech, OH[:, :, :, DH]).then_inc(d3.sem, 1)
                        dve.wait_ge(d3.sem, d3.at(item(3), 1))
                        if has(4):
                            dve.wait_ge(q["ot"].sem, q["ot"].at(item(4)))
                        dve.tensor_tensor(ON[:, :, :].rearrange("p (b h) d -> p b h d", b=2), OH[:, :, :, 0:DH],
                                          rech.unsqueeze(3).to_broadcast([P, 2, 4, DH]), ALU.mult)\
                            .then_inc(d3.sem, 1)
                    if has(4):
                        bb, t4 = b - 1, t
                        dve.wait_ge(q["wo"].sem, q["wo"].at(item(4)))
                        xs = S[:, bb * TB + t4, :]
                        dve.tensor_tensor(xs, xs, WP, ALU.add).then_inc(q["xadd"].sem, 1)
                run(dve, slot)


def ffn_sems(steps, Norm, ctx):
    per = dict(w_in=1, sh=1, hb=1, tp=1, ht=1, g=3, a=3, ge=3, z=3, w2=1, xb=1, upd=1)
    made = {k: steps("ffn_" + k, v) for k, v in per.items()}
    made["ln"] = Norm("ffn_ln", ctx, 2)
    return made


def feed_forward(nc, L, sb, ps, steps, q, env):
    NB, S, ident, shiftm, CH, HID = (env[k] for k in ("NB", "S", "ident", "shiftm", "CH", "HID"))
    lng, lnb, w1, b1, w2, b2 = (env[k] for k in ("lng", "lnb", "w1", "b1", "w2", "b2"))
    ln = q["ln"]
    NCH = len(CH)
    HALF = D // 2
    with ExitStack() as ctx:
        w1t = sb("w1", [P, 2 * HID], ctx=ctx)
        w2t = sb("w2", [P, NCH, D], ctx=ctx)
        gb = sb("ln_gb", [P, 2], ctx=ctx)
        b1t = sb("b1", [P, 2, NCH], ctx=ctx)
        b2t = sb("b2", [P, D], ctx=ctx)
        HB = sb("h_normed", [P, TB, D], ctx=ctx)
        HF = sb("h_t", [P, SEQ], ctx=ctx)
        GE = [sb(f"gelu{k}", [P, SEQ], ctx=ctx) for k in range(2)]
        Z = [[sb(f"z{u}_{c}", [P, SEQ], ctx=ctx) for c in range(NCH)] for u in range(2)]
        XB = [sb(f"x_b2_{u}", [P, TB, D], ctx=ctx) for u in range(2)]
        SH = ps("shifted", [P, TB, HALF], ctx)
        TP = ps("h_t_ps", [P, SEQ], ctx)
        GP = [ps(f"g_ps{k}", [P, SEQ], ctx) for k in range(2)]
        AP_ = [ps(f"a_ps{k}", [P, SEQ], ctx) for k in range(2)]
        OB = ps("ffn_out", [P, TB, D], ctx)
        base = L * NB
        NW = 4 + 1 + 2 * NCH + NCH

        def run(eng, slot):
            def one(g, u, n=None):
                has = lambda k: n is None or 0 <= n - k < NB
                slot(g * 2 + u, u, has)
            for n in range(2):
                one(0, n, n)
            with eng.Fori(1, NB // 2) as g:
                for u in range(2):
                    one(g, u)
            for n in range(2):
                one(NB // 2, n, NB + n)

        with nc.Block() as block:
            @block.sync
            def _(sp):
                def load(dst, src):
                    sp.dma_start(dst, src).then_inc(q["w_in"].sem, 16)
                load(w1t[:, :], w1[L])
                for c, n in enumerate(CH):
                    load(w2t[0:n, c, :], w2[L, c * P:c * P + n, :])
                    for k in range(2):
                        load(b1t[0:n, k, c:c + 1], b1[L, k * HID + c * P:k * HID + c * P + n].rearrange("(n a) -> n a", a=1))
                load(gb[:, 0:1], lng[L].rearrange("(n a) -> n a", a=1))
                load(gb[:, 1:2], lnb[L].rearrange("(n a) -> n a", a=1))
                load(b2t[:, :], b2[L].rearrange("(a n) -> a n", a=1).to_broadcast([P, D]))
                sp.wait_ge(q["w_in"].sem, (L + 1) * (16 * (4 + 3 * NCH)))
                settle(sp, env["ready"])
            W_ALL = (L + 1) * (16 * (4 + 3 * NCH))

            @block.gpsimd
            def _(pool):
                pool.wait_ge(q["w_in"].sem, W_ALL)

                def slot(b, u, has):
                    n = base + b
                    if has(0):
                        if has(2):
                            pool.wait_ge(q["upd"].sem, q["upd"].at(n - 2))
                        ln.power(pool, n)
                        pool.tensor_tensor(XB[u][:, :, :], S[:, bass.ds(b * TB, TB), :],
                                           b2t[:, :].unsqueeze(1).to_broadcast([P, TB, D]), ALU.add)\
                            .then_inc(q["xb"].sem, 1)
                run(pool, slot)

            @block.tensor
            def _(pe):
                pe.wait_ge(q["w_in"].sem, W_ALL)

                def slot(b, u, has):
                    n = base + b
                    if has(0):
                        if has(1):
                            pe.wait_ge(q["hb"].sem, q["hb"].at(n - 1))
                        pe.matmul(SH[:, :, :], shiftm[:, 0, :], S[:, bass.ds(b * TB, TB), HALF:D],
                                  start=True, stop=False, skip_group_check=True)
                        pe.matmul(SH[:, 1:TB, :], shiftm[:, 1, :], S[:, bass.ds(b * TB, TB - 1), HALF:D],
                                  start=False, stop=True, skip_group_check=True).then_inc(q["sh"].sem, 1)
                    if has(1):
                        pe.wait_ge(q["hb"].sem, q["hb"].at(n - 1))
                        if has(2):
                            pe.wait_ge(q["ht"].sem, q["ht"].at(n - 2))
                        for t in range(TB):
                            last = pe.transpose(TP[:, t * P:(t + 1) * P], HB[:, t, :], ident[:, :])
                        last.then_inc(q["tp"].sem, 1)
                    if has(2):
                        pe.wait_ge(q["z"].sem, q["z"].at(n - 2))
                        if has(3):
                            pe.wait_ge(q["upd"].sem, q["upd"].at(n - 3))
                        for t in range(TB):
                            for c, m in enumerate(CH):
                                last = pe.matmul(OB[:, t, :], Z[u][c][0:m, t * P:(t + 1) * P], w2t[0:m, c, :],
                                                 start=(c == 0), stop=(c == NCH - 1), skip_group_check=True)
                        last.then_inc(q["w2"].sem, 1)
                    if has(1):
                        pe.wait_ge(q["ht"].sem, q["ht"].at(n - 1))
                        for c, m in enumerate(CH):
                            if c >= 2:
                                pe.wait_ge(q["z"].sem, q["z"].at(n - 1, c - 1))
                            elif has(2):
                                pe.wait_ge(q["z"].sem, q["z"].at(n - 2, 2 if c == 1 else 3))
                            pe.matmul(GP[c % 2][0:m, :], w1t[:, HID + c * P:HID + c * P + m], HF[:, :],
                                      start=True, stop=True).then_inc(q["g"].sem, 1)
                            pe.matmul(AP_[c % 2][0:m, :], w1t[:, c * P:c * P + m], HF[:, :],
                                      start=True, stop=True).then_inc(q["a"].sem, 1)
                run(pe, slot)

            @block.scalar
            def _(act):
                def slot(b, u, has):
                    n = base + b
                    if has(1):
                        act.wait_ge(q["tp"].sem, q["tp"].at(n - 1))
                        if has(2):
                            act.wait_ge(q["a"].sem, q["a"].at(n - 2))
                        act.activation(HF[:, :], TP[:, :], ACT.Identity, bias=gb[:, 1:2], scale=gb[:, 0:1])\
                            .then_inc(q["ht"].sem, 1)
                        for c, m in enumerate(CH):
                            act.wait_ge(q["g"].sem, q["g"].at(n - 1, c + 1))
                            if c >= 2:
                                act.wait_ge(q["z"].sem, q["z"].at(n - 1, c - 1))
                            elif has(2):
                                act.wait_ge(q["z"].sem, q["z"].at(n - 2, 2 if c == 1 else 3))
                            act.activation(GE[c % 2][0:m, :], GP[c % 2][0:m, :], ACT.Gelu, bias=b1t[0:m, 1, c:c + 1])\
                                .then_inc(q["ge"].sem, 1)
                act.wait_ge(q["w_in"].sem, W_ALL)
                run(act, slot)

            @block.vector
            def _(dve):
                dve.wait_ge(q["w_in"].sem, W_ALL)

                def slot(b, u, has):
                    n = base + b
                    pieces = lambda t: [S[:, b * TB + t, 0:HALF], SH[:, t, :]]
                    if has(0):
                        dve.wait_ge(q["sh"].sem, q["sh"].at(n))
                        ln.stats(dve, n, pieces)
                    if has(2):
                        dve.wait_ge(q["w2"].sem, q["w2"].at(n - 2))
                        dve.wait_ge(q["xb"].sem, q["xb"].at(n - 2))
                        dve.tensor_tensor(S[:, bass.ds((b - 2) * TB, TB), :], OB[:, :, :], XB[u][:, :, :], ALU.add)\
                            .then_inc(q["upd"].sem, 1)
                    if has(0):
                        if has(1):
                            dve.wait_ge(q["tp"].sem, q["tp"].at(n - 1))
                        ln.apply(dve, n, lambda t: [HB[:, t, 0:HALF], HB[:, t, HALF:D]], pieces)\
                          .then_inc(q["hb"].sem, 1)
                    if has(1):
                        for c, m in enumerate(CH):
                            dve.wait_ge(q["a"].sem, q["a"].at(n - 1, c + 1))
                            dve.wait_ge(q["ge"].sem, q["ge"].at(n - 1, c + 1))
                            if c == 0 and has(3):
                                dve.wait_ge(q["w2"].sem, q["w2"].at(n - 3))
                            dve.scalar_tensor_tensor(Z[1 - u][c][0:m, :], AP_[c % 2][0:m, :], b1t[0:m, 0, c:c + 1],
                                                     GE[c % 2][0:m, :], ALU.add, ALU.mult).then_inc(q["z"].sem, 1)
                run(dve, slot)


def causal_attention(nc, sb, ps, steps, Norm, env):
    NB, NT, X, S, ident, mk, split_dram, ready = (
        env[k] for k in ("NB", "NT", "X", "S", "ident", "mk", "split_dram", "ready"))
    wat, bat, H2, D2 = (env[k] for k in ("wat", "bat", "H2", "D2"))
    SCALE = float(D2) ** -0.5
    SV = S[:, :, :].rearrange("p (b t) d -> p b t d", t=TB)
    with ExitStack() as outer:
        VP = sb("values", [P, TB, NB * H2, D2 + 1], ctx=outer)
        QS = [sb(f"q_stack{u}", [P, H2, SEQ], BF16, ctx=outer) for u in range(2)]
        KS = [sb(f"k_stack{u}", [P, H2, SEQ], BF16, ctx=outer) for u in range(2)]
        with ExitStack() as ctx:
            w = sb("w_attn", [P, 3 * D], ctx=ctx)
            bqk = sb("b_qk", [P, 2], ctx=ctx)
            bqs = sb("b_qk_scaled", [P, 2], ctx=ctx)
            bv = sb("b_v", [P, D], ctx=ctx)
            T = sb("s_normed", [P, TB, D], ctx=ctx)
            Y = sb("attn_in", [P, TB, D], ctx=ctx)
            YT = sb("attn_in_t", [P, SEQ], ctx=ctx)
            F = [sb(f"qk_full{k}", [P, SEQ], ctx=ctx) for k in range(2)]
            Rm = [sb(f"qk_rest{k}", [P, SEQ], ctx=ctx) for k in range(2)]
            PARTS = [sb(f"qk_parts{u}", [P, 2, 3, SEQ], BF16, ctx=ctx) for u in range(2)]
            TPp = ps("in_t_ps", [P, SEQ], ctx)
            QP = [ps(f"qk_p{k}", [P, SEQ], ctx) for k in range(2)]
            VPp = ps("v_p", [P, TB, D], ctx)
            ln1, ln2 = Norm("cln1", ctx), Norm("cln2", ctx)
            w_in, t_ok, x_ok, y_ok, tp, yt, qk, vps, vst = (
                steps("cin_" + n) for n in ("w_in", "t_ok", "x_ok", "y_ok", "tp", "yt", "qk", "vps", "vst"))
            bs_ok, full, rest = steps("cin_bs"), steps("cin_full", 2), steps("cin_rest", 2)
            p1, p2, p3 = steps("cin_part1", 2), steps("cin_part2", 2), steps("cin_part3", 2)
            stored = [steps(f"cin_stored{u}") for u in range(2)]
            ones = steps("cin_ones")
            NW = 5

            def run(eng, slot):
                def one(g, u, n=None):
                    has = lambda k: n is None or 0 <= n - k < NB
                    slot(g * 2 + u, u, has)
                for n in range(2):
                    one(0, n, n)
                with eng.Fori(1, NB // 2) as g:
                    for u in range(2):
                        one(g, u)
                for n in range(2):
                    one(NB // 2, n, NB + n)

            with nc.Block() as block:
                @block.sync
                def _(sp):
                    sp.dma_start(w[:, :], wat).then_inc(w_in.sem, 16)
                    for k in range(2):
                        sp.dma_start(bqk[:, k:k + 1], bat[k * D:(k + 1) * D].rearrange("(n a) -> n a", a=1))\
                          .then_inc(w_in.sem, 16)
                    sp.dma_start(bv[:, :], bat[2 * D:3 * D].rearrange("(a n) -> a n", a=1).to_broadcast([P, D]))\
                      .then_inc(w_in.sem, 16)

                    def slot(b, u, has):
                        if has(2):
                            sp.wait_ge(p3.sem, p3.at(b - 2))
                            settle(sp, ready)
                            sp.dma_start(split_dram[b - 2].rearrange("k c d s -> d (k c) s"),
                                         PARTS[u][:, :, :, :].rearrange("p k c s -> p (k c) s"))\
                              .then_inc(stored[u].sem, 16)
                    run(sp, slot)
                    for u in range(2):
                        sp.wait_ge(stored[u].sem, 16 * (NB // 2))

                @block.gpsimd
                def _(pool):
                    pool.memset(VP[:, :, :, :], 1.0).then_inc(ones.sem, 1)

                    def slot(b, u, has):
                        if has(0):
                            ln1.power(pool, b)
                            ln2.power(pool, b)
                    run(pool, slot)

                @block.tensor
                def _(pe):
                    pe.wait_ge(w_in.sem, 64)

                    def slot(b, u, has):
                        if has(1):
                            n = b - 1
                            pe.wait_ge(y_ok.sem, y_ok.at(n))
                            if has(2):
                                pe.wait_ge(yt.sem, yt.at(n - 1))
                            for t in range(TB):
                                last = pe.transpose(TPp[:, t * P:(t + 1) * P], Y[:, t, :], ident[:, :])
                            last.then_inc(tp.sem, 1)
                            pe.wait_ge(yt.sem, yt.at(n))
                            if has(2):
                                pe.wait_ge(full.sem, full.at(n - 1))
                                pe.wait_ge(p1.sem, p1.at(n - 1))
                            for k in range(2):
                                last = pe.matmul(QP[k][:, :], w[:, k * D:(k + 1) * D], YT[:, :], start=True, stop=True)
                            last.then_inc(qk.sem, 1)
                            if has(2):
                                pe.wait_ge(vst.sem, vst.at(n - 1))
                            for t in range(TB):
                                last = pe.matmul(VPp[:, t, :], YT[:, t * P:(t + 1) * P], w[:, 2 * D:3 * D],
                                                 start=True, stop=True)
                            last.then_inc(vps.sem, 1)
                    run(pe, slot)

                @block.scalar
                def _(act):
                    act.wait_ge(w_in.sem, 64)
                    act.activation(bqs[:, 0:1], bqk[:, 0:1], ACT.Copy, scale=SCALE)
                    act.activation(bqs[:, 1:2], bqk[:, 1:2], ACT.Copy).then_inc(bs_ok.sem, 1)
                    act.wait_ge(bs_ok.sem, 1)

                    def slot(b, u, has):
                        if has(1):
                            n = b - 1
                            act.wait_ge(tp.sem, tp.at(n))
                            if has(2):
                                act.wait_ge(vps.sem, vps.at(n - 1))
                            act.activation(YT[:, :], TPp[:, :], ACT.Copy).then_inc(yt.sem, 1)
                            act.wait_ge(qk.sem, qk.at(n))
                            if has(2):
                                act.wait_ge(rest.sem, rest.at(n - 1))
                            if has(3):
                                act.wait_ge(stored[1 - u].sem, (b - 3 - (1 - u)) * 8 + 16)
                            for k in range(2):
                                act.activation(F[k][:, :], QP[k][:, :], ACT.Identity, bias=bqs[:, k:k + 1],
                                               scale=SCALE if k == 0 else 1.0).then_inc(full.sem, 1)
                            for k in range(2):
                                act.activation(PARTS[1 - u][:, k, 0, :], QP[k][:, :], ACT.Identity,
                                               bias=bqs[:, k:k + 1], scale=SCALE if k == 0 else 1.0)\
                                   .then_inc(p1.sem, 1)
                            for k in range(2):
                                act.wait_ge(rest.sem, rest.at(n, k + 1))
                                act.activation(PARTS[1 - u][:, k, 1, :], Rm[k][:, :], ACT.Copy).then_inc(p2.sem, 1)
                    run(act, slot)

                @block.vector
                def _(dve):
                    dve.wait_ge(w_in.sem, 64)
                    dve.wait_ge(ones.sem, 1)

                    def slot(b, u, has):
                        xt = lambda t: [X[:, b * TB + t, :]]
                        st = lambda t: [S[:, b * TB + t, :]]
                        if has(0):
                            ln1.stats(dve, b, st)
                        if has(1):
                            n = b - 1
                            for k in range(2):
                                dve.wait_ge(p1.sem, p1.at(n, k + 1))
                                if has(2):
                                    dve.wait_ge(p3.sem, p3.at(n - 1))
                                dve.tensor_tensor(Rm[k][:, :], F[k][:, :], PARTS[1 - u][:, k, 0, :], ALU.subtract)\
                                   .then_inc(rest.sem, 1)
                            dve.wait_ge(vps.sem, vps.at(n))
                            for t in range(TB):
                                last = dve.tensor_tensor(VP[:, t, bass.ds(n * H2, H2), 0:D2],
                                                         VPp[:, t, :].rearrange("p (h d) -> p h d", d=D2),
                                                         bv[:, :].rearrange("p (h d) -> p h d", d=D2), ALU.add)
                            last.then_inc(vst.sem, 1)
                            for k in range(2):
                                dve.wait_ge(p2.sem, p2.at(n, k + 1))
                                dve.tensor_tensor(PARTS[1 - u][:, k, 2, :], Rm[k][:, :], PARTS[1 - u][:, k, 1, :],
                                                  ALU.subtract).then_inc(p3.sem, 1)
                        if has(0):
                            ln1.apply(dve, b, lambda t: [T[:, t, :]], st).then_inc(t_ok.sem, 1)
                            dve.wait_ge(t_ok.sem, t_ok.at(b))
                            xb = X[:, bass.ds(b * TB, TB), :]
                            dve.tensor_tensor(xb, xb, T[:, :, :], ALU.add).then_inc(x_ok.sem, 1)
                            dve.wait_ge(x_ok.sem, x_ok.at(b))
                            ln2.stats(dve, b, xt)
                            if has(1):
                                dve.wait_ge(tp.sem, tp.at(b - 1))
                            ln2.apply(dve, b, lambda t: [Y[:, t, :]], xt).then_inc(y_ok.sem, 1)
                    run(dve, slot)

        NR = 9 * D2
        GH = 8
        OFF = [0, 1 * 512, 1 * P, 2 * 512]
        OFT = [0, 512, 1024, 512 + 3 * P]
        with ExitStack() as ctx:
            MX = [sb(f"maxima{g}", [P, GH, TB], ctx=ctx) for g in range(2)]
            NM = sb("neg_max", [GH * TB, P], ctx=ctx)
            MR = sb("neg_max_rest", [GH * TB, P], ctx=ctx)
            MP = [sb(f"neg_max_parts{g}", [GH * TB, 3, P], BF16, ctx=ctx) for g in range(2)]
            PT = [sb(f"probs_t{u}", [P, 3 * 512], ctx=ctx) for u in range(2)]
            rec = [sb(f"crec{u}", [P, TB], ctx=ctx) for u in range(2)]
            A = ps("scores_a", [P, 3 * 512], ctx)
            B = ps("scores_b", [P, 3 * 512], ctx)
            O = ps("o_c", [P, TB, D2 + 1], ctx)
            MT = ps("max_t", [P, P], ctx)
            loaded = [steps(f"cat_loaded{u}") for u in range(2)]
            one_ok = steps("cat_ones")
            sc1, red = steps("cat_sc1", 3), steps("cat_red", 3)
            mt, nm, mp = steps("cat_mt"), steps("cat_nm", 4), steps("cat_mp", 1)
            mdma = [steps(f"cat_mdma{g}") for g in range(2)]
            sc2, ex = steps("cat_sc2", 2), steps("cat_ex", 2)
            pv, rc, st = steps("cat_pv"), steps("cat_rec"), steps("cat_store")
            SO = S[:, :, :].rearrange("p n d -> p (n d)").rearrange("p (i m d) -> p i m d", i=TB, d=D2)

            def run(eng, first, second, batch=None, last=None):
                def heads(b, ub, do1, do2, peeled):
                    if batch:
                        batch(b, ub, do1, do2)
                    for g in range(2):
                        def unit(h, uh, cold):
                            if do1:
                                first(b, ub, g, h, uh, cold)
                            if do2:
                                second(b - 1, 1 - ub, g, h, uh, cold and g == 0)
                        lo = 0
                        if first is not None:
                            unit(0, 0, True)
                            unit(1, 1, False)
                            with eng.Fori(1, GH // 2) as hp:
                                for uh in range(2):
                                    unit(hp * 2 + uh, uh, False)
                        if last:
                            last(b, ub, g, do1, do2)
                heads(0, 0, True, False, True)
                heads(1, 1, True, True, True)
                with eng.Fori(1, NB // 2) as bp:
                    for ub in range(2):
                        heads(bp * 2 + ub, ub, True, True, False)
                heads(NB, 0, False, True, True)

            with nc.Block() as block:
                @block.sync
                def _(sp):
                    def load(b, u):
                        for a in range(3):
                            for c in range(3):
                                r = (3 * a + c) * D2
                                for k, dst, part in ((0, QS[u], a), (1, KS[u], c)):
                                    sp.dma_start(dst[r:r + D2, :, :],
                                                 split_dram[b, k, part].rearrange("(h r) s -> r h s", r=D2))\
                                      .then_inc(loaded[u].sem, 16)

                    def batch(b, ub, do1, do2):
                        if do1 and isinstance(b, int):
                            load(b, ub)

                    def maxima(b, ub, g, do1, do2):
                        if do1:
                            n = b * 2 + g
                            sp.wait_ge(mp.sem, mp.at(n))
                            settle(sp, ready)
                            for c in range(3):
                                sp.dma_start(QS[ub][NR + c:NR + c + 1, g * GH:(g + 1) * GH, :]
                                             .rearrange("p h s -> p (h s)"), MP[g][:, c, :]).then_inc(mdma[g].sem, 16)
                    sp.wait_ge(one_ok.sem, 1)
                    for b in range(2):
                        load(b, b)
                        for g in range(2):
                            maxima(b, b, g, True, True)
                    with sp.Fori(1, NB // 2) as bp:
                        for ub in range(2):
                            b = bp * 2 + ub
                            sp.wait_ge(sc2.sem, sc2.at((b - 1) * H2 - 1))
                            settle(sp, ready)
                            load(b, ub)
                            for g in range(2):
                                maxima(b, ub, g, True, True)

                @block.tensor
                def _(pe):
                    pe.wait_ge(one_ok.sem, 1)

                    def first(b, ub, g, h, uh, cold):
                        m = b * H2 + g * GH + h
                        q, k = QS[ub], KS[ub]
                        hh = g * GH + h
                        if cold and g == 0:
                            pe.wait_ge(loaded[ub].sem, ((b - ub) * 8 + 16) * 18)
                        early = cold and g == 0 and isinstance(b, int) and b == 0
                        for s, tiles in enumerate(([3], [1], [0, 2])):
                            if not early:
                                pe.wait_ge(red.sem, red.at(m - 1, s + 1))
                            for i in tiles:
                                o = A[:, OFF[i]:OFF[i] + (i + 1) * P]
                                pe.matmul(o, q[0:NR, hh, i * P:(i + 1) * P], k[0:NR, hh, 0:(i + 1) * P],
                                          start=True, stop=False, skip_group_check=True)
                                last = pe.matmul(o[:, i * P:], mk[:, 4, :], mk[:, 2, :], start=False, stop=True,
                                                 skip_group_check=True)
                            last.then_inc(sc1.sem, 1)

                    def values(m, uh):
                        pe.wait_ge(ex.sem, ex.at(m))
                        for i in range(TB):
                            for j in range(i + 1):
                                c = OFT[j] + (i - j) * P
                                last = pe.matmul(O[:, i, :], PT[uh][:, c:c + P], VP[:, j, m, :],
                                                 start=(j == 0), stop=(j == i), skip_group_check=True)
                        last.then_inc(pv.sem, 1)

                    def second(b, ub, g, h, uh, cold):
                        m = b * H2 + g * GH + h
                        q, k = QS[ub], KS[ub]
                        hh = g * GH + h
                        early = cold and isinstance(b, int) and b == 0
                        if isinstance(h, int) and h == 0:
                            pe.wait_ge(mdma[g].sem, (b + 1) * 48)
                        for s, tiles in enumerate(([0, 1, 3], [2])):
                            if not early:
                                pe.wait_ge(ex.sem, ex.at(m - 1, s + 1))
                            for j in tiles:
                                o = B[:, OFT[j]:OFT[j] + (TB - j) * P]
                                pe.matmul(o, k[0:NR + 3, hh, j * P:(j + 1) * P], q[0:NR + 3, hh, j * P:],
                                          start=True, stop=False, skip_group_check=True)
                                last = pe.matmul(o[:, 0:P], mk[:, 4, :], mk[:, 3, :], start=False, stop=True,
                                                 skip_group_check=True)
                            last.then_inc(sc2.sem, 1)
                        if not early:
                            if not (isinstance(m, int) and m < 2):
                                pe.wait_ge(st.sem, st.at(m - 2))
                            values(m - 1, 1 - uh)

                    def last(b, ub, g, do1, do2):
                        if do1:
                            n = b * 2 + g
                            pe.wait_ge(red.sem, red.at(b * H2 + g * GH + GH - 1))
                            if not (isinstance(b, int) and b == 0 and g == 0):
                                pe.wait_ge(nm.sem, nm.at(n - 1, 1))
                            pe.transpose(MT[0:GH * TB, :], MX[g][:, :, :].rearrange("p h i -> p (h i)"), ident[:, :])\
                              .then_inc(mt.sem, 1)
                    run(pe, first, second, None, last)
                    M = NB * H2 - 1
                    pe.wait_ge(st.sem, st.at(M - 1))
                    values(M, 1)

                @block.scalar
                def _(act):
                    def second(b, ub, g, h, uh, cold):
                        m = b * H2 + g * GH + h
                        act.wait_ge(sc2.sem, sc2.at(m, 1))
                        if not (isinstance(m, int) and m < 2):
                            act.wait_ge(pv.sem, pv.at(m - 2))
                        act.activation(PT[uh][:, 0:1024], B[:, 0:1024], ACT.Exp).then_inc(ex.sem, 1)
                        act.wait_ge(sc2.sem, sc2.at(m, 2))
                        act.activation(PT[uh][:, 1024:1280], B[:, 1024:1280], ACT.Exp).then_inc(ex.sem, 1)

                    def last(b, ub, g, do1, do2):
                        if do1:
                            n = b * 2 + g
                            act.wait_ge(mt.sem, mt.at(n))
                            act.activation(NM[:, :], MT[0:GH * TB, :], ACT.Copy, scale=-1.0).then_inc(nm.sem, 1)
                    run(act, lambda *a: None, second, None, last)

                @block.vector
                def _(dve):
                    for u in range(2):
                        last = dve.memset(KS[u][64:P, :, :], 1.0)
                    last.then_inc(one_ok.sem, 1)

                    def first(b, ub, g, h, uh, cold):
                        m = b * H2 + g * GH + h
                        if isinstance(h, int) and h == 0 and not (isinstance(b, int) and b == 0):
                            dve.wait_ge(mt.sem, mt.at(b * 2 + g - 2))
                        for s, tiles in enumerate(([3], [1], [0, 2])):
                            dve.wait_ge(sc1.sem, sc1.at(m, s + 1))
                            for i in tiles:
                                last = dve.tensor_reduce(MX[g][:, h, i:i + 1], A[:, OFF[i]:OFF[i] + (i + 1) * P], AX, ALU.max)
                            last.then_inc(red.sem, 1)

                    def store(m, uh):
                        dve.wait_ge(pv.sem, pv.at(m))
                        dve.reciprocal(rec[uh][:, :], O[:, :, D2]).then_inc(rc.sem, 1)
                        dve.wait_ge(rc.sem, rc.at(m))
                        dve.tensor_tensor(SO[:, :, m, :], O[:, :, 0:D2], rec[uh][:, :].unsqueeze(2).to_broadcast([P, TB, D2]),
                                          ALU.mult).then_inc(st.sem, 1)

                    def second(b, ub, g, h, uh, cold):
                        m = b * H2 + g * GH + h
                        if not (cold and isinstance(b, int) and b == 0):
                            store(m - 1, 1 - uh)

                    def last(b, ub, g, do1, do2):
                        if do1:
                            n = b * 2 + g
                            dve.wait_ge(nm.sem, nm.at(n, 1))
                            if not (isinstance(b, int) and b == 0):
                                dve.wait_ge(mdma[g].sem, (b - 1) * 48 + 48)
                            dve.tensor_copy(MP[g][:, 0, :], NM[:, :]).then_inc(nm.sem, 1)
                            dve.wait_ge(nm.sem, nm.at(n, 2))
                            dve.tensor_tensor(MR[:, :], NM[:, :], MP[g][:, 0, :], ALU.subtract).then_inc(nm.sem, 1)
                            dve.wait_ge(nm.sem, nm.at(n, 3))
                            dve.tensor_copy(MP[g][:, 1, :], MR[:, :]).then_inc(nm.sem, 1)
                            dve.wait_ge(nm.sem, nm.at(n, 4))
                            dve.tensor_tensor(MP[g][:, 2, :], MR[:, :], MP[g][:, 1, :], ALU.subtract).then_inc(mp.sem, 1)
                    run(dve, first, second, None, last)
                    store(NB * H2 - 1, 1)


def experts(nc, sb, ps, steps, Norm, env):
    NB, X, S, ident, out, NE, ready = (env[k] for k in ("NB", "X", "S", "ident", "out", "NE", "ready"))
    wpr, bpr, cenT, ebias, wrT, br, wsT, bs = (env[k] for k in ("wpr", "bpr", "cenT", "ebias", "wrT", "br", "wsT", "bs"))
    SOV = S[:, :, :].rearrange("p (i b) d -> p i b d", i=TB)
    NS = wsT.shape[1]
    EB = 4
    with ExitStack() as ctx:
        wp = sb("w_proj", [P, D], ctx=ctx)
        bp_ = sb("b_proj", [P, D], ctx=ctx)
        cen = sb("centroids", [P, NE], ctx=ctx)
        eb = sb("expert_bias", [P, NE], ctx=ctx)
        wr = sb("w_routed", [P, NE, D], ctx=ctx)
        ws = sb("w_shared", [P, NS, D], ctx=ctx)
        wss = sb("w_shared_mean", [P, D], ctx=ctx)
        brs = sb("biases", [P, D], ctx=ctx)
        GT = sb("gates_t", [P, SEQ], ctx=ctx)
        iot = sb("iota", [P, NE], ctx=ctx)
        iot_i = sb("iota_i", [P, NE], mybir.dt.int32, ctx=ctx)
        AO = [sb(f"attn_out{u}", [P, TB, D], ctx=ctx) for u in range(2)]
        AT = sb("attn_out_t", [P, SEQ], ctx=ctx)
        PO = sb("proj", [P, TB, D], ctx=ctx)
        T = sb("proj_normed", [P, TB, D], ctx=ctx)
        U = sb("u", [P, TB, D], ctx=ctx)
        UT = sb("u_t", [P, SEQ], ctx=ctx)
        sc = sb("route", [P, TB, NE], ctx=ctx)
        se = sb("route_exp", [P, TB, NE], ctx=ctx)
        sp_ = sb("route_p", [P, TB, NE], ctx=ctx)
        sm = sb("route_stat", [P, 3, TB], ctx=ctx)
        top = sb("top8", [P, TB, 8], ctx=ctx)
        tix = sb("top8_index", [P, TB, 8], mybir.dt.uint32, ctx=ctx)
        tif = sb("top2_index", [P, TB, 2], ctx=ctx)
        g2 = sb("gate_parts", [P, 2, TB, NE], ctx=ctx)
        gt = sb("gates", [P, TB, NE], ctx=ctx)
        ACC = sb("acc", [P, 2, TB, D], ctx=ctx)
        OUT = [sb(f"out{u}", [P, TB, D], ctx=ctx) for u in range(2)]
        TN = sb("out_normed", [P, TB, D], ctx=ctx)
        R = [ps(f"e_ring{k}", [P, SEQ], ctx) for k in range(2)]
        BP = ps("base_ps", [P, TB, D], ctx)
        E = [ps(f"experts{k}", [P, EB, D], ctx) for k in range(4)]
        ln1, ln2, ln3 = Norm("eln1", ctx), Norm("eln2", ctx), Norm("eln3", ctx)
        (w_in, init, ao, at_ps, at, po_ps, po, t_ok, x_ok, u_ok, ut_ps, ut, sc_ps, gt_ok, gtt_ps, gtt, bp_ps, fin) = (
            steps("exp_" + n) for n in ("w_in", "init", "ao", "at_ps", "at", "po_ps", "po", "t_ok", "x_ok", "u_ok",
                                        "ut_ps", "ut", "sc_ps", "gates", "gtt_ps", "gtt", "bp_ps", "fin"))
        rt, rex = steps("exp_route", 6), steps("exp_rex")
        eps_, acc = steps("exp_e", 16), steps("exp_acc", 17)
        n_ok, o_ok = steps("exp_norm"), steps("exp_out")
        shared_w = steps("exp_shared_w")
        chain, tk = steps("exp_chain", 48), steps("exp_topk", 4)
        stored = [steps(f"exp_stored{u}") for u in range(2)]
        NW = 8 + 1
        OV = out.rearrange("b (t p) d -> b p t d", p=P)

        def run(eng, slot, extra=2):
            def one(g, u, n=None):
                has = lambda k: n is None or 0 <= n - k < NB
                slot(g * 2 + u, u, has)
            for n in range(2):
                one(0, n, n)
            with eng.Fori(1, NB // 2) as g:
                for u in range(2):
                    one(g, u)
            for n in range(extra):
                one(NB // 2, n, NB + n)

        with nc.Block() as block:
            @block.sync
            def _(sp):
                row = lambda a, n: a.rearrange("(a n) -> a n", a=1).to_broadcast([P, n])
                sp.wait_ge(init.sem, 2)
                for dst, src in ((wp[:, :], wpr), (bp_[:, :], row(bpr, D)), (cen[:, :], cenT), (eb[:, :], row(ebias, NE)),
                                 (wr[:, :, :], wrT), (ws[:, :, :], wsT), (brs[0:NE, :], br), (brs[32:32 + NS, :], bs)):
                    sp.dma_start(dst, src).then_inc(w_in.sem, 16)

                def slot(b, u, has):
                    if has(2):
                        sp.wait_ge(o_ok.sem, o_ok.at(b - 2))
                        settle(sp, ready)
                        sp.dma_start(OV[b - 2], OUT[u][:, :, :]).then_inc(stored[u].sem, 16)
                run(sp, slot)
                for u in range(2):
                    sp.wait_ge(stored[u].sem, 16 * (NB // 2))

            @block.gpsimd
            def _(pool):
                pool.memset(brs[:, :], 0.0).then_inc(init.sem, 1)
                pool.memset(GT[:, :], 0.0).then_inc(init.sem, 1)
                pool.wait_ge(init.sem, 2)
                pool.memset(GT[32:32 + NS, :], 1.0 / NS).then_inc(init.sem, 1)
                pool.wait_ge(init.sem, 3)
                pool.iota(iot_i[:, :], pattern=[[1, NE]], base=0, channel_multiplier=0).then_inc(init.sem, 1)
                pool.wait_ge(init.sem, 4)
                pool.tensor_copy(iot[:, :], iot_i[:, :]).then_inc(init.sem, 1)

                def slot(b, u, has):
                    if has(0):
                        if has(2):
                            pool.wait_ge(at_ps.sem, at_ps.at(b - 2))
                        settle(pool, ready)
                        pool.tensor_copy(AO[u][:, :, :], SOV[:, :, b, :]).then_inc(ao.sem, 1)
                        ln1.power(pool, b)
                        ln2.power(pool, b)
                    if has(1):
                        ln3.power(pool, b - 1)
                run(pool, slot, 1)

            @block.tensor
            def _(pe):
                pe.wait_ge(w_in.sem, 16 * 8)
                pe.wait_ge(init.sem, 5)
                pe.wait_ge(shared_w.sem, 2)

                def slot(b, u, has):
                    if has(0):
                        pe.wait_ge(ao.sem, ao.at(b))
                        if has(1):
                            pe.wait_ge(gtt.sem, gtt.at(b - 1))
                        for t in range(TB):
                            last = pe.transpose(R[0][:, t * P:(t + 1) * P], AO[u][:, t, :], ident[:, :])
                        last.then_inc(at_ps.sem, 1)
                        pe.wait_ge(at.sem, at.at(b))
                        if has(1):
                            pe.wait_ge(rt.sem, rt.at(b - 1, 1))
                        for t in range(TB):
                            last = pe.matmul(R[1][:, t * P:(t + 1) * P], AT[:, t * P:(t + 1) * P], wp[:, :],
                                             start=True, stop=True)
                        last.then_inc(po_ps.sem, 1)
                    if has(1):
                        n = b - 1
                        for t in range(TB):
                            for k in range(4):
                                if t > 0:
                                    pe.wait_ge(acc.sem, acc.at(n, 4 * (t - 1) + k + 2))
                                elif has(2):
                                    pe.wait_ge(acc.sem, acc.at(n - 1, 4 * 3 + k + 2))
                                pe.matmul(E[k][:, :, :], UT[:, t * P:(t + 1) * P],
                                          wr[:, EB * k:EB * (k + 1), :], start=True, stop=True).then_inc(eps_.sem, 1)
                    if has(0):
                        pe.wait_ge(u_ok.sem, u_ok.at(b))
                        for t in range(TB):
                            last = pe.transpose(R[0][:, t * P:(t + 1) * P], U[:, t, :], ident[:, :])
                        last.then_inc(ut_ps.sem, 1)
                        pe.wait_ge(ut.sem, ut.at(b))
                        pe.wait_ge(po.sem, po.at(b))
                        for t in range(TB):
                            last = pe.matmul(R[1][:, t * NE:(t + 1) * NE], UT[:, t * P:(t + 1) * P], cen[:, :],
                                             start=True, stop=True)
                        last.then_inc(sc_ps.sem, 1)
                        pe.wait_ge(gt_ok.sem, gt_ok.at(b))
                        for t in range(TB):
                            last = pe.transpose(R[0][0:NE, t * P:(t + 1) * P], gt[:, t, :], ident[:, :])
                        last.then_inc(gtt_ps.sem, 1)
                        pe.wait_ge(gtt.sem, gtt.at(b))
                        if has(1):
                            pe.wait_ge(acc.sem, acc.at(b - 1, 1))
                        for t in range(TB):
                            pe.matmul(BP[:, t, :], GT[:, t * P:(t + 1) * P], brs[:, :], start=True, stop=False,
                                      skip_group_check=True)
                            last = pe.matmul(BP[:, t, :], UT[:, t * P:(t + 1) * P], wss[:, :], start=False, stop=True,
                                             skip_group_check=True)
                        last.then_inc(bp_ps.sem, 1)
                run(pe, slot, 1)

            @block.scalar
            def _(act):
                act.wait_ge(w_in.sem, 16 * 8)

                def slot(b, u, has):
                    if has(0):
                        act.wait_ge(at_ps.sem, at_ps.at(b))
                        if has(1):
                            act.wait_ge(po_ps.sem, po_ps.at(b - 1))
                        act.activation(AT[:, :], R[0][:, :], ACT.Copy).then_inc(at.sem, 1)
                        act.wait_ge(ut_ps.sem, ut_ps.at(b))
                        act.activation(UT[:, :], R[0][:, :], ACT.Copy).then_inc(ut.sem, 1)
                        act.wait_ge(rt.sem, rt.at(b, 3))
                        act.activation(se[:, :, :], sc[:, :, :], ACT.Exp).then_inc(rex.sem, 1)
                        act.wait_ge(gtt_ps.sem, gtt_ps.at(b))
                        if has(1):
                            act.wait_ge(bp_ps.sem, bp_ps.at(b - 1))
                        act.activation(GT[0:NE, :], R[0][0:NE, :], ACT.Copy).then_inc(gtt.sem, 1)
                run(act, slot, 1)

            @block.vector
            def _(dve):
                dve.wait_ge(w_in.sem, 16 * 8)
                assert NS == 2
                dve.tensor_tensor(wss[:, :], ws[:, 0, :], ws[:, 1, :], ALU.add).then_inc(shared_w.sem, 1)
                dve.wait_ge(shared_w.sem, 1)
                dve.tensor_scalar(wss[:, :], wss[:, :], 1.0 / NS, None, ALU.mult).then_inc(shared_w.sem, 1)
                dve.wait_ge(init.sem, 5)

                def slot(b, u, has):
                    xt = lambda t: [X[:, b * TB + t, :]]
                    if has(0):
                        dve.wait_ge(po_ps.sem, po_ps.at(b))
                        dve.tensor_tensor(PO[:, :, :], R[1][:, :].rearrange("p (t d) -> p t d", d=D),
                                          bp_[:, :].unsqueeze(1).to_broadcast([P, TB, D]), ALU.add).then_inc(po.sem, 1)
                        dve.wait_ge(po.sem, po.at(b))
                        ln1.stats(dve, b, lambda t: [PO[:, t, :]])
                    if has(1):
                        n = b - 1
                        dve.wait_ge(bp_ps.sem, bp_ps.at(n))
                        dve.tensor_tensor(ACC[:, 0, :, :], BP[:, :, :], U[:, :, :], ALU.add).then_inc(acc.sem, 1)
                        for t in range(TB):
                            for k in range(4):
                                dve.wait_ge(eps_.sem, eps_.at(n, 4 * t + k + 1))
                                dve.wait_ge(acc.sem, acc.at(n, 4 * t + k + 1))
                                for e in range(EB):
                                    i = EB * k + e
                                    last = dve.scalar_tensor_tensor(
                                        ACC[:, (i + 1) % 2, t, :], E[k][:, e, :], gt[:, t, i:i + 1], ACC[:, i % 2, t, :],
                                        ALU.mult, ALU.add)
                                    if e < EB - 1:
                                        last.then_inc(chain.sem, 1)
                                        dve.wait_ge(chain.sem, chain.at(n, 12 * t + 3 * k + e + 1))
                                last.then_inc(acc.sem, 1)
                        dve.wait_ge(acc.sem, acc.at(n))
                        ln3.stats(dve, n, lambda t: [ACC[:, 0, t, :]])
                    if has(0):
                        ln1.apply(dve, b, lambda t: [T[:, t, :]], lambda t: [PO[:, t, :]]).then_inc(t_ok.sem, 1)
                        dve.wait_ge(t_ok.sem, t_ok.at(b))
                        xb = X[:, bass.ds(b * TB, TB), :]
                        dve.tensor_tensor(xb, xb, T[:, :, :], ALU.add).then_inc(x_ok.sem, 1)
                        dve.wait_ge(x_ok.sem, x_ok.at(b))
                        ln2.stats(dve, b, xt)
                    if has(1):
                        n = b - 1
                        if has(3):
                            dve.wait_ge(stored[1 - u].sem, (n - 2 - (1 - u)) * 8 + 16)
                        ln3.apply(dve, n, lambda t: [TN[:, t, :]], lambda t: [ACC[:, 0, t, :]]).then_inc(n_ok.sem, 1)
                        dve.wait_ge(n_ok.sem, n_ok.at(n))
                        dve.tensor_tensor(OUT[1 - u][:, :, :], X[:, bass.ds(n * TB, TB), :], TN[:, :, :], ALU.add)\
                            .then_inc(o_ok.sem, 1)
                    if has(0):
                        ln2.apply(dve, b, lambda t: [U[:, t, :]], xt).then_inc(u_ok.sem, 1)
                        dve.wait_ge(sc_ps.sem, sc_ps.at(b))
                        ebb = eb[:, :].unsqueeze(1).to_broadcast([P, TB, NE])
                        dve.tensor_tensor(sc[:, :, :], R[1][:, 0:TB * NE].rearrange("p (t e) -> p t e", e=NE), ebb, ALU.add)\
                            .then_inc(rt.sem, 1)
                        dve.wait_ge(rt.sem, rt.at(b, 1))
                        dve.tensor_reduce(sm[:, 0, :], sc[:, :, :], AX, ALU.max).then_inc(rt.sem, 1)
                        dve.wait_ge(rt.sem, rt.at(b, 2))
                        bc = lambda k: sm[:, k, :].unsqueeze(2).to_broadcast([P, TB, NE])
                        dve.tensor_tensor(sc[:, :, :], sc[:, :, :], bc(0), ALU.subtract).then_inc(rt.sem, 1)
                        dve.wait_ge(rex.sem, rex.at(b))
                        dve.tensor_reduce(sm[:, 1, :], se[:, :, :], AX, ALU.add).then_inc(rt.sem, 1)
                        dve.wait_ge(rt.sem, rt.at(b, 4))
                        dve.reciprocal(sm[:, 2, :], sm[:, 1, :]).then_inc(rt.sem, 1)
                        dve.wait_ge(rt.sem, rt.at(b, 5))
                        dve.tensor_tensor(sp_[:, :, :], se[:, :, :], bc(2), ALU.mult).then_inc(rt.sem, 1)
                        dve.wait_ge(rt.sem, rt.at(b, 6))
                        settle(dve, ready)
                        for t in range(TB):
                            last = dve.max(top[:, t, :], sp_[:, t, :])
                        last.then_inc(tk.sem, 1)
                        dve.wait_ge(tk.sem, tk.at(b, 1))
                        settle(dve, ready)
                        for t in range(TB):
                            last = dve.max_index(tix[:, t, :], top[:, t, :], sp_[:, t, :])
                        last.then_inc(tk.sem, 1)
                        dve.wait_ge(tk.sem, tk.at(b, 2))
                        dve.tensor_copy(tif[:, :, :], tix[:, :, 0:2]).then_inc(tk.sem, 1)
                        dve.wait_ge(tk.sem, tk.at(b, 3))
                        for k in range(2):
                            for t in range(TB):
                                last = dve.scalar_tensor_tensor(g2[:, k, t, :], iot[:, :], tif[:, t, k:k + 1],
                                                                sp_[:, t, :], ALU.is_equal, ALU.mult)
                        last.then_inc(tk.sem, 1)
                        dve.wait_ge(tk.sem, tk.at(b, 4))
                        dve.tensor_tensor(gt[:, :, :], g2[:, 0, :, :], g2[:, 1, :, :], ALU.add).then_inc(gt_ok.sem, 1)
                run(dve, slot, 1)


def constants():
    half = np.arange(0, 64, 2, dtype=np.float32)
    inv = (np.float32(1.0) / np.float32(10000.0) ** (half / np.float32(64))).astype(np.float32)
    t = np.arange(SEQ, dtype=np.float32)
    fr = (t[:, None] * inv[None, :]).astype(np.float32)
    fr = np.concatenate([fr, fr], -1)
    base = ((half + np.float32(0.4 * 64)) / np.float32(1.4 * 64)).astype(np.float32)
    power = ((t - SEQ // 2) / np.float32(32.0)).astype(np.float32)
    sc = (base[None, :] ** power[:, None]).astype(np.float32)
    sc = np.concatenate([sc, sc], -1)
    cos, sin = np.cos(fr), np.sin(fr)
    sgn = np.concatenate([-np.ones(32, np.float32), np.ones(32, np.float32)])
    tabs = np.stack([cos * sc * 8, cos / sc, sgn * sin * sc * 8, sgn * sin / sc], 1).astype(np.float32)
    rot = np.ascontiguousarray(tabs.reshape(TB, P, 4, 64).transpose(1, 0, 2, 3))
    r, c = np.arange(P)[:, None], np.arange(P)[None, :]
    rr, cc = r % 64, c % 64
    cur, prev = cc <= rr, cc >= rr
    loc = np.where(r < 64, np.where(c < 64, cur, prev), np.where(c < 64, prev, cur))
    loc0 = loc & ~((r < 64) & (c >= 64))
    neg = lambda ok: np.where(ok, 0.0, MASKED)
    eye = np.eye(P)
    mk = np.stack([neg(loc), neg(loc0), neg(c <= r), neg(r <= c), eye], 1).astype(np.float32)
    shift = (c == r + 1).astype(np.float32)
    carry = ((r == P - 1) & (c == 0)).astype(np.float32)
    return {"rot": rot, "mk": mk, "ident": eye.astype(np.float32), "shift": shift, "carry": carry}


ORDER = ["L0_attn_x", "L0_attn_filt", "L0_ffn_wqkv", "L0_ffn_q_scale", "L0_ffn_k_scale", "L0_ffn_wo", "L0_ffn_ln_g",
         "L0_ffn_ln_b", "L0_ffn_w1", "L0_ffn_b1", "L0_ffn_w2", "L0_ffn_b2", "L1_attn_w_attn", "L1_attn_b_attn",
         "L1_attn_w_proj", "L1_attn_b_proj", "L1_ffn_centroids", "L1_ffn_expert_biases", "L1_ffn_Wr", "L1_ffn_br",
         "L1_ffn_Ws", "L1_ffn_bs"]


def build(nc, inputs, stop=99):
    arrays = {}

    def give(name, a):
        arrays[name] = np.ascontiguousarray(a)
        return nc.dram_tensor(name, a.shape, mybir.dt.from_np(arrays[name].dtype), kind="ExternalInput").ap()

    args = []
    for name in ORDER:
        a = np.asarray(inputs[name])
        if name == "L1_ffn_centroids":
            a = a.T
        if name in ("L1_ffn_Wr", "L1_ffn_Ws"):
            a = a.transpose(2, 0, 1)
        args.append(give("in_" + name, a))
    k = constants()
    rot = give("c_rot", k["rot"])
    masks = [give("c_" + n, k[n]) for n in ("mk", "ident", "shift", "carry")]
    shape = np.asarray(inputs["L0_attn_x"]).shape
    out = nc.dram_tensor("out_dram", shape, F32, kind="ExternalOutput").ap()
    program(nc, *args, rot, masks, out, stop=stop)
    return arrays


def kernel(**inputs):
    import concourse.bacc as bacc
    from concourse.bass_utils import run_bass_kernel_spmd

    nc = bacc.Bacc("TRN2", target_bir_lowering=False, num_devices=1)
    arrays = build(nc, inputs)
    r = run_bass_kernel_spmd(nc, [arrays], core_ids=[0])
    return r.results[0]["out_dram"]
```

```python
from contextlib import ExitStack

import numpy as np

import concourse.bass as bass
from concourse import mybir

F32 = mybir.dt.float32
BF16 = mybir.dt.bfloat16
ALU = mybir.AluOpType
ACT = mybir.ActivationFunctionType
AX = mybir.AxisListType.X

P = 128
D = 128
TB = 4
SEQ = TB * P
EPS = 1e-5
MASKED = -1e30


TWO_ONES = float(np.array([0x3F803F80], np.uint32).view(np.float32)[0])


class Steps:

    def __init__(self, sem, per=1):
        self.sem, self.per = sem, per

    def at(self, n, k=None):
        return n * self.per + (self.per if k is None else k)


def settle(eng, ready):
    eng.sem_inc(ready.sem, 1)


def back(b, t, k, unroll):
    return (b, t - k) if t >= k else (b - 1, t - k + unroll)


def program(nc, x, filt, wqkv, qsc, ksc, wo, lng, lnb, w1, b1, w2, b2, wat, bat, wpr, bpr, cenT, ebias,
            wrT, br, wsT, bs, rot, masks, out, stop=99):
    NB = x.shape[0]
    DEPTH = wqkv.shape[0]
    NT = NB * TB
    HEADS, DH = 8, 64
    WIN = 64
    HID = w2.shape[1]
    CH = [min(P, HID - P * c) for c in range(-(-HID // P))]
    NC_ = len(CH)
    TAPS = filt.shape[0]
    H2, D2 = 16, 8
    NE = wrT.shape[1]
    assert x.shape[1:] == (SEQ, D) and TAPS == 2 * P and NB % 4 == 0 and NC_ == 3

    pad = nc.dram_tensor("filter_padded", [4 * P], F32, kind="Internal").ap()
    split_dram = nc.dram_tensor("qk_split", [NB, 2, 3, D, SEQ], BF16, kind="Internal").ap()

    with ExitStack() as whole:
        def sb(name, shape, dt=F32, ctx=whole):
            return ctx.enter_context(nc.sbuf_tensor(name, shape, dt))

        def ps(name, shape, ctx, dt=F32):
            return ctx.enter_context(nc.psum_tensor(name, shape, dt))

        def steps(name, per=1):
            return Steps(whole.enter_context(nc.semaphore(name)), per)

        X = sb("X", [P, NT, D])
        S = sb("S", [P, NT, D])
        ident = sb("ident", [P, P])
        mk = sb("mk", [P, 5, P], BF16)
        mhalf = sb("mhalf", [P, 16])
        ready = steps("marks")

        class Norm:

            def __init__(self, name, ctx, pieces=1, on_act=False):
                self.pieces = pieces
                self.st = sb(name + "_st", [P, TB, pieces, 6], ctx=ctx)
                self.mv = sb(name + "_mv", [P, TB, 2], ctx=ctx)
                self.ve = sb(name + "_ve", [P, TB], ctx=ctx)
                self.rs = sb(name + "_rs", [P, TB], ctx=ctx)
                self.done = steps(name + "_var", 3)
                self.rstd = steps(name + "_rstd")
                if on_act:
                    self.sh = sb(name + "_sh", [P, TB], ctx=ctx)
                    self.shifted = steps(name + "_shifted")

            def stats(self, dve, n, pieces):
                self.pieces_stats(dve, pieces)
                self.aggregate(dve, n)
                self.variance(dve, n)

            def pieces_stats(self, dve, pieces):
                settle(dve, ready)
                for t in range(TB):
                    for k, piece in enumerate(pieces(t)):
                        last = dve.bn_stats(self.st[:, t, k, :], piece)
                last.then_inc(self.done.sem, 1)

            def aggregate(self, dve, n):
                dve.wait_ge(self.done.sem, self.done.at(n, 1))
                settle(dve, ready)
                for t in range(TB):
                    last = dve.bn_aggr(self.mv[:, t, :], self.st[:, t, :, :].rearrange("p k s -> p (k s)"))
                last.then_inc(self.done.sem, 1)

            def variance(self, dve, n):
                dve.wait_ge(self.done.sem, self.done.at(n, 2))
                dve.tensor_scalar(self.ve[:, :], self.mv[:, :, 1], EPS, None, ALU.add).then_inc(self.done.sem, 1)

            def power(self, pool, n):
                pool.wait_ge(self.done.sem, self.done.at(n))
                pool.tensor_tensor(self.rs[:, :], self.ve[:, :], mhalf[:, 0:TB], ALU.pow).then_inc(self.rstd.sem, 1)

            def apply(self, dve, n, outs, pieces):
                dve.wait_ge(self.rstd.sem, self.rstd.at(n))
                for t in range(TB):
                    for o, i in zip(outs(t), pieces(t)):
                        last = dve.tensor_scalar(o, i, self.mv[:, t, 0:1], self.rs[:, t:t + 1],
                                                 ALU.subtract, ALU.mult)
                return last

            def shift(self, dve, n):
                dve.wait_ge(self.rstd.sem, self.rstd.at(n))
                dve.scalar_tensor_tensor(self.sh[:, :], self.mv[:, :, 0], -1.0, self.rs[:, :], ALU.mult, ALU.mult)\
                   .then_inc(self.shifted.sem, 1)

            def apply_act(self, act, n, outs, pieces):
                act.wait_ge(self.shifted.sem, self.shifted.at(n))
                for t in range(TB):
                    for o, i in zip(outs(t), pieces(t)):
                        last = act.activation(o, i, ACT.Identity, bias=self.sh[:, t:t + 1], scale=self.rs[:, t:t + 1])
                return last

        with ExitStack() as ctx:
            hank = sb("hankel", [P, 3 * P], ctx=ctx)
            toep = sb("toeplitz", [P, 3, P], ctx=ctx)
            zero = sb("zero_row", [1, P], ctx=ctx)
            mkf = sb("masks_f32", [P, 5, P], ctx=ctx)
            Y = [sb(f"conv_in{u}", [P, SEQ], ctx=ctx) for u in range(2)]
            T = sb("conv_normed", [P, TB, D], ctx=ctx)
            C = [ps(f"conv_out{u}", [P, SEQ], ctx) for u in range(2)]
            lnA, lnB, lnC = (Norm(f"ln{c}", ctx) for c in "abc")
            consts = steps("constants")
            x_in = [steps(f"x_in{j}") for j in range(4)]
            zeroed = steps("zeroed")
            padded = steps("padded")
            hank_in = steps("hankel_in")
            toep_ok = steps("toeplitz_built")
            half_ok = steps("half_set")
            y_ok = steps("conv_in_ready")
            conv = steps("conv_done")
            t_ok = steps("conv_normed_ready")
            x_ok = steps("x_updated")
            s_ok = steps("stream_ready")
            XV = x.rearrange("b (t p) d -> b p t d", p=P)

            with nc.Block() as block:
                @block.sync
                def _(sp):
                    sp.wait_ge(zeroed.sem, 1)
                    for o in (0, 3 * P):
                        sp.dma_start(pad[o:o + P].rearrange("(a n) -> a n", a=1), zero[:, :]).then_inc(padded.sem, 16)
                    sp.dma_start(pad[P:3 * P].rearrange("(a n) -> a n", a=1),
                                 filt.rearrange("(a n) -> a n", a=1)).then_inc(padded.sem, 16)
                    sp.wait_ge(padded.sem, 48)
                    rows = bass.AP(pad.tensor, 1, [[1, P], [1, 3 * P]])
                    sp.dma_start(hank[:, :], rows).then_inc(hank_in.sem, 16)

                @block.scalar
                def _(act):
                    act.dma_start(ident[:, :], masks[1]).then_inc(consts.sem, 16)
                    act.dma_start(mkf[:, :, :], masks[0]).then_inc(consts.sem, 16)

                    def load(b, j):
                        act.dma_start(X[:, bass.ds(b * TB, TB), :], XV[b]).then_inc(x_in[j].sem, 16)
                    for j in range(4):
                        load(j, j)
                    with act.Fori(1, NB // 4) as g:
                        for j in range(4):
                            act.wait_ge(lnA.done.sem, lnA.done.at(g * 4 + j - 4))
                            load(g * 4 + j, j)
                    act.wait_ge(consts.sem, 32)
                    act.activation(mk[:, :, :], mkf[:, :, :], ACT.Copy)

                @block.gpsimd
                def _(pool):
                    pool.memset(mhalf[:, :], -0.5).then_inc(half_ok.sem, 1)
                    pool.wait_ge(half_ok.sem, 1)

                    def slot(b, first):
                        lnA.power(pool, b)
                        if not first:
                            lnC.power(pool, b - 1)
                        lnB.power(pool, b)
                    slot(0, True)
                    with pool.Fori(1, NB) as b:
                        slot(b, False)
                    lnC.power(pool, NB - 1)

                @block.vector
                def _(dve):
                    dve.memset(zero[:, :], 0.0).then_inc(zeroed.sem, 1)
                    dve.wait_ge(hank_in.sem, 16)
                    for j in range(3):
                        last = dve.tensor_copy(toep[:, j, :], hank[:, j * P:(j + 1) * P][:, ::-1])
                    last.then_inc(toep_ok.sem, 1)

                    def first_norm(b, j, fresh):
                        xt = lambda t: [X[:, b * TB + t, :]]
                        if fresh is not None:
                            dve.wait_ge(x_in[j].sem, fresh)
                        lnA.stats(dve, b, xt)

                    def residual(b, u):
                        lnB.apply(dve, b, lambda t: [T[:, t, :]], lambda t: [C[u][:, t * P:(t + 1) * P]])\
                            .then_inc(t_ok.sem, 1)
                        dve.wait_ge(t_ok.sem, t_ok.at(b))
                        dve.tensor_tensor(X[:, bass.ds(b * TB, TB), :], X[:, bass.ds(b * TB, TB), :], T[:, :, :],
                                          ALU.add).then_inc(x_ok.sem, 1)
                        dve.wait_ge(x_ok.sem, x_ok.at(b))
                        lnC.stats(dve, b, lambda t: [X[:, b * TB + t, :]])

                    def stream(b):
                        lnC.apply(dve, b, lambda t: [S[:, b * TB + t, :]], lambda t: [X[:, b * TB + t, :]])\
                            .then_inc(s_ok.sem, 1)

                    def slot(b, j, loads, first, warm):
                        u = j % 2
                        first_norm(b, j, loads)
                        if not first:
                            residual(b - 1, 1 - u)
                        if warm:
                            dve.wait_ge(conv.sem, conv.at(b - 2))
                        lnA.apply(dve, b, lambda t: [Y[u][:, t * P:(t + 1) * P]], lambda t: [X[:, b * TB + t, :]])\
                            .then_inc(y_ok.sem, 1)
                        if not first:
                            stream(b - 1)
                        dve.wait_ge(conv.sem, conv.at(b))
                        lnB.stats(dve, b, lambda t: [C[u][:, t * P:(t + 1) * P]])

                    for j in range(4):
                        slot(j, j, 16, j == 0, j >= 2)
                    with dve.Fori(1, NB // 4) as g:
                        for j in range(4):
                            slot(g * 4 + j, j, g * 16 + 16, False, True)
                    residual(NB - 1, 1)
                    stream(NB - 1)

                @block.tensor
                def _(pe):
                    pe.wait_ge(toep_ok.sem, 1)

                    def slot(b, u, warm):
                        pe.wait_ge(y_ok.sem, y_ok.at(b))
                        if warm:
                            pe.wait_ge(t_ok.sem, t_ok.at(b - 2))
                        for j in range(3):
                            last = pe.matmul(C[u][:, 0:(TB - j) * P], toep[:, j, :], Y[u][:, j * P:SEQ],
                                             start=(j == 0), stop=(j == 2), skip_group_check=True)
                        last.then_inc(conv.sem, 1)
                    slot(0, 0, False)
                    slot(1, 1, False)
                    with pe.Fori(1, NB // 2) as g:
                        for u in range(2):
                            slot(g * 2 + u, u, True)

        if stop <= 1:
            return dump(nc, out, S if stop else X, NB)

        with ExitStack() as layers:
            rotc = sb("rot_const", [P, TB, 4, DH], ctx=layers)
            rot_in = steps("rot_in")
            shiftm = sb("shift", [P, 2, P], ctx=layers)
            shift_in = steps("shift_in")
            VN = [sb(f"v{t}", [P, HEADS, DH + 1], ctx=layers) for t in range(TB)]
            KZ = sb("kz", [P, 2, HEADS, P], ctx=layers)
            HT = [sb(f"ht{t}", [P, P], ctx=layers) for t in range(TB)]
            zcol = sb("zero_col", [P, 1], ctx=layers)
            init = steps("layers_init")
            with nc.Block() as block:
                @block.sync
                def _(sp):
                    sp.dma_start(rotc[:, :, :, :], rot).then_inc(rot_in.sem, 16)
                    for k in range(2):
                        sp.dma_start(shiftm[:, k, :], masks[2 + k]).then_inc(shift_in.sem, 16)
                    sp.wait_ge(rot_in.sem, 16)
                    sp.wait_ge(shift_in.sem, 32)

                @block.vector
                def _(dve):
                    for v in VN:
                        dve.memset(v[:, :, :], 1.0)
                    dve.memset(KZ[:, :, :, :], 0.0)
                    dve.memset(zcol[:, :], 0.0)
                    dve.memset(HT[0][:, 0:1], 0.0).then_inc(init.sem, 1)
                    dve.wait_ge(init.sem, 1)
            env = dict(locals())
            sems_a, sems_f = attention_sems(steps), ffn_sems(steps, Norm, layers)
            with nc.Fori(0, DEPTH) as L:
                local_attention(nc, L, sb, ps, steps, sems_a, env)
                if stop > 2:
                    feed_forward(nc, L, sb, ps, steps, sems_f, env)
        if stop <= 3:
            return dump(nc, out, S, NB)
        env = dict(locals())
        causal_attention(nc, sb, ps, steps, Norm, env)
        if stop <= 4:
            return dump(nc, out, S, NB)
        experts(nc, sb, ps, steps, Norm, env)


def dump(nc, out, S, NB):
    with nc.semaphore("dumped") as dumped, nc.Block() as block:
        @block.sync
        def _(sp):
            for b in range(NB):
                sp.dma_start(out[b].rearrange("(t p) d -> p t d", p=P), S[:, b * TB:(b + 1) * TB, :]).then_inc(dumped, 16)
            sp.wait_ge(dumped, 16 * NB)


def attention_sems(steps):
    per = dict(w_in=1, tab=2, xst=1, hps=1, ht=1, qkps=2, vps=1, sq=2, rn=1, d1=4, tq=1, tk=1, eq=1, ek=1, ev=1, sc=1, radd=1,
               d2=2, ex=1, pt=2, ept=2, pv=1, d3=2, ot=1, eot=1, wo=1, xadd=1)
    made = {k: steps("att_" + k, v) for k, v in per.items()}
    made["vx"] = [steps(f"att_vx{t}") for t in range(TB)]
    return made


def local_attention(nc, L, sb, ps, steps, q, env):
    NB, NT, S, ident, mk, mhalf = (env[k] for k in ("NB", "NT", "S", "ident", "mk", "mhalf"))
    HEADS, DH, WIN, ready = env["HEADS"], env["DH"], env["WIN"], env["ready"]
    VN, KZ, HT, zcol, rotc = (env[k] for k in ("VN", "KZ", "HT", "zcol", "rotc"))
    wqkv, qsc, ksc, wo = (env[k] for k in ("wqkv", "qsc", "ksc", "wo"))
    INNER = HEADS * DH
    NG = INNER // P
    LAST = 4
    with ExitStack() as ctx:
        wq = sb("wq", [P, 3 * INNER], ctx=ctx)
        wot = sb("wo", [P, NG, D], ctx=ctx)
        scb = sb("qk_scales", [P, 4, DH], ctx=ctx)
        tab = sb("rot_scaled", [P, TB, 4, DH], ctx=ctx)
        xst = [sb(f"xst{u}", [P, P], ctx=ctx) for u in range(2)]
        SQ = sb("squares", [P, 2 * INNER], ctx=ctx)
        ss = sb("sumsq", [P, 16], ctx=ctx)
        rn = sb("rnorm", [P, 16], ctx=ctx)
        A1 = sb("rot_a", [P, 2 * INNER], ctx=ctx)
        A2 = sb("rot_b", [P, 2 * INNER], ctx=ctx)
        QKN = sb("qk_normed", [P, 2 * INNER], ctx=ctx)
        QT = sb("qt", [P, NG, P], ctx=ctx)
        VX = [sb(f"vx{t}", [P, HEADS, DH + 1], ctx=ctx) for t in range(TB)]
        mx = sb("score_max", [P, HEADS], ctx=ctx)
        SS = sb("scores_less_max", [P, HEADS, P], ctx=ctx)
        PP = sb("probs", [P, HEADS, P], ctx=ctx)
        PT = sb("probs_t", [P, HEADS, P], ctx=ctx)
        rec = sb("rec", [P, HEADS], ctx=ctx)
        ON = sb("o_normed", [P, HEADS, DH], ctx=ctx)
        OT = sb("o_t", [P, NG, P], ctx=ctx)
        QK = ps("qk_ps", [P, 2 * INNER], ctx)
        R = [ps(f"ring{k}", [P, 512], ctx) for k in range(2)]
        SC = ps("scores_ps", [P, HEADS, P], ctx)
        OP = ps("o_ps", [P, 2, 512], ctx)
        OH = OP[:, :, 0:4 * (DH + 1)].rearrange("p b (h d) -> p b h d", d=DH + 1)
        base = L * NT

        def num(b, t):
            return base + b * TB + t

        def run(eng, slot):
            def one(b, t, n=None):
                has = lambda k: n is None or 0 <= n - k < NT
                slot(b, t, lambda k: num(*back(b, t, k, TB)) if k <= TB else num(*back(b - 1, t, k - TB, TB)), has)
            for t in range(TB):
                one(0, t, t)
            with eng.Fori(1, NB) as b:
                for t in range(TB):
                    one(b, t)
            for t in range(LAST):
                one(NB, t, NT + t)

        USES = [("h", 0, 0, "ht", 1), ("q", 2, 1, "eq", 1), ("k", 2, 0, "ek", 1), ("v", 1, 1, "ev", 1),
                ("p0", 3, 0, "ept", 1), ("p1", 3, 1, "ept", 2), ("o", 4, 0, "eot", 1), ("w", 4, 1, "xadd", 1)]
        HP, WP = R[0][:, 0:P], R[1][:, 0:P]

        def ring_wait(pe, use, item, has):
            at = [u[0] for u in USES].index(use)
            bank = USES[at][2]
            earlier = [(u, 0) for u in USES[:at][::-1]] + [(u, 1) for u in USES[::-1]] + [(u, 2) for u in USES[::-1]]
            for (name, lag, bk, sem, step), slots in earlier:
                if bk == bank and has(lag + slots):
                    pe.wait_ge(q[sem].sem, q[sem].at(item(lag + slots), step))
                    return

        with nc.Block() as block:
            @block.sync
            def _(sp):
                sp.dma_start(wq[:, :], wqkv[L]).then_inc(q["w_in"].sem, 16)
                sp.dma_start(wot[:, :, :], wo[L].rearrange("(c p) d -> p c d", p=P)).then_inc(q["w_in"].sem, 16)
                for k, src in enumerate((qsc, ksc)):
                    row = src[L].rearrange("(a n) -> a n", a=1)
                    half = DH // 2
                    sp.dma_start(scb[:, k, :], row.to_broadcast([P, DH]))\
                      .then_inc(q["w_in"].sem, 16)
                    for h in range(2):
                        sp.dma_start(scb[:, 2 + k, h * half:(h + 1) * half],
                                     row[:, (1 - h) * half:(2 - h) * half].to_broadcast([P, half]))\
                          .then_inc(q["w_in"].sem, 16)

                def slot(b, t, item, has):
                    if has(1):
                        bb, t1 = back(b, t, 1, TB)
                        sp.wait_ge(q["ev"].sem, q["ev"].at(item(1)))
                        settle(sp, ready)
                        if has(5):
                            sp.wait_ge(q["pv"].sem, q["pv"].at(item(5)))
                        settle(sp, ready)
                        for lo, src in ((0, VN[t1]), (WIN, VN[(t1 - 1) % TB])):
                            sp.dma_start(VX[t1][lo:lo + WIN, :, :], src[lo:lo + WIN, :, :]).then_inc(q["vx"][t1].sem, 16)
                run(sp, slot)

            @block.gpsimd
            def _(pool):
                def slot(b, t, item, has):
                    if has(0):
                        if has(2):
                            pool.wait_ge(q["hps"].sem, q["hps"].at(item(2)))
                        settle(pool, ready)
                        pool.tensor_copy(xst[t % 2][:, :], S[:, b * TB + t, :]).then_inc(q["xst"].sem, 1)
                    if has(1):
                        pool.wait_ge(q["d1"].sem, q["d1"].at(item(1), 1))
                        pool.tensor_tensor(A1[:, :], A1[:, :], A2[:, :], ALU.add).then_inc(q["radd"].sem, 1)
                        pool.wait_ge(q["d1"].sem, q["d1"].at(item(1), 3))
                        pool.tensor_tensor(rn[:, :], ss[:, :], mhalf[:, :], ALU.pow).then_inc(q["rn"].sem, 1)
                run(pool, slot)

            @block.tensor
            def _(pe):
                pe.wait_ge(q["w_in"].sem, (L + 1) * (16 * 8))

                def slot(b, t, item, has):
                    if has(1):
                        pe.wait_ge(q["ht"].sem, q["ht"].at(item(1)))
                        if has(2):
                            pe.wait_ge(q["d1"].sem, q["d1"].at(item(2), 1))
                            pe.wait_ge(q["sq"].sem, q["sq"].at(item(2)))
                        for k in range(2):
                            last = pe.matmul(QK[:, k * INNER:(k + 1) * INNER], HT[(t - 1) % TB][:, :],
                                             wq[:, k * INNER:(k + 1) * INNER], start=True, stop=True)
                            last.then_inc(q["qkps"].sem, 1)
                    if has(0):
                        pe.wait_ge(q["xst"].sem, q["xst"].at(item(0)))
                        ring_wait(pe, "h", item, has)
                        pe.transpose(HP, xst[t % 2][:, :], ident[:, :]).then_inc(q["hps"].sem, 1)
                    if has(2):
                        pe.wait_ge(q["d1"].sem, q["d1"].at(item(2)))
                        for k, (use, done) in enumerate((("q", "tq"), ("k", "tk"))):
                            ring_wait(pe, use, item, has)
                            for p in range(NG):
                                last = pe.transpose(R[1 - k][:, p * P:(p + 1) * P],
                                                    QKN[:, k * INNER + p * P:k * INNER + (p + 1) * P], ident[:, :])
                            last.then_inc(q[done].sem, 1)
                    if has(1):
                        ring_wait(pe, "v", item, has)
                        pe.matmul(R[1][:, :], HT[(t - 1) % TB][:, :], wq[:, 2 * INNER:], start=True, stop=True)\
                            .then_inc(q["vps"].sem, 1)
                    if has(2):
                        t2 = (t - 2) % TB
                        u = t2 % 2
                        if has(3):
                            pe.wait_ge(q["d2"].sem, q["d2"].at(item(3)))
                        for h4 in (0, 4):
                            pe.matmul(SC[:, h4:h4 + 4, :], mk[:, 4, :],
                                      mk[:, 1 if t2 == 0 else 0, :].unsqueeze(1).to_broadcast([P, 4, P]),
                                      start=True, stop=False, skip_group_check=True)
                        pe.wait_ge(q["eq"].sem, q["eq"].at(item(2)))
                        pe.wait_ge(q["ek"].sem, q["ek"].at(item(2)))
                        for h in range(HEADS):
                            qt = QT[:, h // 2, :]
                            own = KZ[:, u, h, 0:WIN]
                            mixed = bass.AP(own.tensor, own.offset,
                                            [list(own.ap[0]), [(1 - 2 * u) * HEADS * P + WIN, 2], [1, WIN]])
                            pe.matmul(SC[0:WIN, h, :], qt[:, 0:WIN], mixed, start=False, stop=True, skip_group_check=True)
                            last = pe.matmul(SC[WIN:P, h, :], qt[:, WIN:P], KZ[:, u, h, :],
                                             start=False, stop=True, skip_group_check=True)
                        last.then_inc(q["sc"].sem, 1)
                    if has(3):
                        pe.wait_ge(q["ex"].sem, q["ex"].at(item(3)))
                        for k in range(2):
                            ring_wait(pe, f"p{k}", item, has)
                            for p in range(4):
                                last = pe.transpose(R[k][:, p * P:(p + 1) * P], PP[:, 4 * k + p, :], ident[:, :])
                            last.then_inc(q["pt"].sem, 1)
                    if has(4):
                        pe.wait_ge(q["d3"].sem, q["d3"].at(item(4)))
                        ring_wait(pe, "o", item, has)
                        for p in range(NG):
                            last = pe.transpose(R[0][:, p * P:(p + 1) * P],
                                                ON[:, 2 * p:2 * p + 2, :].rearrange("p a b -> p (a b)"), ident[:, :])
                        last.then_inc(q["ot"].sem, 1)
                    if has(3):
                        bb, t3 = back(b, t, 3, TB)
                        pe.wait_ge(q["vx"][t3].sem, (L * NB + bb) * 32 + 32)
                        if has(4):
                            pe.wait_ge(q["d3"].sem, q["d3"].at(item(4)))
                        for h in range(HEADS):
                            if h % 4 == 0:
                                pe.wait_ge(q["ept"].sem, q["ept"].at(item(3), 1 + h // 4))
                            o = OH[:, h // 4, h % 4, :]
                            pe.matmul(o[WIN:P, :], PT[:, h, WIN:P], VN[t3][:, h, :], start=True, stop=True)
                            last = pe.matmul(o[0:WIN, :], PT[:, h, 0:WIN], VX[t3][:, h, :], start=True, stop=True)
                        last.then_inc(q["pv"].sem, 1)
                    if has(4):
                        pe.wait_ge(q["eot"].sem, q["eot"].at(item(4)))
                        ring_wait(pe, "w", item, has)
                        for c in range(NG):
                            last = pe.matmul(WP, OT[:, c, :], wot[:, c, :], start=(c == 0), stop=(c == NG - 1))
                        last.then_inc(q["wo"].sem, 1)
                run(pe, slot)

            @block.scalar
            def _(act):
                def slot(b, t, item, has):
                    if has(1):
                        if has(2):
                            act.wait_ge(q["d1"].sem, q["d1"].at(item(2), 2))
                        for k in range(2):
                            io = slice(k * INNER, (k + 1) * INNER)
                            act.wait_ge(q["qkps"].sem, q["qkps"].at(item(1), k + 1))
                            act.activation(SQ[:, io], QK[:, io], ACT.Square).then_inc(q["sq"].sem, 1)
                    if has(0):
                        act.wait_ge(q["hps"].sem, q["hps"].at(item(0)))
                        nxt = HT[(t + 1) % TB]
                        act.activation(HT[t][0:64, :], HP[0:64, :], ACT.Copy)
                        act.activation(HT[t][64:P, 1:P], HP[64:P, 0:P - 1], ACT.Copy)
                        act.activation(nxt[64:P, 0:1], HP[64:P, P - 1:P] if t < TB - 1 else zcol[64:P, :], ACT.Copy)\
                            .then_inc(q["ht"].sem, 1)
                    if has(2):
                        u = t % 2
                        act.wait_ge(q["tq"].sem, q["tq"].at(item(2)))
                        if has(3):
                            act.wait_ge(q["sc"].sem, q["sc"].at(item(3)))
                        act.activation(QT[:, :, :].rearrange("p a b -> p (a b)"), R[1][:, :], ACT.Copy)\
                            .then_inc(q["eq"].sem, 1)
                        act.wait_ge(q["tk"].sem, q["tk"].at(item(2)))
                        for half in range(2):
                            r = slice(64 * half, 64 * half + 64)
                            last = act.activation(
                                KZ[r, u, :, :].rearrange("p (a two) k -> p a two k", two=2)[:, :, half, :],
                                R[0][r, :].rearrange("p (a k) -> p a k", k=P), ACT.Copy)
                        last.then_inc(q["ek"].sem, 1)
                    if has(1):
                        t1 = (t - 1) % TB
                        act.wait_ge(q["vps"].sem, q["vps"].at(item(1)))
                        act.activation(VN[t1][:, :, 0:DH], R[1][:, :].rearrange("p (h d) -> p h d", d=DH), ACT.Copy)\
                            .then_inc(q["ev"].sem, 1)
                    if has(3):
                        for k in range(2):
                            act.wait_ge(q["pt"].sem, q["pt"].at(item(3), k + 1))
                            if has(4) and k == 0:
                                act.wait_ge(q["pv"].sem, q["pv"].at(item(4)))
                            act.activation(PT[:, 4 * k:4 * k + 4, :].rearrange("p a b -> p (a b)"), R[k][:, :],
                                           ACT.Copy).then_inc(q["ept"].sem, 1)
                    if has(4):
                        act.wait_ge(q["ot"].sem, q["ot"].at(item(4)))
                        if has(5):
                            act.wait_ge(q["wo"].sem, q["wo"].at(item(5)))
                        act.activation(OT[:, :, :].rearrange("p a b -> p (a b)"), R[0][:, :], ACT.Copy)\
                            .then_inc(q["eot"].sem, 1)
                    if has(2):
                        act.wait_ge(q["d2"].sem, q["d2"].at(item(2)))
                        if has(3):
                            act.wait_ge(q["pt"].sem, q["pt"].at(item(3)))
                        act.activation(PP[:, :, :], SS[:, :, :], ACT.Exp).then_inc(q["ex"].sem, 1)
                run(act, slot)

            @block.vector
            def _(dve):
                dve.wait_ge(q["w_in"].sem, (L + 1) * (16 * 8))
                for t in range(TB):
                    last = dve.tensor_tensor(tab[:, t, :, :], rotc[:, t, :, :], scb[:, :, :], ALU.mult)
                last.then_inc(q["tab"].sem, 2)
                dve.wait_ge(q["tab"].sem, L * 2 + 2)
                qk4 = lambda a: a.rearrange("p (k h d) -> p k h d", k=2, d=DH)

                def slot(b, t, item, has):
                    if has(1):
                        t1 = (t - 1) % TB
                        d1 = q["d1"]
                        half = DH // 2
                        if has(2):
                            dve.wait_ge(d1.sem, d1.at(item(2)))
                        for k in range(2):
                            dve.wait_ge(q["sq"].sem, q["sq"].at(item(1), k + 1))
                            io = slice(k * INNER, (k + 1) * INNER)
                            hd = lambda a: a[:, io].rearrange("p (h d) -> p h d", d=DH)
                            bc = lambda c, lo, hi: tab[:, t1, c, lo:hi].unsqueeze(1).to_broadcast([P, HEADS, hi - lo])
                            dve.tensor_tensor(hd(A1), hd(QK), bc(k, 0, DH), ALU.mult)
                            for h in range(2):
                                lo, sw = h * half, (1 - h) * half
                                last = dve.tensor_tensor(hd(A2)[:, :, lo:lo + half], hd(QK)[:, :, sw:sw + half],
                                                         bc(2 + k, lo, lo + half), ALU.mult)
                        last.then_inc(d1.sem, 1)
                        dve.tensor_reduce(ss[:, :], SQ[:, :].rearrange("p (h d) -> p h d", d=DH), AX, ALU.add)\
                            .then_inc(d1.sem, 1)
                        dve.wait_ge(d1.sem, d1.at(item(1), 2))
                        dve.tensor_scalar(ss[:, :], ss[:, :], 1e-24, None, ALU.max).then_inc(d1.sem, 1)
                    if has(2):
                        d2 = q["d2"]
                        dve.wait_ge(q["sc"].sem, q["sc"].at(item(2)))
                        dve.tensor_reduce(mx[:, :], SC[:, :, :], AX, ALU.max).then_inc(d2.sem, 1)
                        dve.wait_ge(d2.sem, d2.at(item(2), 1))
                        if has(3):
                            dve.wait_ge(q["ex"].sem, q["ex"].at(item(3)))
                        dve.tensor_tensor(SS[:, :, :], SC[:, :, :], mx[:, :].unsqueeze(2).to_broadcast([P, HEADS, P]),
                                          ALU.subtract).then_inc(d2.sem, 1)
                    if has(3):
                        d3 = q["d3"]
                        dve.wait_ge(q["pv"].sem, q["pv"].at(item(3)))
                        rech = rec[:, :].rearrange("p (b h) -> p b h", b=2)
                        dve.reciprocal(rech, OH[:, :, :, DH]).then_inc(d3.sem, 1)
                        dve.wait_ge(d3.sem, d3.at(item(3), 1))
                        if has(4):
                            dve.wait_ge(q["ot"].sem, q["ot"].at(item(4)))
                        dve.tensor_tensor(ON[:, :, :].rearrange("p (b h) d -> p b h d", b=2), OH[:, :, :, 0:DH],
                                          rech.unsqueeze(3).to_broadcast([P, 2, 4, DH]), ALU.mult)\
                            .then_inc(d3.sem, 1)
                    if has(4):
                        bb, t4 = b - 1, t
                        dve.wait_ge(q["wo"].sem, q["wo"].at(item(4)))
                        xs = S[:, bb * TB + t4, :]
                        dve.tensor_tensor(xs, xs, WP, ALU.add).then_inc(q["xadd"].sem, 1)
                    if has(1):
                        d1 = q["d1"]
                        dve.wait_ge(q["radd"].sem, q["radd"].at(item(1)))
                        dve.wait_ge(q["rn"].sem, q["rn"].at(item(1)))
                        if has(2):
                            dve.wait_ge(q["tk"].sem, q["tk"].at(item(2)))
                        dve.tensor_tensor(QKN[:, :].rearrange("p (h d) -> p h d", d=DH),
                                          A1[:, :].rearrange("p (h d) -> p h d", d=DH),
                                          rn[:, :].unsqueeze(2).to_broadcast([P, 16, DH]), ALU.mult)\
                            .then_inc(d1.sem, 1)
                run(dve, slot)


def ffn_sems(steps, Norm, ctx):
    per = dict(w_in=1, sh=1, hb=1, tp=1, ht=1, g=3, a=3, ge=3, z=3, w2=1, xb=1, upd=1)
    made = {k: steps("ffn_" + k, v) for k, v in per.items()}
    made["ln"] = Norm("ffn_ln", ctx, 2)
    return made


def feed_forward(nc, L, sb, ps, steps, q, env):
    NB, S, ident, shiftm, CH, HID = (env[k] for k in ("NB", "S", "ident", "shiftm", "CH", "HID"))
    lng, lnb, w1, b1, w2, b2 = (env[k] for k in ("lng", "lnb", "w1", "b1", "w2", "b2"))
    ln = q["ln"]
    NCH = len(CH)
    HALF = D // 2
    with ExitStack() as ctx:
        w1t = sb("w1", [P, 2 * HID], ctx=ctx)
        w2t = sb("w2", [P, NCH, D], ctx=ctx)
        gb = sb("ln_gb", [P, 2], ctx=ctx)
        b1t = sb("b1", [P, 2, NCH], ctx=ctx)
        b2t = sb("b2", [P, D], ctx=ctx)
        HB = sb("h_normed", [P, TB, D], ctx=ctx)
        HF = sb("h_t", [P, SEQ], ctx=ctx)
        GE = [sb(f"gelu{k}", [P, SEQ], ctx=ctx) for k in range(2)]
        Z = [[sb(f"z{u}_{c}", [P, SEQ], ctx=ctx) for c in range(NCH)] for u in range(2)]
        XB = [sb(f"x_b2_{u}", [P, TB, D], ctx=ctx) for u in range(2)]
        SH = ps("shifted", [P, TB, HALF], ctx)
        TP = ps("h_t_ps", [P, SEQ], ctx)
        GP = [ps(f"g_ps{k}", [P, SEQ], ctx) for k in range(2)]
        AP_ = [ps(f"a_ps{k}", [P, SEQ], ctx) for k in range(2)]
        OB = ps("ffn_out", [P, TB, D], ctx)
        base = L * NB
        NW = 4 + 1 + 2 * NCH + NCH

        def run(eng, slot):
            def one(g, u, n=None):
                has = lambda k: n is None or 0 <= n - k < NB
                slot(g * 2 + u, u, has)
            for n in range(2):
                one(0, n, n)
            with eng.Fori(1, NB // 2) as g:
                for u in range(2):
                    one(g, u)
            for n in range(2):
                one(NB // 2, n, NB + n)

        with nc.Block() as block:
            @block.sync
            def _(sp):
                def load(dst, src):
                    sp.dma_start(dst, src).then_inc(q["w_in"].sem, 16)
                load(w1t[:, :], w1[L])
                for c, n in enumerate(CH):
                    load(w2t[0:n, c, :], w2[L, c * P:c * P + n, :])
                    for k in range(2):
                        load(b1t[0:n, k, c:c + 1], b1[L, k * HID + c * P:k * HID + c * P + n].rearrange("(n a) -> n a", a=1))
                load(gb[:, 0:1], lng[L].rearrange("(n a) -> n a", a=1))
                load(gb[:, 1:2], lnb[L].rearrange("(n a) -> n a", a=1))
                load(b2t[:, :], b2[L].rearrange("(a n) -> a n", a=1).to_broadcast([P, D]))
                sp.wait_ge(q["w_in"].sem, (L + 1) * (16 * (4 + 3 * NCH)))
                settle(sp, env["ready"])
            W_ALL = (L + 1) * (16 * (4 + 3 * NCH))

            @block.gpsimd
            def _(pool):
                pool.wait_ge(q["w_in"].sem, W_ALL)

                def slot(b, u, has):
                    n = base + b
                    if has(0):
                        if has(2):
                            pool.wait_ge(q["upd"].sem, q["upd"].at(n - 2))
                        ln.power(pool, n)
                        pool.tensor_tensor(XB[u][:, :, :], S[:, bass.ds(b * TB, TB), :],
                                           b2t[:, :].unsqueeze(1).to_broadcast([P, TB, D]), ALU.add)\
                            .then_inc(q["xb"].sem, 1)
                run(pool, slot)

            @block.tensor
            def _(pe):
                pe.wait_ge(q["w_in"].sem, W_ALL)

                def slot(b, u, has):
                    n = base + b
                    if has(0):
                        if has(1):
                            pe.wait_ge(q["hb"].sem, q["hb"].at(n - 1))
                        pe.matmul(SH[:, :, :], shiftm[:, 0, :], S[:, bass.ds(b * TB, TB), HALF:D],
                                  start=True, stop=False, skip_group_check=True)
                        pe.matmul(SH[:, 1:TB, :], shiftm[:, 1, :], S[:, bass.ds(b * TB, TB - 1), HALF:D],
                                  start=False, stop=True, skip_group_check=True).then_inc(q["sh"].sem, 1)
                    if has(1):
                        pe.wait_ge(q["hb"].sem, q["hb"].at(n - 1))
                        if has(2):
                            pe.wait_ge(q["ht"].sem, q["ht"].at(n - 2))
                        for t in range(TB):
                            last = pe.transpose(TP[:, t * P:(t + 1) * P], HB[:, t, :], ident[:, :])
                        last.then_inc(q["tp"].sem, 1)
                    if has(2):
                        pe.wait_ge(q["z"].sem, q["z"].at(n - 2))
                        if has(3):
                            pe.wait_ge(q["upd"].sem, q["upd"].at(n - 3))
                        for t in range(TB):
                            for c, m in enumerate(CH):
                                last = pe.matmul(OB[:, t, :], Z[u][c][0:m, t * P:(t + 1) * P], w2t[0:m, c, :],
                                                 start=(c == 0), stop=(c == NCH - 1), skip_group_check=True)
                        last.then_inc(q["w2"].sem, 1)
                    if has(1):
                        pe.wait_ge(q["ht"].sem, q["ht"].at(n - 1))
                        for c, m in enumerate(CH):
                            if c >= 2:
                                pe.wait_ge(q["z"].sem, q["z"].at(n - 1, c - 1))
                            elif has(2):
                                pe.wait_ge(q["z"].sem, q["z"].at(n - 2, 2 if c == 1 else 3))
                            pe.matmul(GP[c % 2][0:m, :], w1t[:, HID + c * P:HID + c * P + m], HF[:, :],
                                      start=True, stop=True).then_inc(q["g"].sem, 1)
                            pe.matmul(AP_[c % 2][0:m, :], w1t[:, c * P:c * P + m], HF[:, :],
                                      start=True, stop=True).then_inc(q["a"].sem, 1)
                run(pe, slot)

            @block.scalar
            def _(act):
                def slot(b, u, has):
                    n = base + b
                    if has(1):
                        act.wait_ge(q["tp"].sem, q["tp"].at(n - 1))
                        if has(2):
                            act.wait_ge(q["a"].sem, q["a"].at(n - 2))
                        act.activation(HF[:, :], TP[:, :], ACT.Identity, bias=gb[:, 1:2], scale=gb[:, 0:1])\
                            .then_inc(q["ht"].sem, 1)
                        for c, m in enumerate(CH):
                            act.wait_ge(q["g"].sem, q["g"].at(n - 1, c + 1))
                            if c >= 2:
                                act.wait_ge(q["z"].sem, q["z"].at(n - 1, c - 1))
                            elif has(2):
                                act.wait_ge(q["z"].sem, q["z"].at(n - 2, 2 if c == 1 else 3))
                            act.activation(GE[c % 2][0:m, :], GP[c % 2][0:m, :], ACT.Gelu, bias=b1t[0:m, 1, c:c + 1])\
                                .then_inc(q["ge"].sem, 1)
                act.wait_ge(q["w_in"].sem, W_ALL)
                run(act, slot)

            @block.vector
            def _(dve):
                dve.wait_ge(q["w_in"].sem, W_ALL)

                def slot(b, u, has):
                    n = base + b
                    pieces = lambda t: [S[:, b * TB + t, 0:HALF], SH[:, t, :]]
                    if has(0):
                        dve.wait_ge(q["sh"].sem, q["sh"].at(n))
                        ln.stats(dve, n, pieces)
                    if has(2):
                        dve.wait_ge(q["w2"].sem, q["w2"].at(n - 2))
                        dve.wait_ge(q["xb"].sem, q["xb"].at(n - 2))
                        dve.tensor_tensor(S[:, bass.ds((b - 2) * TB, TB), :], OB[:, :, :], XB[u][:, :, :], ALU.add)\
                            .then_inc(q["upd"].sem, 1)
                    if has(0):
                        if has(1):
                            dve.wait_ge(q["tp"].sem, q["tp"].at(n - 1))
                        ln.apply(dve, n, lambda t: [HB[:, t, 0:HALF], HB[:, t, HALF:D]], pieces)\
                          .then_inc(q["hb"].sem, 1)
                    if has(1):
                        for c, m in enumerate(CH):
                            dve.wait_ge(q["a"].sem, q["a"].at(n - 1, c + 1))
                            dve.wait_ge(q["ge"].sem, q["ge"].at(n - 1, c + 1))
                            if c == 0 and has(3):
                                dve.wait_ge(q["w2"].sem, q["w2"].at(n - 3))
                            dve.scalar_tensor_tensor(Z[1 - u][c][0:m, :], AP_[c % 2][0:m, :], b1t[0:m, 0, c:c + 1],
                                                     GE[c % 2][0:m, :], ALU.add, ALU.mult).then_inc(q["z"].sem, 1)
                run(dve, slot)


def causal_attention(nc, sb, ps, steps, Norm, env):
    NB, NT, X, S, ident, mk, split_dram, ready = (
        env[k] for k in ("NB", "NT", "X", "S", "ident", "mk", "split_dram", "ready"))
    wat, bat, H2, D2 = (env[k] for k in ("wat", "bat", "H2", "D2"))
    SCALE = float(D2) ** -0.5
    with ExitStack() as outer:
        QS = [sb(f"q_stack{u}", [P, H2, SEQ], BF16, ctx=outer) for u in range(2)]
        KS = [sb(f"k_stack{u}", [P, H2, SEQ], BF16, ctx=outer) for u in range(2)]
        GH = 8
        loaded = [[steps(f"cat_loaded{u}{g}") for g in range(2)] for u in range(2)]
        set_ok = steps("cat_stacks_set")

        def load_stacks(sp, b, u, g):
            for a in range(3):
                for c in range(3):
                    r = (3 * a + c) * D2
                    for k, dst, part in ((0, QS[u], a), (1, KS[u], c)):
                        src = split_dram[b, k, part, g * GH * D2:(g + 1) * GH * D2, :]
                        sp.dma_start(dst[r:r + D2, g * GH:(g + 1) * GH, :], src.rearrange("(h r) s -> r h s", r=D2))\
                          .then_inc(loaded[u][g].sem, 16)

        with ExitStack() as ctx:
            w = sb("w_attn", [P, 3 * D], ctx=ctx)
            bqk = sb("b_qk", [P, 2], ctx=ctx)
            bqs = sb("b_qk_scaled", [P, 2], ctx=ctx)
            bv = sb("b_v", [P, D], ctx=ctx)
            T = sb("s_normed", [P, TB, D], ctx=ctx)
            Y = sb("attn_in", [P, TB, D], ctx=ctx)
            YT = sb("attn_in_t", [P, SEQ], ctx=ctx)
            F = [sb(f"qk_full{k}", [P, SEQ], ctx=ctx) for k in range(2)]
            Rm = [sb(f"qk_rest{k}", [P, SEQ], ctx=ctx) for k in range(2)]
            PARTS = [sb(f"qk_parts{u}", [P, 2, 3, SEQ], BF16, ctx=ctx) for u in range(2)]
            TPp = ps("in_t_ps", [P, SEQ], ctx)
            QP = [ps(f"qk_p{k}", [P, SEQ], ctx) for k in range(2)]
            VPp = ps("v_p", [P, TB, D], ctx)
            ln1, ln2 = Norm("cln1", ctx), Norm("cln2", ctx)
            w_in, t_ok, x_ok, y_ok, tp, yt, qk, vps, vst = (
                steps("cin_" + n) for n in ("w_in", "t_ok", "x_ok", "y_ok", "tp", "yt", "qk", "vps", "vst"))
            bs_ok, full, rest = steps("cin_bs"), steps("cin_full", 2), steps("cin_rest", 2)
            p1, p2, p3 = steps("cin_part1", 2), steps("cin_part2", 2), steps("cin_part3", 2)
            stored = [steps(f"cin_stored{u}") for u in range(2)]
            def run(eng, slot, after=None):
                def one(g, u, n=None):
                    has = lambda k: n is None or 0 <= n - k < NB
                    slot(g * 2 + u, u, has)
                for n in range(4):
                    one(n // 2, n % 2, n)
                if after:
                    after()
                with eng.Fori(2, NB // 2) as g:
                    for u in range(2):
                        one(g, u)
                for n in range(2):
                    one(NB // 2, n, NB + n)

            with nc.Block() as block:
                @block.sync
                def _(sp):
                    sp.dma_start(w[:, :], wat).then_inc(w_in.sem, 16)
                    for k in range(2):
                        sp.dma_start(bqk[:, k:k + 1], bat[k * D:(k + 1) * D].rearrange("(n a) -> n a", a=1))\
                          .then_inc(w_in.sem, 16)
                    sp.dma_start(bv[:, :], bat[2 * D:3 * D].rearrange("(a n) -> a n", a=1).to_broadcast([P, D]))\
                      .then_inc(w_in.sem, 16)

                    def slot(b, u, has):
                        if has(2):
                            sp.wait_ge(p3.sem, p3.at(b - 2))
                            settle(sp, ready)
                            sp.dma_start(split_dram[b - 2].rearrange("k c d s -> d (k c) s"),
                                         PARTS[u][:, :, :, :].rearrange("p k c s -> p (k c) s"))\
                              .then_inc(stored[u].sem, 16)

                    def first_stacks():
                        for u in range(2):
                            sp.wait_ge(set_ok.sem, 2 * (u + 1))
                            sp.wait_ge(stored[u].sem, 16)
                            for g in range(2):
                                load_stacks(sp, u, u, g)
                    run(sp, slot, first_stacks)
                    for u in range(2):
                        sp.wait_ge(stored[u].sem, 16 * (NB // 2))

                @block.gpsimd
                def _(pool):
                    def slot(b, u, has):
                        if has(0):
                            ln1.power(pool, b)
                            ln2.power(pool, b)
                        if isinstance(b, int) and b < 2:
                            pool.wait_ge(ln2.rstd.sem, ln2.rstd.at(b))
                            pool.memset(QS[b][64:P, :, :].bitcast(F32), 0.0).then_inc(set_ok.sem, 1)
                            pool.wait_ge(set_ok.sem, 2 * b + 1)
                            pool.memset(KS[b][64:P, :, :].bitcast(F32), TWO_ONES).then_inc(set_ok.sem, 1)
                            pool.wait_ge(set_ok.sem, 2 * b + 2)
                    run(pool, slot)

                @block.tensor
                def _(pe):
                    pe.wait_ge(w_in.sem, 64)

                    def slot(b, u, has):
                        if has(1):
                            n = b - 1
                            pe.wait_ge(y_ok.sem, y_ok.at(n))
                            if has(2):
                                pe.wait_ge(yt.sem, yt.at(n - 1))
                            for t in range(TB):
                                last = pe.transpose(TPp[:, t * P:(t + 1) * P], Y[:, t, :], ident[:, :])
                            last.then_inc(tp.sem, 1)
                            pe.wait_ge(yt.sem, yt.at(n))
                            if has(2):
                                pe.wait_ge(full.sem, full.at(n - 1))
                                pe.wait_ge(p1.sem, p1.at(n - 1))
                            for k in range(2):
                                last = pe.matmul(QP[k][:, :], w[:, k * D:(k + 1) * D], YT[:, :], start=True, stop=True)
                            last.then_inc(qk.sem, 1)
                            if has(2):
                                pe.wait_ge(vst.sem, vst.at(n - 1))
                            for t in range(TB):
                                last = pe.matmul(VPp[:, t, :], YT[:, t * P:(t + 1) * P], w[:, 2 * D:3 * D],
                                                 start=True, stop=True)
                            last.then_inc(vps.sem, 1)
                    run(pe, slot)

                @block.scalar
                def _(act):
                    act.wait_ge(w_in.sem, 64)
                    act.activation(bqs[:, 0:1], bqk[:, 0:1], ACT.Copy, scale=SCALE)
                    act.activation(bqs[:, 1:2], bqk[:, 1:2], ACT.Copy).then_inc(bs_ok.sem, 1)
                    act.wait_ge(bs_ok.sem, 1)

                    def slot(b, u, has):
                        if has(1):
                            n = b - 1
                            act.wait_ge(tp.sem, tp.at(n))
                            if has(2):
                                act.wait_ge(vps.sem, vps.at(n - 1))
                            act.activation(YT[:, :], TPp[:, :], ACT.Copy).then_inc(yt.sem, 1)
                            act.wait_ge(qk.sem, qk.at(n))
                            if has(2):
                                act.wait_ge(rest.sem, rest.at(n - 1))
                            if has(3):
                                act.wait_ge(stored[1 - u].sem, (b - 3 - (1 - u)) * 8 + 16)
                            for k in range(2):
                                act.activation(F[k][:, :], QP[k][:, :], ACT.Identity, bias=bqs[:, k:k + 1],
                                               scale=SCALE if k == 0 else 1.0).then_inc(full.sem, 1)
                            for k in range(2):
                                act.activation(PARTS[1 - u][:, k, 0, :], QP[k][:, :], ACT.Identity,
                                               bias=bqs[:, k:k + 1], scale=SCALE if k == 0 else 1.0)\
                                   .then_inc(p1.sem, 1)
                            for k in range(2):
                                act.wait_ge(rest.sem, rest.at(n, k + 1))
                                act.activation(PARTS[1 - u][:, k, 1, :], Rm[k][:, :], ACT.Copy).then_inc(p2.sem, 1)
                    run(act, slot)

                @block.vector
                def _(dve):
                    dve.wait_ge(w_in.sem, 64)

                    def slot(b, u, has):
                        xt = lambda t: [X[:, b * TB + t, :]]
                        st = lambda t: [S[:, b * TB + t, :]]
                        if has(0):
                            ln1.stats(dve, b, st)
                        if has(1):
                            n = b - 1
                            for k in range(2):
                                dve.wait_ge(p1.sem, p1.at(n, k + 1))
                                if has(2):
                                    dve.wait_ge(p3.sem, p3.at(n - 1))
                                dve.tensor_tensor(Rm[k][:, :], F[k][:, :], PARTS[1 - u][:, k, 0, :], ALU.subtract)\
                                   .then_inc(rest.sem, 1)
                            dve.wait_ge(vps.sem, vps.at(n))
                            dve.tensor_tensor(S[:, bass.ds(n * TB, TB), :], VPp[:, :, :],
                                              bv[:, :].unsqueeze(1).to_broadcast([P, TB, D]), ALU.add)\
                               .then_inc(vst.sem, 1)
                            for k in range(2):
                                dve.wait_ge(p2.sem, p2.at(n, k + 1))
                                dve.tensor_tensor(PARTS[1 - u][:, k, 2, :], Rm[k][:, :], PARTS[1 - u][:, k, 1, :],
                                                  ALU.subtract).then_inc(p3.sem, 1)
                        if has(0):
                            ln1.apply(dve, b, lambda t: [T[:, t, :]], st).then_inc(t_ok.sem, 1)
                            dve.wait_ge(t_ok.sem, t_ok.at(b))
                            xb = X[:, bass.ds(b * TB, TB), :]
                            dve.tensor_tensor(xb, xb, T[:, :, :], ALU.add).then_inc(x_ok.sem, 1)
                            dve.wait_ge(x_ok.sem, x_ok.at(b))
                            ln2.stats(dve, b, xt)
                            if has(1):
                                dve.wait_ge(tp.sem, tp.at(b - 1))
                            ln2.apply(dve, b, lambda t: [Y[:, t, :]], xt).then_inc(y_ok.sem, 1)
                    run(dve, slot)

        DATA, FULL, MAXR = 9 * D2, P, 96
        QH = 4
        NQ = NB * H2 // QH
        CW = P // QH
        OFF = [0, 1 * 512, 1 * P, 2 * 512]
        OFT = [0, 512, 1024, 512 + 3 * P]
        PIECES = [[], [0], [1], [2, 3]]
        with ExitStack() as ctx:
            MX = [sb(f"maxima{g}", [P, GH, TB], ctx=ctx) for g in range(2)]
            NM = sb("neg_max", [GH * TB, P], ctx=ctx)
            MR = sb("neg_max_rest", [GH * TB, P], ctx=ctx)
            MP = [sb(f"neg_max_parts{g}", [GH * TB, 3, P], BF16, ctx=ctx) for g in range(2)]
            PT = [[sb(f"probs_t{u}_{c}", [P, 1280], ctx=ctx) for c in range(QH)] for u in range(2)]
            VS = [sb(f"values_quad{u}", [P, TB, QH, CW], ctx=ctx) for u in range(2)]
            OS = sb("o_quad", [P, SEQ], ctx=ctx)
            rec = sb("crec", [P, TB, QH], ctx=ctx)
            A = ps("scores_a", [P, 3 * 512], ctx)
            B = ps("scores_b", [P, 3 * 512], ctx)
            OP = ps("o_t_quad", [P, SEQ], ctx)
            OX = ps("o_back", [P, TB, QH, CW], ctx)
            MT = OX[0:GH * TB, 0, :, :].rearrange("p c w -> p (c w)")
            vs_zero = steps("cat_vs_zero")
            sc1, red = steps("cat_sc1", 3), steps("cat_red", 3)
            mt, nm, mp = steps("cat_mt"), steps("cat_nm", 4), steps("cat_mp", 1)
            mdma = [steps(f"cat_mdma{g}") for g in range(2)]
            sc2, ex = steps("cat_sc2", 2), steps("cat_ex", 2)
            vs, pv, os_, ox, st = (steps("cat_" + n) for n in ("vs", "pv", "os", "ox", "store"))
            rc = steps("cat_rec")

            def quad(b, hh, k=0):
                b, c = back(b, hh // QH, k, H2 // QH)
                return S[:, bass.ds(b * TB, TB), QH * D2 * c:QH * D2 * (c + 1)].rearrange("p i (h d) -> p i h d", d=D2)

            def run(eng, first, second, last=None, late=3):
                def heads(b, ub, do1, do2):
                    for hh in range(H2):
                        if do1:
                            first(b, ub, hh)
                        if do2:
                            second(b - 1, 1 - ub, hh)
                        if last and hh == late and do2:
                            last(b - 1, 1 - ub, 1)
                        if last and hh == GH + late and do1:
                            last(b, ub, 0)
                heads(0, 0, True, False)
                heads(1, 1, True, True)
                with eng.Fori(1, NB // 2) as bp:
                    for ub in range(2):
                        heads(bp * 2 + ub, ub, True, True)
                heads(NB, 0, False, True)

            def at_least(n, low):
                return not isinstance(n, int) or n >= low

            with nc.Block() as block:
                @block.sync
                def _(sp):
                    def maxima(b, ub, g):
                        sp.wait_ge(mp.sem, mp.at(b * 2 + g))
                        settle(sp, ready)
                        for c in range(3):
                            sp.dma_start(QS[ub][MAXR + c:MAXR + c + 1, g * GH:(g + 1) * GH, :]
                                         .rearrange("p h s -> p (h s)"), MP[g][:, c, :]).then_inc(mdma[g].sem, 16)

                    def load(b, ub, g):
                        sp.wait_ge(sc2.sem, sc2.at((b - 2) * H2 + (g + 1) * GH - 1))
                        settle(sp, ready)
                        load_stacks(sp, b, ub, g)
                    maxima(0, 0, 0)
                    with sp.Fori(0, NB // 2 - 1) as j:
                        for k in range(2):
                            b, ub = j * 2 + 1 + k, 1 - k
                            maxima(b - 1, 1 - ub, 1)
                            load(b + 1, 1 - ub, 0)
                            maxima(b, ub, 0)
                            load(b + 1, 1 - ub, 1)
                    maxima(NB - 2, 0, 1)
                    for g in range(2):
                        maxima(NB - 1, 1, g)

                @block.gpsimd
                def _(pool):
                    for u in range(2):
                        last = pool.memset(VS[u][:, :, :, :], 0.0)
                    last.then_inc(vs_zero.sem, 1)
                    pool.wait_ge(vs_zero.sem, 1)
                    for u in range(2):
                        last = pool.memset(VS[u][:, :, :, D2:D2 + 1], 1.0)
                    last.then_inc(vs_zero.sem, 1)
                    pool.wait_ge(vs_zero.sem, 2)

                    def second(b, ub, hh):
                        if hh % QH == 0:
                            n = b * (H2 // QH) + hh // QH
                            if at_least(n, 2):
                                pool.wait_ge(pv.sem, pv.at(n - 2))
                                settle(pool, ready)
                            pool.tensor_copy(VS[(hh // QH) % 2][:, :, :, 0:D2], quad(b, hh))\
                                .then_inc(vs.sem, 1)
                    run(pool, lambda *a: None, second)

                @block.tensor
                def _(pe):
                    def first(b, ub, hh):
                        m = b * H2 + hh
                        q, k = QS[ub], KS[ub]
                        if hh % GH == 0:
                            pe.wait_ge(loaded[ub][hh // GH].sem, ((b - ub) * 8 + 16) * 18)
                        for s, tiles in enumerate(([3], [1], [0, 2])):
                            if at_least(m, 1):
                                pe.wait_ge(red.sem, red.at(m - 1, s + 1))
                            for i in tiles:
                                o = A[:, OFF[i]:OFF[i] + (i + 1) * P]
                                pe.matmul(o, q[0:MAXR, hh, i * P:(i + 1) * P], k[0:MAXR, hh, 0:(i + 1) * P],
                                          start=True, stop=False, skip_group_check=True)
                                last = pe.matmul(o[:, i * P:], mk[:, 4, :], mk[:, 2, :], start=False, stop=True,
                                                 skip_group_check=True)
                            last.then_inc(sc1.sem, 1)

                    def values(n, u, pieces):
                        if 0 in pieces:
                            pe.wait_ge(ex.sem, ex.at(n * QH + QH - 1))
                            pe.wait_ge(vs.sem, vs.at(n))
                            if at_least(n, 1):
                                pe.wait_ge(os_.sem, os_.at(n - 1))
                        for j in pieces:
                            for c in range(QH):
                                last = pe.matmul(OP[CW * c:CW * (c + 1), j * P:], VS[u][:, j, c, :],
                                                 PT[u][c][:, OFT[j]:OFT[j] + (TB - j) * P],
                                                 start=(j == 0), stop=(j == TB - 1), skip_group_check=True)
                            if j == TB - 1:
                                last.then_inc(pv.sem, 1)

                    def turn(n):
                        pe.wait_ge(os_.sem, os_.at(n))
                        if at_least(n, 1):
                            pe.wait_ge(st.sem, st.at(n - 1))
                        for i in range(TB):
                            last = pe.transpose(OX[:, i, :, :].rearrange("p c w -> p (c w)"), OS[:, i * P:(i + 1) * P],
                                                ident[:, :])
                        last.then_inc(ox.sem, 1)

                    def second(b, ub, hh):
                        m = b * H2 + hh
                        n, c = b * (H2 // QH) + hh // QH, hh % QH
                        q, k = QS[ub], KS[ub]
                        if at_least(n, 1) and PIECES[c]:
                            values(n - 1, (hh // QH - 1) % 2, PIECES[c])
                        if c == 1 and at_least(n, 2):
                            went = (b + 1) * 2 - 2 + (hh > 3) + (hh > GH + 3 and not (isinstance(b, int) and b == NB - 1))
                            pe.wait_ge(nm.sem, nm.at(went, 1))
                            turn(n - 2)
                        if hh % GH == 0:
                            pe.wait_ge(mdma[hh // GH].sem, (b + 1) * 48)
                        for s, tiles in enumerate(([0, 1, 3], [2])):
                            if at_least(m, 1):
                                pe.wait_ge(ex.sem, ex.at(m - 1, s + 1))
                            for j in tiles:
                                o = B[:, OFT[j]:OFT[j] + (TB - j) * P]
                                pe.matmul(o, k[0:FULL, hh, j * P:(j + 1) * P], q[0:FULL, hh, j * P:],
                                          start=True, stop=False, skip_group_check=True)
                                last = pe.matmul(o[:, 0:P], mk[:, 4, :], mk[:, 3, :], start=False, stop=True,
                                                 skip_group_check=True)
                            last.then_inc(sc2.sem, 1)

                    def last(b, ub, g):
                        n = b * 2 + g
                        pe.wait_ge(red.sem, red.at(b * H2 + g * GH + GH - 1))
                        if at_least(n, 1):
                            pe.wait_ge(nm.sem, nm.at(n - 1, 1))
                        done = b * (H2 // QH) - 4 + (2 * g + 2) - 2
                        if at_least(done, 0):
                            pe.wait_ge(st.sem, st.at(done))
                        pe.transpose(MT, MX[g][:, :, :].rearrange("p h i -> p (h i)"), ident[:, :]).then_inc(mt.sem, 1)
                    run(pe, first, second, last)
                    values(NQ - 1, 1, [0, 1, 2, 3])
                    turn(NQ - 2)
                    turn(NQ - 1)

                @block.scalar
                def _(act):
                    def out(n):
                        act.wait_ge(pv.sem, pv.at(n))
                        if at_least(n, 1):
                            act.wait_ge(ox.sem, ox.at(n - 1))
                        act.activation(OS[:, :], OP[:, :], ACT.Copy).then_inc(os_.sem, 1)

                    def second(b, ub, hh):
                        m = b * H2 + hh
                        n, c = b * (H2 // QH) + hh // QH, hh % QH
                        u = (hh // QH) % 2
                        if c == 0 and at_least(n, 2):
                            out(n - 2)
                        act.wait_ge(sc2.sem, sc2.at(m, 1))
                        act.activation(PT[u][c][:, 0:1024], B[:, 0:1024], ACT.Exp).then_inc(ex.sem, 1)
                        act.wait_ge(sc2.sem, sc2.at(m, 2))
                        act.activation(PT[u][c][:, 1024:1280], B[:, 1024:1280], ACT.Exp).then_inc(ex.sem, 1)

                    def last(b, ub, g):
                        act.wait_ge(mt.sem, mt.at(b * 2 + g))
                        act.activation(NM[:, :], MT, ACT.Copy, scale=-1.0).then_inc(nm.sem, 1)
                    run(act, lambda *a: None, second, last)
                    out(NQ - 2)
                    out(NQ - 1)

                @block.vector
                def _(dve):
                    def first(b, ub, hh):
                        m, g = b * H2 + hh, hh // GH
                        if hh % GH == 0 and at_least(b, 1):
                            dve.wait_ge(mt.sem, mt.at(b * 2 + g - 2))
                        for s, tiles in enumerate(([3], [1], [0, 2])):
                            dve.wait_ge(sc1.sem, sc1.at(m, s + 1))
                            for i in tiles:
                                last = dve.tensor_reduce(MX[g][:, hh % GH, i:i + 1], A[:, OFF[i]:OFF[i] + (i + 1) * P],
                                                         AX, ALU.max)
                            last.then_inc(red.sem, 1)

                    def store(n, place):
                        dve.wait_ge(ox.sem, ox.at(n))
                        dve.reciprocal(rec[:, :, :], OX[:, :, :, D2]).then_inc(rc.sem, 1)
                        dve.wait_ge(rc.sem, rc.at(n))
                        dve.tensor_tensor(place, OX[:, :, :, 0:D2],
                                          rec[:, :, :].unsqueeze(3).to_broadcast([P, TB, QH, D2]), ALU.mult)\
                            .then_inc(st.sem, 1)

                    def second(b, ub, hh):
                        n, c = b * (H2 // QH) + hh // QH, hh % QH
                        if c == 1 and at_least(n, 2):
                            store(n - 2, quad(b, hh, 2))

                    def last(b, ub, g):
                        n = b * 2 + g
                        dve.wait_ge(nm.sem, nm.at(n, 1))
                        if at_least(b, 1):
                            dve.wait_ge(mdma[g].sem, (b - 1) * 48 + 48)
                        dve.tensor_copy(MP[g][:, 0, :], NM[:, :]).then_inc(nm.sem, 1)
                        dve.wait_ge(nm.sem, nm.at(n, 2))
                        dve.tensor_tensor(MR[:, :], NM[:, :], MP[g][:, 0, :], ALU.subtract).then_inc(nm.sem, 1)
                        dve.wait_ge(nm.sem, nm.at(n, 3))
                        dve.tensor_copy(MP[g][:, 1, :], MR[:, :]).then_inc(nm.sem, 1)
                        dve.wait_ge(nm.sem, nm.at(n, 4))
                        dve.tensor_tensor(MP[g][:, 2, :], MR[:, :], MP[g][:, 1, :], ALU.subtract).then_inc(mp.sem, 1)
                    run(dve, first, second, last, 4)
                    store(NQ - 2, quad(NB - 1, H2 - 1, 1))
                    store(NQ - 1, quad(NB - 1, H2 - 1))


def experts(nc, sb, ps, steps, Norm, env):
    NB, X, S, ident, out, NE, ready = (env[k] for k in ("NB", "X", "S", "ident", "out", "NE", "ready"))
    wpr, bpr, cenT, ebias, wrT, br, wsT, bs = (env[k] for k in ("wpr", "bpr", "cenT", "ebias", "wrT", "br", "wsT", "bs"))
    NS = wsT.shape[1]
    EB = 4
    with ExitStack() as ctx:
        wp = sb("w_proj", [P, D], ctx=ctx)
        bp_ = sb("b_proj", [P, D], ctx=ctx)
        cen = sb("centroids", [P, NE], ctx=ctx)
        eb = sb("expert_bias", [P, NE], ctx=ctx)
        wr = sb("w_routed", [P, NE, D], ctx=ctx)
        ws = sb("w_shared", [P, NS, D], ctx=ctx)
        wss = sb("w_shared_mean", [P, D], ctx=ctx)
        brs = sb("biases", [P, D], ctx=ctx)
        GT = sb("gates_t", [P, SEQ], ctx=ctx)
        iot = sb("iota", [P, NE], ctx=ctx)
        iot_i = sb("iota_i", [P, NE], mybir.dt.int32, ctx=ctx)
        AO = [sb(f"attn_out{u}", [P, TB, D], ctx=ctx) for u in range(2)]
        AT = sb("attn_out_t", [P, SEQ], ctx=ctx)
        PO = sb("proj", [P, TB, D], ctx=ctx)
        T = sb("proj_normed", [P, TB, D], ctx=ctx)
        U = [sb(f"u{u}", [P, TB, D], ctx=ctx) for u in range(2)]
        UT = [sb(f"u_t{u}", [P, SEQ], ctx=ctx) for u in range(2)]
        sc = sb("route", [P, TB, NE], ctx=ctx)
        se = sb("route_exp", [P, TB, NE], ctx=ctx)
        sp_ = sb("route_p", [P, TB, NE], ctx=ctx)
        sm = sb("route_stat", [P, 3, TB], ctx=ctx)
        top = sb("top8", [P, TB, 8], ctx=ctx)
        tix = sb("top8_index", [P, TB, 8], mybir.dt.uint32, ctx=ctx)
        tif = sb("top2_index", [P, TB, 2], ctx=ctx)
        eq = sb("chosen", [P, TB, 2, NE], ctx=ctx)
        g2 = sb("gate_parts", [P, TB, 2, NE], ctx=ctx)
        gt = [sb(f"gates{u}", [P, TB, NE], ctx=ctx) for u in range(2)]
        ACC = sb("acc", [P, TB, D], ctx=ctx)
        PR = sb("products", [P, TB, EB, D], ctx=ctx)
        H = sb("products_half", [P, TB, 2, D], ctx=ctx)
        Q = sb("products_sum", [P, TB, D], ctx=ctx)
        Z = sb("mixture", [P, TB, D], ctx=ctx)
        OUT = [sb(f"out{u}", [P, TB, D], ctx=ctx) for u in range(2)]
        TN = sb("out_normed", [P, TB, D], ctx=ctx)
        R = [ps(f"e_ring{k}", [P, SEQ], ctx) for k in range(2)]
        BP = ps("base_ps", [P, TB, D], ctx)
        E = [ps(f"experts{k}", [P, EB, D], ctx) for k in range(4)]
        EA = ps("experts_act", [P, EB, D], ctx)
        ln1, ln2, ln3 = (Norm(f"eln{k}", ctx, on_act=True) for k in (1, 2, 3))
        (w_in, init, ao, at_ps, at, po_ps, po, t_ok, x_ok, u_ok, ut_ps, ut, sc_ps, gt_ok, gtt_ps, gtt, bp_ps, fin) = (
            steps("exp_" + n) for n in ("w_in", "init", "ao", "at_ps", "at", "po_ps", "po", "t_ok", "x_ok", "u_ok",
                                        "ut_ps", "ut", "sc_ps", "gates", "gtt_ps", "gtt", "bp_ps", "fin"))
        rt, rex = steps("exp_route", 6), steps("exp_rex")
        KD = NE // EB - 1
        eps_, chain, total = steps("exp_e", 4 * KD), steps("exp_chain", 4 * KD * EB), steps("exp_total", 2)
        ea_ps, ea, pool_sum = steps("exp_ea_ps", TB), steps("exp_ea", TB), steps("exp_pool_sum", 2)
        n_ok, o_ok = steps("exp_norm"), steps("exp_out")
        shared_w = steps("exp_shared_w")
        tk = steps("exp_topk", 5)
        stored = [steps(f"exp_stored{u}") for u in range(2)]
        OV = out.rearrange("b (t p) d -> b p t d", p=P)
        PIECES = [(p, k) for p in range(2) for k in range(KD)]

        def run(eng, slot, extra=2):
            def one(g, u, n=None):
                has = lambda k: n is None or 0 <= n - k < NB
                slot(g * 2 + u, u, has)
            for n in range(4):
                one(n // 2, n % 2, n)
            with eng.Fori(2, NB // 2) as g:
                for u in range(2):
                    one(g, u)
            for n in range(extra):
                one(NB // 2, n, NB + n)

        with nc.Block() as block:
            @block.sync
            def _(sp):
                row = lambda a, n: a.rearrange("(a n) -> a n", a=1).to_broadcast([P, n])
                sp.wait_ge(init.sem, 2)
                for dst, src in ((wp[:, :], wpr), (bp_[:, :], row(bpr, D)), (cen[:, :], cenT), (eb[:, :], row(ebias, NE)),
                                 (wr[:, :, :], wrT), (ws[:, :, :], wsT), (brs[0:NE, :], br), (brs[32:32 + NS, :], bs)):
                    sp.dma_start(dst, src).then_inc(w_in.sem, 16)

                def slot(b, u, has):
                    if has(2):
                        sp.wait_ge(o_ok.sem, o_ok.at(b - 2))
                        settle(sp, ready)
                        sp.dma_start(OV[b - 2], OUT[u][:, :, :]).then_inc(stored[u].sem, 16)
                run(sp, slot)
                for u in range(2):
                    sp.wait_ge(stored[u].sem, 16 * (NB // 2))

            @block.gpsimd
            def _(pool):
                pool.memset(brs[:, :], 0.0).then_inc(init.sem, 1)
                pool.memset(GT[:, :], 0.0).then_inc(init.sem, 1)
                pool.wait_ge(init.sem, 2)
                pool.memset(GT[32:32 + NS, :], 1.0 / NS).then_inc(init.sem, 1)
                pool.wait_ge(init.sem, 3)
                pool.iota(iot_i[:, :], pattern=[[1, NE]], base=0, channel_multiplier=0).then_inc(init.sem, 1)
                pool.wait_ge(init.sem, 4)
                pool.tensor_copy(iot[:, :], iot_i[:, :]).then_inc(init.sem, 1)
                pool.wait_ge(init.sem, 5)

                def slot(b, u, has):
                    if has(0):
                        if has(2):
                            pool.wait_ge(at_ps.sem, at_ps.at(b - 2))
                        if has(2):
                            pool.wait_ge(pool_sum.sem, pool_sum.at(b - 2))
                        elif has(1):
                            pool.wait_ge(ln2.rstd.sem, ln2.rstd.at(b - 1))
                        settle(pool, ready)
                        pool.tensor_copy(AO[u][:, :, :], S[:, bass.ds(b * TB, TB), :]).then_inc(ao.sem, 1)
                        pool.wait_ge(ao.sem, ao.at(b))
                    elif has(2):
                        pool.wait_ge(pool_sum.sem, pool_sum.at(b - 2))
                    if has(2):
                        ln3.power(pool, b - 2)
                        pool.wait_ge(ln3.rstd.sem, ln3.rstd.at(b - 2))
                    if has(0):
                        ln1.power(pool, b)
                        pool.wait_ge(ln1.rstd.sem, ln1.rstd.at(b))
                    if has(0):
                        pool.wait_ge(t_ok.sem, t_ok.at(b))
                        xb = X[:, bass.ds(b * TB, TB), :]
                        pool.tensor_tensor(xb, xb, T[:, :, :], ALU.add).then_inc(x_ok.sem, 1)
                        pool.wait_ge(x_ok.sem, x_ok.at(b))
                    if has(2):
                        pool.wait_ge(n_ok.sem, n_ok.at(b - 2))
                        if has(4):
                            pool.wait_ge(stored[u].sem, (b - 4 - u) * 8 + 16)
                        pool.tensor_tensor(OUT[u][:, :, :], X[:, bass.ds((b - 2) * TB, TB), :], TN[:, :, :], ALU.add)\
                            .then_inc(o_ok.sem, 1)
                        pool.wait_ge(o_ok.sem, o_ok.at(b - 2))
                    if has(0):
                        ln2.power(pool, b)
                    if has(1):
                        if has(0):
                            pool.wait_ge(ln2.rstd.sem, ln2.rstd.at(b))
                        pool.wait_ge(ea.sem, ea.at(b - 1))
                        pool.tensor_tensor(H[:, :, :, :], PR[:, :, 0:2, :], PR[:, :, 2:4, :], ALU.add)\
                            .then_inc(pool_sum.sem, 1)
                        pool.wait_ge(pool_sum.sem, pool_sum.at(b - 1, 1))
                        if has(2):
                            pool.wait_ge(total.sem, total.at(b - 2))
                        pool.tensor_tensor(Q[:, :, :], H[:, :, 0, :], H[:, :, 1, :], ALU.add).then_inc(pool_sum.sem, 1)
                run(pool, slot)

            @block.tensor
            def _(pe):
                pe.wait_ge(w_in.sem, 16 * 8)
                pe.wait_ge(init.sem, 5)
                pe.wait_ge(shared_w.sem, 2)

                def fill(n, u, has, j):
                    if not has(1):
                        return
                    p, k = PIECES[j]
                    for tt in range(2):
                        f = 2 * j + tt
                        if f >= 4:
                            pe.wait_ge(chain.sem, chain.at(n, (f - 4) // 2 * 8 + 7 + tt))
                        elif has(2):
                            pe.wait_ge(chain.sem, chain.at(n - 1, (f + 4 * KD - 4) // 2 * 8 + 7 + tt))
                        t = 2 * p + tt
                        pe.matmul(E[f % 4][:, :, :], UT[u][:, t * P:(t + 1) * P], wr[:, EB * k:EB * (k + 1), :],
                                  start=True, stop=True).then_inc(eps_.sem, 1)

                def fill_act(n, u, has, t):
                    if not has(1):
                        return
                    if t > 0:
                        pe.wait_ge(ea.sem, ea.at(n, t))
                    elif has(2):
                        pe.wait_ge(ea.sem, ea.at(n - 1))
                    pe.matmul(EA[:, :, :], UT[u][:, t * P:(t + 1) * P], wr[:, EB * KD:, :], start=True, stop=True)\
                      .then_inc(ea_ps.sem, 1)

                def slot(b, u, has):
                    n, v = b - 1, 1 - u
                    if has(0):
                        pe.wait_ge(ao.sem, ao.at(b))
                        if has(1):
                            pe.wait_ge(ut.sem, ut.at(b - 1))
                        for t in range(TB):
                            last = pe.transpose(R[0][:, t * P:(t + 1) * P], AO[u][:, t, :], ident[:, :])
                        last.then_inc(at_ps.sem, 1)
                    fill(n, v, has, 0)
                    if has(0):
                        pe.wait_ge(at.sem, at.at(b))
                        if has(1):
                            pe.wait_ge(rt.sem, rt.at(b - 1, 1))
                        for t in range(TB):
                            last = pe.matmul(R[1][:, t * P:(t + 1) * P], AT[:, t * P:(t + 1) * P], wp[:, :],
                                             start=True, stop=True)
                        last.then_inc(po_ps.sem, 1)
                    fill(n, v, has, 1)
                    fill_act(n, v, has, 0)
                    if has(1):
                        pe.wait_ge(gt_ok.sem, gt_ok.at(n))
                        if not has(0):
                            pe.wait_ge(ut.sem, ut.at(n))
                        for t in range(TB):
                            last = pe.transpose(R[0][0:NE, t * P:(t + 1) * P], gt[v][:, t, :], ident[:, :])
                        last.then_inc(gtt_ps.sem, 1)
                    fill(n, v, has, 2)
                    if has(1):
                        pe.wait_ge(gtt.sem, gtt.at(n))
                        if has(2):
                            pe.wait_ge(total.sem, total.at(n - 1))
                        for t in range(TB):
                            pe.matmul(BP[:, t, :], GT[:, t * P:(t + 1) * P], brs[:, :], start=True, stop=False,
                                      skip_group_check=True)
                            last = pe.matmul(BP[:, t, :], UT[v][:, t * P:(t + 1) * P], wss[:, :], start=False, stop=True,
                                             skip_group_check=True)
                        last.then_inc(bp_ps.sem, 1)
                    fill_act(n, v, has, 1)
                    fill(n, v, has, 3)
                    fill_act(n, v, has, 2)
                    fill(n, v, has, 4)
                    fill_act(n, v, has, 3)
                    fill(n, v, has, 5)
                    if has(0):
                        pe.wait_ge(u_ok.sem, u_ok.at(b))
                        if has(1):
                            pe.wait_ge(gtt.sem, gtt.at(n))
                        for t in range(TB):
                            last = pe.transpose(R[0][:, t * P:(t + 1) * P], U[u][:, t, :], ident[:, :])
                        last.then_inc(ut_ps.sem, 1)
                    if has(0):
                        pe.wait_ge(ut.sem, ut.at(b))
                        pe.wait_ge(po.sem, po.at(b))
                        for t in range(TB):
                            last = pe.matmul(R[1][:, t * NE:(t + 1) * NE], UT[u][:, t * P:(t + 1) * P], cen[:, :],
                                             start=True, stop=True)
                        last.then_inc(sc_ps.sem, 1)
                run(pe, slot, 1)

            @block.scalar
            def _(act):
                act.wait_ge(w_in.sem, 16 * 8)

                def products(n, u, has, t):
                    if not has(1):
                        return
                    act.wait_ge(ea_ps.sem, ea_ps.at(n, t + 1))
                    if has(2) and t == 0:
                        act.wait_ge(pool_sum.sem, pool_sum.at(n - 1, 1))
                    if t == 0:
                        act.wait_ge(gt_ok.sem, gt_ok.at(n))
                    for e in range(EB):
                        i = EB * KD + e
                        last = act.activation(PR[:, t, e, :], EA[:, e, :], ACT.Copy, scale=gt[u][:, t, i:i + 1])
                    last.then_inc(ea.sem, 1)

                def slot(b, u, has):
                    n, v = b - 1, 1 - u
                    if has(0):
                        act.wait_ge(at_ps.sem, at_ps.at(b))
                        if has(1):
                            act.wait_ge(po_ps.sem, po_ps.at(b - 1))
                        act.activation(AT[:, :], R[0][:, :], ACT.Copy).then_inc(at.sem, 1)
                    products(n, v, has, 0)
                    if has(1):
                        act.wait_ge(gtt_ps.sem, gtt_ps.at(n))
                        if has(2):
                            act.wait_ge(bp_ps.sem, bp_ps.at(n - 1))
                        act.activation(GT[0:NE, :], R[0][0:NE, :], ACT.Copy).then_inc(gtt.sem, 1)
                    if has(0):
                        if has(1):
                            act.wait_ge(x_ok.sem, x_ok.at(n))
                        ln1.apply_act(act, b, lambda t: [T[:, t, :]], lambda t: [PO[:, t, :]]).then_inc(t_ok.sem, 1)
                    if has(2):
                        if has(3):
                            act.wait_ge(o_ok.sem, o_ok.at(b - 3))
                        ln3.apply_act(act, b - 2, lambda t: [TN[:, t, :]], lambda t: [Z[:, t, :]]).then_inc(n_ok.sem, 1)
                    products(n, v, has, 1)
                    products(n, v, has, 2)
                    products(n, v, has, 3)
                    if has(0):
                        ln2.apply_act(act, b, lambda t: [U[u][:, t, :]], lambda t: [X[:, b * TB + t, :]])\
                           .then_inc(u_ok.sem, 1)
                        act.wait_ge(ut_ps.sem, ut_ps.at(b))
                        act.activation(UT[u][:, :], R[0][:, :], ACT.Copy).then_inc(ut.sem, 1)
                        act.wait_ge(rt.sem, rt.at(b, 3))
                        act.activation(se[:, :, :], sc[:, :, :], ACT.Exp).then_inc(rex.sem, 1)
                run(act, slot)

            @block.vector
            def _(dve):
                dve.wait_ge(w_in.sem, 16 * 8)
                assert NS == 2
                dve.tensor_tensor(wss[:, :], ws[:, 0, :], ws[:, 1, :], ALU.add).then_inc(shared_w.sem, 1)
                dve.wait_ge(shared_w.sem, 1)
                dve.tensor_scalar(wss[:, :], wss[:, :], 1.0 / NS, None, ALU.mult).then_inc(shared_w.sem, 1)
                dve.wait_ge(init.sem, 5)

                def piece(n, u, has, j):
                    if not has(1):
                        return
                    p, k = PIECES[j]
                    for e in range(EB):
                        for tt in range(2):
                            i, t, f = EB * k + e, 2 * p + tt, 2 * j + tt
                            step = j * 8 + e * 2 + tt
                            if e == 0:
                                dve.wait_ge(eps_.sem, eps_.at(n, f + 1))
                            if i > 0:
                                dve.wait_ge(chain.sem, chain.at(n, step - 1))
                            base = U[u][:, t, :] if i == 0 else ACC[:, t, :]
                            dve.scalar_tensor_tensor(ACC[:, t, :], E[f % 4][:, e, :], gt[u][:, t, i:i + 1], base,
                                                     ALU.mult, ALU.add).then_inc(chain.sem, 1)

                def slot(b, u, has):
                    n, v = b - 1, 1 - u
                    xt = lambda t: [X[:, b * TB + t, :]]
                    if has(0):
                        dve.wait_ge(po_ps.sem, po_ps.at(b))
                        dve.tensor_tensor(PO[:, :, :], R[1][:, :].rearrange("p (t d) -> p t d", d=D),
                                          bp_[:, :].unsqueeze(1).to_broadcast([P, TB, D]), ALU.add).then_inc(po.sem, 1)
                    if has(1):
                        dve.wait_ge(gt_ok.sem, gt_ok.at(n))
                    piece(n, v, has, 0)
                    if has(0):
                        dve.wait_ge(po.sem, po.at(b))
                        ln1.stats(dve, b, lambda t: [PO[:, t, :]])
                    if has(2):
                        ln3.shift(dve, b - 2)
                    piece(n, v, has, 1)
                    if has(0):
                        ln1.shift(dve, b)
                    piece(n, v, has, 2)
                    piece(n, v, has, 3)
                    if has(0):
                        dve.wait_ge(x_ok.sem, x_ok.at(b))
                        ln2.stats(dve, b, xt)
                    piece(n, v, has, 4)
                    if has(0):
                        ln2.shift(dve, b)
                    piece(n, v, has, 5)
                    if has(1):
                        dve.wait_ge(bp_ps.sem, bp_ps.at(n))
                        dve.wait_ge(chain.sem, chain.at(n))
                        if has(2):
                            dve.wait_ge(n_ok.sem, n_ok.at(n - 1))
                        dve.tensor_tensor(Z[:, :, :], ACC[:, :, :], BP[:, :, :], ALU.add).then_inc(total.sem, 1)
                        dve.wait_ge(pool_sum.sem, pool_sum.at(n))
                        dve.wait_ge(total.sem, total.at(n, 1))
                        dve.tensor_tensor(Z[:, :, :], Z[:, :, :], Q[:, :, :], ALU.add).then_inc(total.sem, 1)
                    if has(0):
                        dve.wait_ge(sc_ps.sem, sc_ps.at(b))
                        ebb = eb[:, :].unsqueeze(1).to_broadcast([P, TB, NE])
                        dve.tensor_tensor(sc[:, :, :], R[1][:, 0:TB * NE].rearrange("p (t e) -> p t e", e=NE), ebb, ALU.add)\
                            .then_inc(rt.sem, 1)
                    if has(1):
                        dve.wait_ge(total.sem, total.at(n))
                        ln3.pieces_stats(dve, lambda t: [Z[:, t, :]])
                    if has(0):
                        dve.wait_ge(rt.sem, rt.at(b, 1))
                        dve.tensor_reduce(sm[:, 0, :], sc[:, :, :], AX, ALU.max).then_inc(rt.sem, 1)
                        dve.wait_ge(rt.sem, rt.at(b, 2))
                        bc = lambda k: sm[:, k, :].unsqueeze(2).to_broadcast([P, TB, NE])
                        dve.tensor_tensor(sc[:, :, :], sc[:, :, :], bc(0), ALU.subtract).then_inc(rt.sem, 1)
                    if has(1):
                        ln3.aggregate(dve, n)
                        ln3.variance(dve, n)
                    if has(0):
                        dve.wait_ge(rex.sem, rex.at(b))
                        dve.tensor_reduce(sm[:, 1, :], se[:, :, :], AX, ALU.add).then_inc(rt.sem, 1)
                        dve.wait_ge(rt.sem, rt.at(b, 4))
                        dve.reciprocal(sm[:, 2, :], sm[:, 1, :]).then_inc(rt.sem, 1)
                        dve.wait_ge(rt.sem, rt.at(b, 5))
                        dve.tensor_tensor(sp_[:, :, :], se[:, :, :], bc(2), ALU.mult).then_inc(rt.sem, 1)
                        dve.wait_ge(rt.sem, rt.at(b, 6))
                        settle(dve, ready)
                        for t in range(TB):
                            last = dve.max(top[:, t, :], sp_[:, t, :])
                        last.then_inc(tk.sem, 1)
                        dve.wait_ge(tk.sem, tk.at(b, 1))
                        settle(dve, ready)
                        for t in range(TB):
                            last = dve.max_index(tix[:, t, :], top[:, t, :], sp_[:, t, :])
                        last.then_inc(tk.sem, 1)
                        dve.wait_ge(tk.sem, tk.at(b, 2))
                        dve.tensor_copy(tif[:, :, :], tix[:, :, 0:2]).then_inc(tk.sem, 1)
                        dve.wait_ge(tk.sem, tk.at(b, 3))
                        pairs = [P, TB, 2, NE]
                        dve.tensor_tensor(eq[:, :, :, :], iot[:, :].unsqueeze(1).unsqueeze(1).to_broadcast(pairs),
                                          tif[:, :, :].unsqueeze(3).to_broadcast(pairs), ALU.is_equal).then_inc(tk.sem, 1)
                        dve.wait_ge(tk.sem, tk.at(b, 4))
                        dve.tensor_tensor(g2[:, :, :, :], eq[:, :, :, :],
                                          sp_[:, :, :].unsqueeze(2).to_broadcast(pairs), ALU.mult).then_inc(tk.sem, 1)
                        dve.wait_ge(tk.sem, tk.at(b, 5))
                        dve.tensor_tensor(gt[u][:, :, :], g2[:, :, 0, :], g2[:, :, 1, :], ALU.add).then_inc(gt_ok.sem, 1)
                run(dve, slot)


def constants():
    half = np.arange(0, 64, 2, dtype=np.float32)
    inv = (np.float32(1.0) / np.float32(10000.0) ** (half / np.float32(64))).astype(np.float32)
    t = np.arange(SEQ, dtype=np.float32)
    fr = (t[:, None] * inv[None, :]).astype(np.float32)
    fr = np.concatenate([fr, fr], -1)
    base = ((half + np.float32(0.4 * 64)) / np.float32(1.4 * 64)).astype(np.float32)
    power = ((t - SEQ // 2) / np.float32(32.0)).astype(np.float32)
    sc = (base[None, :] ** power[:, None]).astype(np.float32)
    sc = np.concatenate([sc, sc], -1)
    cos, sin = np.cos(fr), np.sin(fr)
    sgn = np.concatenate([-np.ones(32, np.float32), np.ones(32, np.float32)])
    tabs = np.stack([cos * sc * 8, cos / sc, sgn * sin * sc * 8, sgn * sin / sc], 1).astype(np.float32)
    rot = np.ascontiguousarray(tabs.reshape(TB, P, 4, 64).transpose(1, 0, 2, 3))
    r, c = np.arange(P)[:, None], np.arange(P)[None, :]
    rr, cc = r % 64, c % 64
    cur, prev = cc <= rr, cc >= rr
    loc = np.where(r < 64, np.where(c < 64, cur, prev), np.where(c < 64, prev, cur))
    loc0 = loc & ~((r < 64) & (c >= 64))
    neg = lambda ok: np.where(ok, 0.0, MASKED)
    eye = np.eye(P)
    mk = np.stack([neg(loc), neg(loc0), neg(c <= r), neg(r <= c), eye], 1).astype(np.float32)
    shift = (c == r + 1).astype(np.float32)
    carry = ((r == P - 1) & (c == 0)).astype(np.float32)
    return {"rot": rot, "mk": mk, "ident": eye.astype(np.float32), "shift": shift, "carry": carry}


ORDER = ["L0_attn_x", "L0_attn_filt", "L0_ffn_wqkv", "L0_ffn_q_scale", "L0_ffn_k_scale", "L0_ffn_wo", "L0_ffn_ln_g",
         "L0_ffn_ln_b", "L0_ffn_w1", "L0_ffn_b1", "L0_ffn_w2", "L0_ffn_b2", "L1_attn_w_attn", "L1_attn_b_attn",
         "L1_attn_w_proj", "L1_attn_b_proj", "L1_ffn_centroids", "L1_ffn_expert_biases", "L1_ffn_Wr", "L1_ffn_br",
         "L1_ffn_Ws", "L1_ffn_bs"]


def build(nc, inputs, stop=99):
    arrays = {}

    def give(name, a):
        arrays[name] = np.ascontiguousarray(a)
        return nc.dram_tensor(name, a.shape, mybir.dt.from_np(arrays[name].dtype), kind="ExternalInput").ap()

    args = []
    for name in ORDER:
        a = np.asarray(inputs[name])
        if name == "L1_ffn_centroids":
            a = a.T
        if name in ("L1_ffn_Wr", "L1_ffn_Ws"):
            a = a.transpose(2, 0, 1)
        args.append(give("in_" + name, a))
    k = constants()
    rot = give("c_rot", k["rot"])
    masks = [give("c_" + n, k[n]) for n in ("mk", "ident", "shift", "carry")]
    shape = np.asarray(inputs["L0_attn_x"]).shape
    out = nc.dram_tensor("out_dram", shape, F32, kind="ExternalOutput").ap()
    program(nc, *args, rot, masks, out, stop=stop)
    return arrays


def kernel(**inputs):
    import concourse.bacc as bacc
    from concourse.bass_utils import run_bass_kernel_spmd

    nc = bacc.Bacc("TRN2", target_bir_lowering=False, num_devices=1)
    arrays = build(nc, inputs)
    r = run_bass_kernel_spmd(nc, [arrays], core_ids=[0])
    return r.results[0]["out_dram"]
```

```python
from contextlib import ExitStack

import numpy as np

import concourse.bass as bass
from concourse import mybir

F32 = mybir.dt.float32
BF16 = mybir.dt.bfloat16
ALU = mybir.AluOpType
ACT = mybir.ActivationFunctionType
AX = mybir.AxisListType.X

P = 128
D = 128
TB = 4
SEQ = TB * P
EPS = 1e-5
MASKED = -1e30


TWO_ONES = float(np.array([0x3F803F80], np.uint32).view(np.float32)[0])


class Steps:

    def __init__(self, sem, per=1, base=0):
        self.sem, self.per, self.base = sem, per, base

    def again(self, items):
        return Steps(self.sem, self.per, self.base + items * self.per)

    def at(self, n, k=None):
        return self.base + n * self.per + (self.per if k is None else k)


def settle(eng, ready):
    eng.sem_inc(ready.sem, 1)


def back(b, t, k, unroll):
    return (b, t - k) if t >= k else (b - 1, t - k + unroll)


def program(nc, x, filt, wqkv, qsc, ksc, wo, lng, lnb, w1, b1, w2, b2, wat, bat, wpr, bpr, cenT, ebias,
            wrT, br, wsT, bs, rot, masks, out):
    NB = x.shape[0]
    DEPTH = wqkv.shape[0]
    NT = NB * TB
    HEADS, DH = 8, 64
    WIN = 64
    HID = w2.shape[1]
    CH = [min(P, HID - P * c) for c in range(-(-HID // P))]
    NC_ = len(CH)
    TAPS = filt.shape[0]
    H2, D2 = 16, 8
    NE = wrT.shape[1]
    assert x.shape[1:] == (SEQ, D) and TAPS == 2 * P and NB % 4 == 0 and NC_ == 3

    pad = nc.dram_tensor("filter_padded", [4 * P], F32, kind="Internal").ap()
    split_dram = nc.dram_tensor("qk_split", [NB, 2, 3, D, SEQ], BF16, kind="Internal").ap()

    with ExitStack() as whole:
        def sb(name, shape, dt=F32, ctx=whole):
            return ctx.enter_context(nc.sbuf_tensor(name, shape, dt))

        def ps(name, shape, ctx, dt=F32):
            return ctx.enter_context(nc.psum_tensor(name, shape, dt))

        def steps(name, per=1):
            return Steps(whole.enter_context(nc.semaphore(name)), per)

        X = sb("X", [P, NT, D])
        S = sb("S", [P, NT, D])
        ident = sb("ident", [P, P])
        mk = sb("mk", [P, 5, P], BF16)
        mhalf = sb("mhalf", [P, 16])
        ready = steps("marks")

        class Norm:

            def __init__(self, name, ctx, pieces=1, on_act=False, after=None):
                self.pieces = pieces
                self.st = sb(name + "_st", [P, TB, pieces, 6], ctx=ctx)
                self.mv = sb(name + "_mv", [P, TB, 2], ctx=ctx)
                self.ve = sb(name + "_ve", [P, TB], ctx=ctx)
                self.rs = sb(name + "_rs", [P, TB], ctx=ctx)
                if on_act:
                    self.sh = sb(name + "_sh", [P, TB], ctx=ctx)
                if after:
                    self.done, self.rstd, self.shifted = (q.again(NB) for q in (after.done, after.rstd, after.shifted))
                    return
                self.done = steps(name + "_var", 3)
                self.rstd = steps(name + "_rstd")
                if on_act:
                    self.shifted = steps(name + "_shifted")

            def stats(self, dve, n, pieces):
                self.pieces_stats(dve, pieces)
                self.aggregate(dve, n)
                self.variance(dve, n)

            def pieces_stats(self, dve, pieces):
                settle(dve, ready)
                for t in range(TB):
                    for k, piece in enumerate(pieces(t)):
                        last = dve.bn_stats(self.st[:, t, k, :], piece)
                last.then_inc(self.done.sem, 1)

            def aggregate(self, dve, n):
                dve.wait_ge(self.done.sem, self.done.at(n, 1))
                settle(dve, ready)
                for t in range(TB):
                    last = dve.bn_aggr(self.mv[:, t, :], self.st[:, t, :, :].rearrange("p k s -> p (k s)"))
                last.then_inc(self.done.sem, 1)

            def variance(self, dve, n):
                dve.wait_ge(self.done.sem, self.done.at(n, 2))
                dve.tensor_scalar(self.ve[:, :], self.mv[:, :, 1], EPS, None, ALU.add).then_inc(self.done.sem, 1)

            def power(self, pool, n):
                pool.wait_ge(self.done.sem, self.done.at(n))
                pool.tensor_tensor(self.rs[:, :], self.ve[:, :], mhalf[:, 0:TB], ALU.pow).then_inc(self.rstd.sem, 1)

            def apply(self, dve, n, outs, pieces):
                dve.wait_ge(self.rstd.sem, self.rstd.at(n))
                for t in range(TB):
                    for o, i in zip(outs(t), pieces(t)):
                        last = dve.tensor_scalar(o, i, self.mv[:, t, 0:1], self.rs[:, t:t + 1],
                                                 ALU.subtract, ALU.mult)
                return last

            def shift(self, dve, n):
                dve.wait_ge(self.rstd.sem, self.rstd.at(n))
                dve.scalar_tensor_tensor(self.sh[:, :], self.mv[:, :, 0], -1.0, self.rs[:, :], ALU.mult, ALU.mult)\
                   .then_inc(self.shifted.sem, 1)

            def apply_act(self, act, n, outs, pieces):
                act.wait_ge(self.shifted.sem, self.shifted.at(n))
                for t in range(TB):
                    for o, i in zip(outs(t), pieces(t)):
                        last = act.activation(o, i, ACT.Identity, bias=self.sh[:, t:t + 1], scale=self.rs[:, t:t + 1])
                return last

        with ExitStack() as ctx:
            hank = sb("hankel", [P, 3 * P], ctx=ctx)
            toep = sb("toeplitz", [P, 3, P], ctx=ctx)
            zero = sb("zero_row", [1, P], ctx=ctx)
            mkf = sb("masks_f32", [P, 5, P], ctx=ctx)
            Y = sb("conv_in", [P, SEQ], ctx=ctx)
            T = sb("conv_normed", [P, TB, D], ctx=ctx)
            C = [ps(f"conv_out{u}", [P, SEQ], ctx) for u in range(2)]
            lnA, lnB, lnC = (Norm(f"ln{c}", ctx, on_act=True) for c in "abc")
            consts = steps("constants")
            x_in = [steps(f"x_in{j}") for j in range(4)]
            zeroed = steps("zeroed")
            padded = steps("padded")
            hank_in = steps("hankel_in")
            toep_ok = steps("toeplitz_built")
            half_ok = steps("half_set")
            y_ok = steps("conv_in_ready")
            conv = steps("conv_done")
            t_ok = steps("conv_normed_ready")
            x_ok = steps("x_updated")
            s_ok = steps("stream_ready")
            LOADS = [(0, 2), (2, 4), (4, NB // 2 + 2), (NB // 2 + 2, NB)]

            def run(eng, slot, before_loop=None):
                def one(g, u, n=None):
                    has = lambda k: n is None or 0 <= n - k < NB
                    slot(g * 2 + u, u, has)
                for n in range(4):
                    one(n // 2, n % 2, n)
                if before_loop:
                    before_loop()
                with eng.Fori(2, NB // 2) as g:
                    for u in range(2):
                        one(g, u)
                for n in range(NB, NB + 5):
                    one(n // 2, n % 2, n)

            with nc.Block() as block:
                @block.sync
                def _(sp):
                    sp.wait_ge(zeroed.sem, 1)
                    for o in (0, 3 * P):
                        sp.dma_start(pad[o:o + P].rearrange("(a n) -> a n", a=1), zero[:, :]).then_inc(padded.sem, 16)
                    sp.dma_start(pad[P:3 * P].rearrange("(a n) -> a n", a=1),
                                 filt.rearrange("(a n) -> a n", a=1)).then_inc(padded.sem, 16)
                    sp.wait_ge(padded.sem, 48)
                    rows = bass.AP(pad.tensor, 1, [[1, P], [1, 3 * P]])
                    sp.dma_start(hank[:, :], rows).then_inc(hank_in.sem, 16)

                @block.scalar
                def _(act):
                    for (lo, hi), arrived in zip(LOADS, x_in):
                        act.dma_start(X[:, lo * TB:hi * TB, :], x[lo:hi].rearrange("b (t p) d -> p (b t) d", p=P))\
                           .then_inc(arrived.sem, 16)
                    act.dma_start(ident[:, :], masks[1]).then_inc(consts.sem, 16)
                    act.dma_start(mkf[:, :, :], masks[0]).then_inc(consts.sem, 16)

                    def slot(b, u, has):
                        if has(3):
                            n = b - 3
                            if has(4):
                                act.wait_ge(x_ok.sem, x_ok.at(n - 1))
                            lnB.apply_act(act, n, lambda t: [T[:, t, :]], lambda t: [C[1 - u][:, t * P:(t + 1) * P]])\
                               .then_inc(t_ok.sem, 1)
                        if has(1):
                            n = b - 1
                            if has(2):
                                act.wait_ge(conv.sem, conv.at(n - 1))
                            lnA.apply_act(act, n, lambda t: [Y[:, t * P:(t + 1) * P]], lambda t: [X[:, n * TB + t, :]])\
                               .then_inc(y_ok.sem, 1)
                        if has(4):
                            n = b - 4
                            lnC.apply_act(act, n, lambda t: [S[:, n * TB + t, :]], lambda t: [X[:, n * TB + t, :]])\
                               .then_inc(s_ok.sem, 1)
                    run(act, slot)
                    act.wait_ge(consts.sem, 32)
                    act.activation(mk[:, :, :], mkf[:, :, :], ACT.Copy)

                @block.gpsimd
                def _(pool):
                    pool.memset(mhalf[:, :], -0.5).then_inc(half_ok.sem, 1)
                    pool.wait_ge(half_ok.sem, 1)

                    def slot(b, u, has):
                        if has(3):
                            n = b - 3
                            pool.wait_ge(t_ok.sem, t_ok.at(n))
                            xb = X[:, bass.ds(n * TB, TB), :]
                            pool.tensor_tensor(xb, xb, T[:, :, :], ALU.add).then_inc(x_ok.sem, 1)
                            pool.wait_ge(x_ok.sem, x_ok.at(n))
                        if has(2):
                            lnB.power(pool, b - 2)
                            pool.wait_ge(lnB.rstd.sem, lnB.rstd.at(b - 2))
                        if has(0):
                            if has(1):
                                pool.wait_ge(y_ok.sem, y_ok.at(b - 1))
                            lnA.power(pool, b)
                            pool.wait_ge(lnA.rstd.sem, lnA.rstd.at(b))
                        if has(3):
                            if has(4):
                                pool.wait_ge(s_ok.sem, s_ok.at(b - 4))
                            lnC.power(pool, b - 3)
                            pool.wait_ge(lnC.rstd.sem, lnC.rstd.at(b - 3))
                    run(pool, slot)

                @block.vector
                def _(dve):
                    dve.memset(zero[:, :], 0.0).then_inc(zeroed.sem, 1)

                    def slot(b, u, has):
                        if has(3):
                            lnB.shift(dve, b - 3)
                        if has(1):
                            lnA.shift(dve, b - 1)
                        if has(4):
                            lnC.shift(dve, b - 4)
                        if has(0):
                            for (lo, _), arrived in zip(LOADS, x_in):
                                if isinstance(b, int) and b == lo:
                                    dve.wait_ge(arrived.sem, 16)
                            lnA.stats(dve, b, lambda t: [X[:, b * TB + t, :]])
                        if isinstance(b, int) and b == 0:
                            dve.wait_ge(hank_in.sem, 16)
                            for j in range(3):
                                last = dve.tensor_copy(toep[:, j, :], hank[:, j * P:(j + 1) * P][:, ::-1])
                            last.then_inc(toep_ok.sem, 1)
                        if has(2):
                            dve.wait_ge(conv.sem, conv.at(b - 2))
                            lnB.stats(dve, b - 2, lambda t: [C[u][:, t * P:(t + 1) * P]])
                        if has(3):
                            dve.wait_ge(x_ok.sem, x_ok.at(b - 3))
                            lnC.stats(dve, b - 3, lambda t: [X[:, (b - 3) * TB + t, :]])

                    def rest_of_x():
                        for arrived in x_in[2:]:
                            dve.wait_ge(arrived.sem, 16)
                    run(dve, slot, rest_of_x)

                @block.tensor
                def _(pe):
                    pe.wait_ge(toep_ok.sem, 1)

                    def slot(b, u, has):
                        if has(1):
                            n = b - 1
                            pe.wait_ge(y_ok.sem, y_ok.at(n))
                            if has(3):
                                pe.wait_ge(t_ok.sem, t_ok.at(n - 2))
                            for j in range(3):
                                last = pe.matmul(C[1 - u][:, 0:(TB - j) * P], toep[:, j, :], Y[:, j * P:SEQ],
                                                 start=(j == 0), stop=(j == 2), skip_group_check=True)
                            last.then_inc(conv.sem, 1)
                    run(pe, slot)

        with ExitStack() as layers:
            rotc = sb("rot_const", [P, TB, 4, DH], ctx=layers)
            rot_in = steps("rot_in")
            shiftm = sb("shift", [P, 2, P], ctx=layers)
            shift_in = steps("shift_in")
            VN = [sb(f"v{t}", [P, HEADS, DH + 1], ctx=layers) for t in range(TB)]
            KZ = sb("kz", [P, 2, HEADS, P], ctx=layers)
            HT = [sb(f"ht{t}", [P, P], ctx=layers) for t in range(TB)]
            zcol = sb("zero_col", [P, 1], ctx=layers)
            init = steps("layers_init")
            sems_a, sems_f = attention_sems(steps), ffn_sems(steps, Norm, layers)
            inner = HEADS * DH
            wq = sb("wq", [P, 3 * inner], ctx=layers)
            wot = sb("wo", [P, inner // P, D], ctx=layers)
            scb = sb("qk_scales", [P, 4, DH], ctx=layers)
            w1t = sb("w1", [P, 2 * HID], ctx=layers)
            w2t = sb("w2", [P, NC_, D], ctx=layers)
            gb = sb("ln_gb", [P, 2], ctx=layers)
            b1t = sb("b1", [P, 2, NC_], ctx=layers)
            b2t = sb("b2", [P, D], ctx=layers)
            sems_a["weights"], sems_f["weights"] = (wq, wot, scb), (w1t, w2t, gb, b1t, b2t)
            assert DEPTH == 2

            def load_attention(sp, L):
                sp.dma_start(wq[:, :], wqkv[L]).then_inc(sems_a["w_in"].sem, 16)
                sp.dma_start(wot[:, :, :], wo[L].rearrange("(c p) d -> p c d", p=P)).then_inc(sems_a["w_in"].sem, 16)
                for k, src in enumerate((qsc, ksc)):
                    row = src[L].rearrange("(a n) -> a n", a=1)
                    half = DH // 2
                    sp.dma_start(scb[:, k, :], row.to_broadcast([P, DH]))\
                      .then_inc(sems_a["w_in"].sem, 16)
                    for h in range(2):
                        sp.dma_start(scb[:, 2 + k, h * half:(h + 1) * half],
                                     row[:, (1 - h) * half:(2 - h) * half].to_broadcast([P, half]))\
                          .then_inc(sems_a["w_in"].sem, 16)

            def load_ffn(sp, L):
                def load(dst, src):
                    sp.dma_start(dst, src).then_inc(sems_f["w_in"].sem, 16)
                load(w1t[:, :], w1[L])
                for c, n in enumerate(CH):
                    load(w2t[0:n, c, :], w2[L, c * P:c * P + n, :])
                    for k in range(2):
                        load(b1t[0:n, k, c:c + 1], b1[L, k * HID + c * P:k * HID + c * P + n].rearrange("(n a) -> n a", a=1))
                load(gb[:, 0:1], lng[L].rearrange("(n a) -> n a", a=1))
                load(gb[:, 1:2], lnb[L].rearrange("(n a) -> n a", a=1))
                load(b2t[:, :], b2[L].rearrange("(a n) -> a n", a=1).to_broadcast([P, D]))

            with nc.Block() as block:
                @block.tensor
                def _(pe):
                    for made, names in ((sems_a, ("pv", "wo", "eot", "xadd")), (sems_f, ("w2", "upd"))):
                        for name in names:
                            pe.sem_inc(made[name].sem, 1)
                            made[name].base = 1

                @block.sync
                def _(sp):
                    sp.dma_start(rotc[:, :, :, :], rot).then_inc(rot_in.sem, 16)
                    for k in range(2):
                        sp.dma_start(shiftm[:, k, :], masks[2 + k]).then_inc(shift_in.sem, 16)
                    load_attention(sp, 0)
                    sp.wait_ge(rot_in.sem, 16)
                    sp.wait_ge(shift_in.sem, 32)

                @block.vector
                def _(dve):
                    for v in VN:
                        dve.memset(v[:, :, :], 1.0)
                    dve.memset(KZ[:, :, :, :], 0.0)
                    dve.memset(zcol[:, :], 0.0)
                    dve.memset(HT[0][:, 0:1], 0.0).then_inc(init.sem, 1)
                    dve.wait_ge(init.sem, 1)
            env = dict(locals())
            with nc.Fori(0, DEPTH) as L:
                local_attention(nc, L, sb, ps, steps, sems_a, env)
                feed_forward(nc, L, sb, ps, steps, sems_f, env)
        NS = wsT.shape[1]
        moe = dict(wp=sb("w_proj", [P, D]), bp_=sb("b_proj", [P, D]), cen=sb("centroids", [P, NE]),
                   eb=sb("expert_bias", [P, NE]), wr=sb("w_routed", [P, NE, D]), ws=sb("w_shared", [P, NS, D]))
        moe_in = steps("moe_weights_in")

        def load_moe(sp):
            row = lambda a, n: a.rearrange("(a n) -> a n", a=1).to_broadcast([P, n])
            for name, src in (("wp", wpr), ("bp_", row(bpr, D)), ("cen", cenT), ("eb", row(ebias, NE)), ("wr", wrT),
                              ("ws", wsT)):
                whole_tile = moe[name][tuple(slice(None) for _ in src.shape)]
                sp.dma_start(whole_tile, src).then_inc(moe_in.sem, 16)
        env = dict(locals())
        norms = causal_attention(nc, sb, ps, steps, Norm, (lnA, lnB), env)
        experts(nc, sb, ps, steps, Norm, (*norms, lnC), env)


def attention_sems(steps):
    per = dict(w_in=1, tab=2, xst=1, hps=1, ht=1, qkps=2, vps=1, sq=2, rn=1, d1=4, tq=1, tk=1, eq=1, ek=1, ev=1, sc=1, radd=1,
               d2=2, ex=1, pt=2, ept=2, pv=1, d3=2, ot=1, eot=1, wo=1, xadd=1)
    made = {k: steps("att_" + k, v) for k, v in per.items()}
    made["vx"] = [steps(f"att_vx{t}") for t in range(TB)]
    return made


def local_attention(nc, L, sb, ps, steps, q, env):
    NB, NT, S, ident, mk, mhalf = (env[k] for k in ("NB", "NT", "S", "ident", "mk", "mhalf"))
    HEADS, DH, WIN, ready = env["HEADS"], env["DH"], env["WIN"], env["ready"]
    VN, KZ, HT, zcol, rotc = (env[k] for k in ("VN", "KZ", "HT", "zcol", "rotc"))
    INNER = HEADS * DH
    NG = INNER // P
    LAST = 4
    with ExitStack() as ctx:
        wq, wot, scb = q["weights"]
        tab = sb("rot_scaled", [P, TB, 4, DH], ctx=ctx)
        xst = [sb(f"xst{u}", [P, P], ctx=ctx) for u in range(2)]
        SQ = sb("squares", [P, 2 * INNER], ctx=ctx)
        ss = sb("sumsq", [P, 16], ctx=ctx)
        rn = sb("rnorm", [P, 16], ctx=ctx)
        A1 = sb("rot_a", [P, 2 * INNER], ctx=ctx)
        A2 = sb("rot_b", [P, 2 * INNER], ctx=ctx)
        QKN = sb("qk_normed", [P, 2 * INNER], ctx=ctx)
        QT = sb("qt", [P, NG, P], ctx=ctx)
        VX = [sb(f"vx{t}", [P, HEADS, DH + 1], ctx=ctx) for t in range(TB)]
        mx = sb("score_max", [P, HEADS], ctx=ctx)
        SS = sb("scores_less_max", [P, HEADS, P], ctx=ctx)
        PP = sb("probs", [P, HEADS, P], ctx=ctx)
        PT = sb("probs_t", [P, HEADS, P], ctx=ctx)
        rec = sb("rec", [P, HEADS], ctx=ctx)
        ON = sb("o_normed", [P, HEADS, DH], ctx=ctx)
        OT = sb("o_t", [P, NG, P], ctx=ctx)
        QK = ps("qk_ps", [P, 2 * INNER], ctx)
        R = [ps(f"ring{k}", [P, 512], ctx) for k in range(2)]
        SC = ps("scores_ps", [P, HEADS, P], ctx)
        OP = ps("o_ps", [P, 2, 512], ctx)
        OH = OP[:, :, 0:4 * (DH + 1)].rearrange("p b (h d) -> p b h d", d=DH + 1)
        base = L * NT

        def num(b, t):
            return base + b * TB + t

        def run(eng, slot):
            def one(b, t, n=None):
                has = lambda k: n is None or 0 <= n - k < NT
                slot(b, t, lambda k: num(*back(b, t, k, TB)) if k <= TB else num(*back(b - 1, t, k - TB, TB)), has)
            for t in range(TB):
                one(0, t, t)
            with eng.Fori(1, NB) as b:
                for t in range(TB):
                    one(b, t)
            for t in range(LAST):
                one(NB, t, NT + t)

        USES = [("q", 2, 0, "eq", 1), ("k", 2, 1, "ek", 1), ("v", 1, 0, "ev", 1), ("p0", 3, 1, "ept", 1),
                ("p1", 3, 0, "ept", 2)]
        TO, WP, HP = OP[:, 0, :], QK[:, 0:P], QK[:, INNER:INNER + P]

        def ring_wait(pe, use, item, has):
            at = [u[0] for u in USES].index(use)
            bank = USES[at][2]
            earlier = [(u, 0) for u in USES[:at][::-1]] + [(u, 1) for u in USES[::-1]] + [(u, 2) for u in USES[::-1]]
            for (name, lag, bk, sem, step), slots in earlier:
                if bk == bank and has(lag + slots):
                    pe.wait_ge(q[sem].sem, q[sem].at(item(lag + slots), step))
                    return

        with nc.Block() as block:
            @block.sync
            def _(sp):
                env["load_ffn"](sp, L)

                def slot(b, t, item, has):
                    if has(1):
                        bb, t1 = back(b, t, 1, TB)
                        sp.wait_ge(q["ev"].sem, q["ev"].at(item(1)))
                        settle(sp, ready)
                        if has(5):
                            sp.wait_ge(q["pv"].sem, q["pv"].at(item(5)))
                        settle(sp, ready)
                        for lo, src in ((0, VN[t1]), (WIN, VN[(t1 - 1) % TB])):
                            sp.dma_start(VX[t1][lo:lo + WIN, :, :], src[lo:lo + WIN, :, :]).then_inc(q["vx"][t1].sem, 16)
                run(sp, slot)

            @block.gpsimd
            def _(pool):
                def slot(b, t, item, has):
                    if has(0):
                        if has(2):
                            pool.wait_ge(q["hps"].sem, q["hps"].at(item(2)))
                        settle(pool, ready)
                        pool.tensor_copy(xst[t % 2][:, :], S[:, b * TB + t, :]).then_inc(q["xst"].sem, 1)
                    if has(1):
                        pool.wait_ge(q["d1"].sem, q["d1"].at(item(1), 2))
                        pool.tensor_tensor(rn[:, :], ss[:, :], mhalf[:, :], ALU.pow).then_inc(q["rn"].sem, 1)
                        pool.wait_ge(q["d1"].sem, q["d1"].at(item(1), 3))
                        pool.tensor_tensor(A1[:, :], A1[:, :], A2[:, :], ALU.add).then_inc(q["radd"].sem, 1)
                run(pool, slot)

            @block.tensor
            def _(pe):
                pe.wait_ge(q["w_in"].sem, (L + 1) * (16 * 8))

                def slot(b, t, item, has):
                    if has(1):
                        pe.wait_ge(q["ht"].sem, q["ht"].at(item(1)))
                        if has(2):
                            pe.wait_ge(q["d1"].sem, q["d1"].at(item(2), 3))
                            pe.wait_ge(q["sq"].sem, q["sq"].at(item(2)))
                        if has(5):
                            pe.wait_ge(q["xadd"].sem, q["xadd"].at(item(5)))
                        for k in range(2):
                            last = pe.matmul(QK[:, k * INNER:(k + 1) * INNER], HT[(t - 1) % TB][:, :],
                                             wq[:, k * INNER:(k + 1) * INNER], start=True, stop=True)
                            last.then_inc(q["qkps"].sem, 1)
                    if has(2):
                        pe.wait_ge(q["d1"].sem, q["d1"].at(item(2)))
                        for k, (use, done) in enumerate((("q", "tq"), ("k", "tk"))):
                            ring_wait(pe, use, item, has)
                            for p in range(NG):
                                last = pe.transpose(R[k][:, p * P:(p + 1) * P],
                                                    QKN[:, k * INNER + p * P:k * INNER + (p + 1) * P], ident[:, :])
                            last.then_inc(q[done].sem, 1)
                    if has(4):
                        pe.wait_ge(q["d3"].sem, q["d3"].at(item(4)))
                        for p in range(NG):
                            last = pe.transpose(TO[:, p * P:(p + 1) * P],
                                                ON[:, 2 * p:2 * p + 2, :].rearrange("p a b -> p (a b)"), ident[:, :])
                        last.then_inc(q["ot"].sem, 1)
                    if has(1):
                        ring_wait(pe, "v", item, has)
                        pe.matmul(R[0][:, :], HT[(t - 1) % TB][:, :], wq[:, 2 * INNER:], start=True, stop=True)\
                            .then_inc(q["vps"].sem, 1)
                    if has(2):
                        t2 = (t - 2) % TB
                        u = t2 % 2
                        if has(3):
                            pe.wait_ge(q["d2"].sem, q["d2"].at(item(3)))
                        for h4 in (0, 4):
                            pe.matmul(SC[:, h4:h4 + 4, :], mk[:, 4, :],
                                      mk[:, 1 if t2 == 0 else 0, :].unsqueeze(1).to_broadcast([P, 4, P]),
                                      start=True, stop=False, skip_group_check=True)
                        pe.wait_ge(q["eq"].sem, q["eq"].at(item(2)))
                        pe.wait_ge(q["ek"].sem, q["ek"].at(item(2)))
                        for h in range(HEADS):
                            qt = QT[:, h // 2, :]
                            own = KZ[:, u, h, 0:WIN]
                            mixed = bass.AP(own.tensor, own.offset,
                                            [list(own.ap[0]), [(1 - 2 * u) * HEADS * P + WIN, 2], [1, WIN]])
                            pe.matmul(SC[0:WIN, h, :], qt[:, 0:WIN], mixed, start=False, stop=True, skip_group_check=True)
                            last = pe.matmul(SC[WIN:P, h, :], qt[:, WIN:P], KZ[:, u, h, :],
                                             start=False, stop=True, skip_group_check=True)
                        last.then_inc(q["sc"].sem, 1)
                    if has(3):
                        pe.wait_ge(q["ex"].sem, q["ex"].at(item(3)))
                        for k in range(2):
                            ring_wait(pe, f"p{k}", item, has)
                            for p in range(4):
                                last = pe.transpose(R[1 - k][:, p * P:(p + 1) * P], PP[:, 4 * k + p, :], ident[:, :])
                            last.then_inc(q["pt"].sem, 1)
                    if has(0):
                        pe.wait_ge(q["xst"].sem, q["xst"].at(item(0)))
                        if has(1):
                            pe.wait_ge(q["d1"].sem, q["d1"].at(item(1), 3))
                        pe.transpose(HP, xst[t % 2][:, :], ident[:, :]).then_inc(q["hps"].sem, 1)
                    if has(4):
                        pe.wait_ge(q["eot"].sem, q["eot"].at(item(4)))
                        if has(1) and not has(0):
                            pe.wait_ge(q["d1"].sem, q["d1"].at(item(1), 3))
                        for c in range(NG):
                            last = pe.matmul(WP, OT[:, c, :], wot[:, c, :], start=(c == 0), stop=(c == NG - 1))
                        last.then_inc(q["wo"].sem, 1)
                    if has(3):
                        bb, t3 = back(b, t, 3, TB)
                        pe.wait_ge(q["vx"][t3].sem, (L * NB + bb) * 32 + 32)
                        if has(4):
                            pe.wait_ge(q["d3"].sem, q["d3"].at(item(4)))
                            pe.wait_ge(q["eot"].sem, q["eot"].at(item(4)))
                        for h in range(HEADS):
                            if h % 4 == 0:
                                pe.wait_ge(q["ept"].sem, q["ept"].at(item(3), 1 + h // 4))
                            o = OH[:, h // 4, h % 4, :]
                            pe.matmul(o[WIN:P, :], PT[:, h, WIN:P], VN[t3][:, h, :], start=True, stop=True)
                            last = pe.matmul(o[0:WIN, :], PT[:, h, 0:WIN], VX[t3][:, h, :], start=True, stop=True)
                        last.then_inc(q["pv"].sem, 1)
                run(pe, slot)

            @block.scalar
            def _(act):
                def slot(b, t, item, has):
                    if has(1):
                        if has(2):
                            act.wait_ge(q["d1"].sem, q["d1"].at(item(2), 1))
                        for k in range(2):
                            io = slice(k * INNER, (k + 1) * INNER)
                            act.wait_ge(q["qkps"].sem, q["qkps"].at(item(1), k + 1))
                            act.activation(SQ[:, io], QK[:, io], ACT.Square).then_inc(q["sq"].sem, 1)
                    if has(2):
                        u = t % 2
                        act.wait_ge(q["tq"].sem, q["tq"].at(item(2)))
                        if has(3):
                            act.wait_ge(q["sc"].sem, q["sc"].at(item(3)))
                        act.activation(QT[:, :, :].rearrange("p a b -> p (a b)"), R[0][:, :], ACT.Copy)\
                            .then_inc(q["eq"].sem, 1)
                        act.wait_ge(q["tk"].sem, q["tk"].at(item(2)))
                        for half in range(2):
                            r = slice(64 * half, 64 * half + 64)
                            last = act.activation(
                                KZ[r, u, :, :].rearrange("p (a two) k -> p a two k", two=2)[:, :, half, :],
                                R[1][r, :].rearrange("p (a k) -> p a k", k=P), ACT.Copy)
                        last.then_inc(q["ek"].sem, 1)
                    if has(4):
                        act.wait_ge(q["ot"].sem, q["ot"].at(item(4)))
                        if has(5):
                            act.wait_ge(q["wo"].sem, q["wo"].at(item(5)))
                        act.activation(OT[:, :, :].rearrange("p a b -> p (a b)"), TO, ACT.Copy)\
                            .then_inc(q["eot"].sem, 1)
                    if has(1):
                        t1 = (t - 1) % TB
                        act.wait_ge(q["vps"].sem, q["vps"].at(item(1)))
                        act.activation(VN[t1][:, :, 0:DH], R[0][:, :].rearrange("p (h d) -> p h d", d=DH), ACT.Copy)\
                            .then_inc(q["ev"].sem, 1)
                    if has(3):
                        for k in range(2):
                            act.wait_ge(q["pt"].sem, q["pt"].at(item(3), k + 1))
                            if has(4) and k == 0:
                                act.wait_ge(q["pv"].sem, q["pv"].at(item(4)))
                            act.activation(PT[:, 4 * k:4 * k + 4, :].rearrange("p a b -> p (a b)"), R[1 - k][:, :],
                                           ACT.Copy).then_inc(q["ept"].sem, 1)
                    if has(0):
                        act.wait_ge(q["hps"].sem, q["hps"].at(item(0)))
                        nxt = HT[(t + 1) % TB]
                        act.activation(HT[t][0:64, :], HP[0:64, :], ACT.Copy)
                        act.activation(HT[t][64:P, 1:P], HP[64:P, 0:P - 1], ACT.Copy)
                        act.activation(nxt[64:P, 0:1], HP[64:P, P - 1:P] if t < TB - 1 else zcol[64:P, :], ACT.Copy)\
                            .then_inc(q["ht"].sem, 1)
                    if has(2):
                        act.wait_ge(q["d2"].sem, q["d2"].at(item(2)))
                        if has(3):
                            act.wait_ge(q["pt"].sem, q["pt"].at(item(3)))
                        act.activation(PP[:, :, :], SS[:, :, :], ACT.Exp).then_inc(q["ex"].sem, 1)
                run(act, slot)

            @block.vector
            def _(dve):
                dve.wait_ge(q["w_in"].sem, (L + 1) * (16 * 8))
                for t in range(TB):
                    last = dve.tensor_tensor(tab[:, t, :, :], rotc[:, t, :, :], scb[:, :, :], ALU.mult)
                last.then_inc(q["tab"].sem, 2)
                dve.wait_ge(q["tab"].sem, L * 2 + 2)

                def slot(b, t, item, has):
                    if has(1):
                        t1 = (t - 1) % TB
                        d1 = q["d1"]
                        half = DH // 2
                        if has(2):
                            dve.wait_ge(d1.sem, d1.at(item(2)))
                        dve.wait_ge(q["sq"].sem, q["sq"].at(item(1)))
                        dve.tensor_reduce(ss[:, :], SQ[:, :].rearrange("p (h d) -> p h d", d=DH), AX, ALU.add)\
                            .then_inc(d1.sem, 1)
                        for k in range(2):
                            io = slice(k * INNER, (k + 1) * INNER)
                            hd = lambda a: a[:, io].rearrange("p (h d) -> p h d", d=DH)
                            bc = lambda c, lo, hi: tab[:, t1, c, lo:hi].unsqueeze(1).to_broadcast([P, HEADS, hi - lo])
                            dve.tensor_tensor(hd(A1), hd(QK), bc(k, 0, DH), ALU.mult)
                            if k == 0:
                                dve.wait_ge(d1.sem, d1.at(item(1), 1))
                                dve.tensor_scalar(ss[:, :], ss[:, :], 1e-24, None, ALU.max).then_inc(d1.sem, 1)
                            for h in range(2):
                                lo, sw = h * half, (1 - h) * half
                                last = dve.tensor_tensor(hd(A2)[:, :, lo:lo + half], hd(QK)[:, :, sw:sw + half],
                                                         bc(2 + k, lo, lo + half), ALU.mult)
                        last.then_inc(d1.sem, 1)
                    if has(2):
                        d2 = q["d2"]
                        dve.wait_ge(q["sc"].sem, q["sc"].at(item(2)))
                        dve.tensor_reduce(mx[:, :], SC[:, :, :], AX, ALU.max).then_inc(d2.sem, 1)
                        dve.wait_ge(d2.sem, d2.at(item(2), 1))
                        if has(3):
                            dve.wait_ge(q["ex"].sem, q["ex"].at(item(3)))
                        dve.tensor_tensor(SS[:, :, :], SC[:, :, :], mx[:, :].unsqueeze(2).to_broadcast([P, HEADS, P]),
                                          ALU.subtract).then_inc(d2.sem, 1)
                    if has(4):
                        bb, t4 = b - 1, t
                        dve.wait_ge(q["wo"].sem, q["wo"].at(item(4)))
                        xs = S[:, bb * TB + t4, :]
                        dve.tensor_tensor(xs, xs, WP, ALU.add).then_inc(q["xadd"].sem, 1)
                    if has(1):
                        d1 = q["d1"]
                        dve.wait_ge(q["radd"].sem, q["radd"].at(item(1)))
                        dve.wait_ge(q["rn"].sem, q["rn"].at(item(1)))
                        if has(2):
                            dve.wait_ge(q["tk"].sem, q["tk"].at(item(2)))
                        dve.tensor_tensor(QKN[:, :].rearrange("p (h d) -> p h d", d=DH),
                                          A1[:, :].rearrange("p (h d) -> p h d", d=DH),
                                          rn[:, :].unsqueeze(2).to_broadcast([P, 16, DH]), ALU.mult)\
                            .then_inc(d1.sem, 1)
                    if has(3):
                        d3 = q["d3"]
                        dve.wait_ge(q["pv"].sem, q["pv"].at(item(3)))
                        rech = rec[:, :].rearrange("p (b h) -> p b h", b=2)
                        dve.reciprocal(rech, OH[:, :, :, DH]).then_inc(d3.sem, 1)
                        dve.wait_ge(d3.sem, d3.at(item(3), 1))
                        if has(4):
                            dve.wait_ge(q["ot"].sem, q["ot"].at(item(4)))
                        dve.tensor_tensor(ON[:, :, :].rearrange("p (b h) d -> p b h d", b=2), OH[:, :, :, 0:DH],
                                          rech.unsqueeze(3).to_broadcast([P, 2, 4, DH]), ALU.mult)\
                            .then_inc(d3.sem, 1)
                run(dve, slot)


def ffn_sems(steps, Norm, ctx):
    per = dict(w_in=1, sh=1, hb=2, tp=1, ht=1, g=3, a=3, ge=3, z=3, w2=1, xb=1, upd=1)
    made = {k: steps("ffn_" + k, v) for k, v in per.items()}
    made["ln"] = Norm("ffn_ln", ctx, 2, on_act=True)
    return made


def feed_forward(nc, L, sb, ps, steps, q, env):
    NB, S, ident, shiftm, CH, HID, ready = (env[k] for k in ("NB", "S", "ident", "shiftm", "CH", "HID", "ready"))
    ln = q["ln"]
    NCH = len(CH)
    HALF = D // 2
    with ExitStack() as ctx:
        w1t, w2t, gb, b1t, b2t = q["weights"]
        HB = sb("h_normed", [P, TB, D], ctx=ctx)
        HF = sb("h_t", [P, SEQ], ctx=ctx)
        GE = [sb(f"gelu{k}", [P, SEQ], ctx=ctx) for k in range(2)]
        Z = [[sb(f"z{u}_{c}", [P, SEQ], ctx=ctx) for c in range(NCH)] for u in range(2)]
        XB = [sb(f"x_b2_{u}", [P, TB, D], ctx=ctx) for u in range(2)]
        SH = ps("shifted", [P, TB, HALF], ctx)
        TP = ps("h_t_ps", [P, SEQ], ctx)
        GP = [ps(f"g_ps{k}", [P, SEQ], ctx) for k in range(2)]
        AP_ = [ps(f"a_ps{k}", [P, SEQ], ctx) for k in range(2)]
        OB = ps("ffn_out", [P, TB, D], ctx)
        base = L * NB

        def run(eng, slot):
            def one(g, u, n=None):
                has = lambda k: n is None or 0 <= n - k < NB
                slot(g * 2 + u, u, has)
            for n in range(2):
                one(0, n, n)
            with eng.Fori(1, NB // 2) as g:
                for u in range(2):
                    one(g, u)
            for n in range(2):
                one(NB // 2, n, NB + n)

        with nc.Block() as block:
            @block.sync
            def _(sp):
                env["load_attention"](sp, env["DEPTH"] - 1 - L)
                sp.wait_ge(env["sems_a"]["w_in"].sem, (L + 2) * (16 * 8))
                settle(sp, ready)

            W_ALL = (L + 1) * (16 * (4 + 3 * NCH))

            @block.gpsimd
            def _(pool):
                pool.wait_ge(q["w_in"].sem, W_ALL)

                def slot(b, u, has):
                    n = base + b
                    if has(0):
                        if has(2):
                            pool.wait_ge(q["upd"].sem, q["upd"].at(n - 2))
                        if has(1):
                            pool.wait_ge(q["hb"].sem, q["hb"].at(n - 1))
                        ln.power(pool, n)
                        pool.tensor_tensor(XB[u][:, :, :], S[:, bass.ds(b * TB, TB), :],
                                           b2t[:, :].unsqueeze(1).to_broadcast([P, TB, D]), ALU.add)\
                            .then_inc(q["xb"].sem, 1)
                run(pool, slot)

            @block.tensor
            def _(pe):
                pe.wait_ge(q["w_in"].sem, W_ALL)

                def slot(b, u, has):
                    n = base + b
                    if has(1):
                        pe.wait_ge(q["hb"].sem, q["hb"].at(n - 1))
                        if has(2):
                            pe.wait_ge(q["ht"].sem, q["ht"].at(n - 2))
                        for t in range(TB):
                            last = pe.transpose(TP[:, t * P:(t + 1) * P], HB[:, t, :], ident[:, :])
                        last.then_inc(q["tp"].sem, 1)
                    if has(0):
                        if has(1):
                            pe.wait_ge(q["hb"].sem, q["hb"].at(n - 1))
                        pe.matmul(SH[:, :, :], shiftm[:, 0, :], S[:, bass.ds(b * TB, TB), HALF:D],
                                  start=True, stop=False, skip_group_check=True)
                        pe.matmul(SH[:, 1:TB, :], shiftm[:, 1, :], S[:, bass.ds(b * TB, TB - 1), HALF:D],
                                  start=False, stop=True, skip_group_check=True).then_inc(q["sh"].sem, 1)
                    if has(2):
                        pe.wait_ge(q["z"].sem, q["z"].at(n - 2))
                        if has(3):
                            pe.wait_ge(q["upd"].sem, q["upd"].at(n - 3))
                        for t in range(TB):
                            for c, m in enumerate(CH):
                                last = pe.matmul(OB[:, t, :], Z[u][c][0:m, t * P:(t + 1) * P], w2t[0:m, c, :],
                                                 start=(c == 0), stop=(c == NCH - 1), skip_group_check=True)
                        last.then_inc(q["w2"].sem, 1)
                    if has(1):
                        pe.wait_ge(q["ht"].sem, q["ht"].at(n - 1))
                        for c, m in enumerate(CH):
                            if c >= 2:
                                pe.wait_ge(q["z"].sem, q["z"].at(n - 1, c - 1))
                            elif has(2):
                                pe.wait_ge(q["z"].sem, q["z"].at(n - 2, 2 if c == 1 else 3))
                            pe.matmul(GP[c % 2][0:m, :], w1t[:, HID + c * P:HID + c * P + m], HF[:, :],
                                      start=True, stop=True).then_inc(q["g"].sem, 1)
                            pe.matmul(AP_[c % 2][0:m, :], w1t[:, c * P:c * P + m], HF[:, :],
                                      start=True, stop=True).then_inc(q["a"].sem, 1)
                run(pe, slot)

            @block.scalar
            def _(act):
                def slot(b, u, has):
                    n = base + b

                    def shifted_half():
                        if has(1):
                            act.wait_ge(q["tp"].sem, q["tp"].at(n - 1))
                        ln.apply_act(act, n, lambda t: [HB[:, t, HALF:D]], lambda t: [SH[:, t, :]])\
                          .then_inc(q["hb"].sem, 1)
                    if has(0) and not has(1):
                        shifted_half()
                    if has(1):
                        act.wait_ge(q["tp"].sem, q["tp"].at(n - 1))
                        if has(2):
                            act.wait_ge(q["a"].sem, q["a"].at(n - 2))
                        act.activation(HF[:, :], TP[:, :], ACT.Identity, bias=gb[:, 1:2], scale=gb[:, 0:1])\
                            .then_inc(q["ht"].sem, 1)
                        for c, m in enumerate(CH):
                            act.wait_ge(q["g"].sem, q["g"].at(n - 1, c + 1))
                            if c >= 2:
                                act.wait_ge(q["z"].sem, q["z"].at(n - 1, c - 1))
                            elif has(2):
                                act.wait_ge(q["z"].sem, q["z"].at(n - 2, 2 if c == 1 else 3))
                            act.activation(GE[c % 2][0:m, :], GP[c % 2][0:m, :], ACT.Gelu, bias=b1t[0:m, 1, c:c + 1])\
                                .then_inc(q["ge"].sem, 1)
                            if c == 0 and has(0):
                                shifted_half()
                act.wait_ge(q["w_in"].sem, W_ALL)
                run(act, slot)

            @block.vector
            def _(dve):
                dve.wait_ge(q["w_in"].sem, W_ALL)

                def slot(b, u, has):
                    n = base + b
                    pieces = lambda t: [S[:, b * TB + t, 0:HALF], SH[:, t, :]]
                    if has(0):
                        dve.wait_ge(q["sh"].sem, q["sh"].at(n))
                        ln.stats(dve, n, pieces)
                    if has(2):
                        dve.wait_ge(q["w2"].sem, q["w2"].at(n - 2))
                        dve.wait_ge(q["xb"].sem, q["xb"].at(n - 2))
                        dve.tensor_tensor(S[:, bass.ds((b - 2) * TB, TB), :], OB[:, :, :], XB[u][:, :, :], ALU.add)\
                            .then_inc(q["upd"].sem, 1)
                    if has(0):
                        ln.shift(dve, n)
                        if has(1):
                            dve.wait_ge(q["tp"].sem, q["tp"].at(n - 1))
                        ln.apply(dve, n, lambda t: [HB[:, t, 0:HALF]], lambda t: [S[:, b * TB + t, 0:HALF]])\
                          .then_inc(q["hb"].sem, 1)
                    if has(1):
                        for c, m in enumerate(CH):
                            dve.wait_ge(q["a"].sem, q["a"].at(n - 1, c + 1))
                            dve.wait_ge(q["ge"].sem, q["ge"].at(n - 1, c + 1))
                            if c == 0 and has(3):
                                dve.wait_ge(q["w2"].sem, q["w2"].at(n - 3))
                            dve.scalar_tensor_tensor(Z[1 - u][c][0:m, :], AP_[c % 2][0:m, :], b1t[0:m, 0, c:c + 1],
                                                     GE[c % 2][0:m, :], ALU.add, ALU.mult).then_inc(q["z"].sem, 1)
                run(dve, slot)


def causal_attention(nc, sb, ps, steps, Norm, before, env):
    NB, NT, X, S, ident, mk, split_dram, ready = (
        env[k] for k in ("NB", "NT", "X", "S", "ident", "mk", "split_dram", "ready"))
    wat, bat, H2, D2 = (env[k] for k in ("wat", "bat", "H2", "D2"))
    SCALE = float(D2) ** -0.5
    with ExitStack() as outer:
        QS = [sb(f"q_stack{u}", [P, H2, SEQ], BF16, ctx=outer) for u in range(2)]
        KS = [sb(f"k_stack{u}", [P, H2, SEQ], BF16, ctx=outer) for u in range(2)]
        GH = 8
        loaded = [[steps(f"cat_loaded{u}{g}") for g in range(2)] for u in range(2)]
        set_ok = steps("cat_stacks_set")

        def load_stacks(sp, b, u, g):
            heads = slice(g * GH, (g + 1) * GH)
            for a in range(3):
                rows = slice(3 * a * D2, 3 * (a + 1) * D2)
                for dst, k, part, step in ((QS[u], 0, a, 0), (KS[u], 1, 0, D * SEQ)):
                    src = split_dram[b, k, part, g * GH, 0:1]
                    sp.dma_start(dst[rows, heads, :].rearrange("p h s -> p (h s)"),
                                 bass.AP(src.tensor, src.offset, [[step, 3], [H2 * SEQ, D2], [1, GH * SEQ]]))\
                      .then_inc(loaded[u][g].sem, 16)

        with ExitStack() as ctx:
            w = sb("w_attn", [P, 3 * D], ctx=ctx)
            wqk = sb("w_qk", [P, 2, D], ctx=ctx)
            bqk = sb("b_qk", [P, 2], ctx=ctx)
            bqs = sb("b_qk_scaled", [P, 2], ctx=ctx)
            bv = sb("b_v", [P, D], ctx=ctx)
            T = sb("s_normed", [P, TB, D], ctx=ctx)
            Y = sb("attn_in", [P, TB, D], ctx=ctx)
            YT = sb("attn_in_t", [P, SEQ], ctx=ctx)
            F = sb("q_full", [P, SEQ], ctx=ctx)
            Rm = [sb(f"qk_rest{k}", [P, SEQ], ctx=ctx) for k in range(2)]
            PARTS = [sb(f"qk_parts{u}", [P, 2, 3, SEQ], BF16, ctx=ctx) for u in range(2)]
            TPp = ps("in_t_ps", [P, SEQ], ctx)
            QP = [ps(f"qk_p{k}", [P, SEQ], ctx) for k in range(2)]
            VPp = ps("v_p", [P, TB, D], ctx)
            ln1, ln2 = (Norm(f"cln{k}", ctx, on_act=True, after=q) for k, q in enumerate(before))
            w_in, t_ok, x_ok, y_ok, tp, yt, qk, vps, vst = (
                steps("cin_" + n) for n in ("w_in", "t_ok", "x_ok", "y_ok", "tp", "yt", "qk", "vps", "vst"))
            bs_ok, full, rest = steps("cin_bs"), steps("cin_full"), steps("cin_rest", 2)
            p1, p2, p3 = steps("cin_part1", 2), steps("cin_part2", 2), steps("cin_part3", 2)
            stored = [steps(f"cin_stored{u}") for u in range(2)]
            AHEAD = 6

            def run(eng, slot, after=None):
                def one(g, u, n=None):
                    has = lambda k: n is None or 0 <= n - k < NB
                    slot(g * 2 + u, u, has)
                for n in range(AHEAD):
                    one(n // 2, n % 2, n)
                if after:
                    after()
                with eng.Fori(AHEAD // 2, NB // 2) as g:
                    for u in range(2):
                        one(g, u)
                for n in range(NB, NB + 5):
                    one(n // 2, n % 2, n)

            with nc.Block() as block:
                @block.sync
                def _(sp):
                    sp.dma_start(w[:, :], wat).then_inc(w_in.sem, 16)
                    for k in range(2):
                        sp.dma_start(bqk[:, k:k + 1], bat[k * D:(k + 1) * D].rearrange("(h r) -> r h", r=D2),
                                     allow_slow_non_contiguous=True)\
                          .then_inc(w_in.sem, 16)
                    sp.dma_start(bv[:, :], bat[2 * D:3 * D].rearrange("(a n) -> a n", a=1).to_broadcast([P, D]))\
                      .then_inc(w_in.sem, 16)

                    def slot(b, u, has):
                        if has(4):
                            n = b - 4
                            sp.wait_ge(p3.sem, p3.at(n))
                            settle(sp, ready)
                            sp.dma_start(split_dram[n].rearrange("k c d s -> d (k c) s"),
                                         PARTS[u][:, :, :, :].rearrange("p k c s -> p (k c) s"))\
                              .then_inc(stored[u].sem, 16)

                    def first_stacks():
                        sp.wait_ge(set_ok.sem, 4)
                        for u in range(2):
                            sp.wait_ge(stored[u].sem, 16)
                            for g in range(2):
                                load_stacks(sp, u, u, g)
                    run(sp, slot, first_stacks)
                    for u in range(2):
                        sp.wait_ge(stored[u].sem, 16 * (NB // 2))

                @block.gpsimd
                def _(pool):
                    fills = [(QS[0], 0.0), (KS[0], TWO_ONES), (QS[1], 0.0), (KS[1], TWO_ONES)]

                    def slot(b, u, has):
                        if has(1):
                            n = b - 1
                            pool.wait_ge(t_ok.sem, t_ok.at(n))
                        if has(0):
                            ln1.power(pool, b)
                            pool.wait_ge(ln1.rstd.sem, ln1.rstd.at(b))
                        if has(1):
                            xb = X[:, bass.ds(n * TB, TB), :]
                            pool.tensor_tensor(xb, xb, T[:, :, :], ALU.add).then_inc(x_ok.sem, 1)
                            if has(2):
                                pool.wait_ge(y_ok.sem, y_ok.at(n - 1))
                            ln2.power(pool, n)
                            pool.wait_ge(ln2.rstd.sem, ln2.rstd.at(n))
                        if isinstance(b, int) and b < 4:
                            stack, value = fills[b]
                            pool.memset(stack[64:P, :, :].bitcast(F32), value).then_inc(set_ok.sem, 1)
                            pool.wait_ge(set_ok.sem, b + 1)
                    run(pool, slot)

                @block.tensor
                def _(pe):
                    pe.wait_ge(w_in.sem, 64)
                    pe.wait_ge(bs_ok.sem, 1)

                    def slot(b, u, has):
                        if has(3):
                            n = b - 3
                            pe.wait_ge(yt.sem, yt.at(n))
                            if has(4):
                                pe.wait_ge(p1.sem, p1.at(n - 1))
                                pe.wait_ge(rest.sem, rest.at(n - 1))
                            for k in range(2):
                                last = pe.matmul(QP[k][:, :], wqk[:, k, :], YT[:, :], start=True, stop=True)
                            last.then_inc(qk.sem, 1)
                            if has(4):
                                pe.wait_ge(vst.sem, vst.at(n - 1))
                            for t in range(TB):
                                last = pe.matmul(VPp[:, t, :], YT[:, t * P:(t + 1) * P], w[:, 2 * D:3 * D],
                                                 start=True, stop=True)
                            last.then_inc(vps.sem, 1)
                        if has(2):
                            n = b - 2
                            pe.wait_ge(y_ok.sem, y_ok.at(n))
                            if has(3):
                                pe.wait_ge(yt.sem, yt.at(n - 1))
                            for t in range(TB):
                                last = pe.transpose(TPp[:, t * P:(t + 1) * P], Y[:, t, :], ident[:, :])
                            last.then_inc(tp.sem, 1)
                    run(pe, slot)

                @block.scalar
                def _(act):
                    act.wait_ge(w_in.sem, 64)
                    act.activation(wqk[:, :, :].rearrange("p k (r h) -> p k h r", h=H2),
                                   w[:, 0:2 * D].rearrange("p (k h r) -> p k h r", k=2, r=D2), ACT.Copy)
                    act.activation(bqs[:, 0:1], bqk[:, 0:1], ACT.Copy, scale=SCALE)
                    act.activation(bqs[:, 1:2], bqk[:, 1:2], ACT.Copy).then_inc(bs_ok.sem, 1)
                    act.wait_ge(bs_ok.sem, 1)

                    def slot(b, u, has):
                        if has(1):
                            n = b - 1
                            if has(2):
                                act.wait_ge(x_ok.sem, x_ok.at(n - 1))
                            ln1.apply_act(act, n, lambda t: [T[:, t, :]], lambda t: [S[:, n * TB + t, :]])\
                               .then_inc(t_ok.sem, 1)
                        if has(3):
                            n = b - 3
                            act.wait_ge(qk.sem, qk.at(n))
                            if has(5):
                                act.wait_ge(stored[1 - u].sem, (n - 2 - (1 - u)) * 8 + 16)
                            for k in range(2):
                                act.activation(PARTS[1 - u][:, k, 0, :], QP[k][:, :], ACT.Identity,
                                               bias=bqs[:, k:k + 1], scale=SCALE if k == 0 else 1.0)\
                                   .then_inc(p1.sem, 1)
                                if k == 0:
                                    if has(4):
                                        act.wait_ge(rest.sem, rest.at(n - 1, 1))
                                    act.activation(F[:, :], QP[0][:, :], ACT.Identity, bias=bqs[:, 0:1], scale=SCALE)\
                                       .then_inc(full.sem, 1)
                        if has(2):
                            n = b - 2
                            if has(3):
                                act.wait_ge(tp.sem, tp.at(n - 1))
                            ln2.apply_act(act, n, lambda t: [Y[:, t, :]], lambda t: [X[:, n * TB + t, :]])\
                               .then_inc(y_ok.sem, 1)
                        if has(3):
                            n = b - 3
                            for k in range(2):
                                act.wait_ge(rest.sem, rest.at(n, k + 1))
                                act.activation(PARTS[1 - u][:, k, 1, :], Rm[k][:, :], ACT.Copy).then_inc(p2.sem, 1)
                        if has(2):
                            n = b - 2
                            act.wait_ge(tp.sem, tp.at(n))
                            if has(3):
                                act.wait_ge(vps.sem, vps.at(n - 1))
                            act.activation(YT[:, :], TPp[:, :], ACT.Copy).then_inc(yt.sem, 1)
                    run(act, slot)

                @block.vector
                def _(dve):
                    dve.wait_ge(w_in.sem, 64)
                    dve.wait_ge(bs_ok.sem, 1)

                    def slot(b, u, has):
                        if has(1):
                            ln1.shift(dve, b - 1)
                        if has(2):
                            ln2.shift(dve, b - 2)
                        if has(0):
                            ln1.stats(dve, b, lambda t: [S[:, b * TB + t, :]])
                        if has(3):
                            n = b - 3
                            parts = PARTS[1 - u]
                            if has(4):
                                dve.wait_ge(p3.sem, p3.at(n - 1))
                            dve.wait_ge(full.sem, full.at(n))
                            dve.tensor_tensor(Rm[0][:, :], F[:, :], parts[:, 0, 0, :], ALU.subtract).then_inc(rest.sem, 1)
                            dve.wait_ge(p1.sem, p1.at(n))
                            dve.scalar_tensor_tensor(Rm[1][:, :], QP[1][:, :], bqs[:, 1:2], parts[:, 1, 0, :],
                                                     ALU.add, ALU.subtract).then_inc(rest.sem, 1)
                            dve.wait_ge(vps.sem, vps.at(n))
                            dve.tensor_tensor(S[:, bass.ds(n * TB, TB), :], VPp[:, :, :],
                                              bv[:, :].unsqueeze(1).to_broadcast([P, TB, D]), ALU.add)\
                               .then_inc(vst.sem, 1)
                        if has(1):
                            dve.wait_ge(x_ok.sem, x_ok.at(b - 1))
                            ln2.stats(dve, b - 1, lambda t: [X[:, (b - 1) * TB + t, :]])
                        if has(3):
                            for k in range(2):
                                dve.wait_ge(p2.sem, p2.at(n, k + 1))
                                dve.tensor_tensor(parts[:, k, 2, :], Rm[k][:, :], parts[:, k, 1, :],
                                                  ALU.subtract).then_inc(p3.sem, 1)
                    run(dve, slot)

        FULL, MAXR = P, 96
        QH = 4
        NQ = NB * H2 // QH
        CW = P // QH
        OFF = [0, 1 * 512, 1 * P, 2 * 512]
        OFT = [0, 512, 1024, 512 + 3 * P]
        PIECES = [[], [0], [1], [2, 3]]
        with ExitStack() as ctx:
            MX = [sb(f"maxima{g}", [P, GH, TB], ctx=ctx) for g in range(2)]
            NM = sb("neg_max", [GH * TB, P], ctx=ctx)
            MR = sb("neg_max_rest", [GH * TB, P], ctx=ctx)
            MP = [sb(f"neg_max_parts{g}", [GH * TB, 3, P], BF16, ctx=ctx) for g in range(2)]
            PT = [[sb(f"probs_t{u}_{c}", [P, 1280], ctx=ctx) for c in range(QH)] for u in range(2)]
            VS = [sb(f"values_quad{u}", [P, TB, QH, CW], ctx=ctx) for u in range(2)]
            OS = sb("o_quad", [P, SEQ], ctx=ctx)
            rec = sb("crec", [P, TB, QH], ctx=ctx)
            A = ps("scores_a", [P, 3 * 512], ctx)
            B = ps("scores_b", [P, 3 * 512], ctx)
            OP = ps("o_t_quad", [P, SEQ], ctx)
            OX = ps("o_back", [P, TB, QH, CW], ctx)
            MT = OX[0:GH * TB, 0, :, :].rearrange("p c w -> p (c w)")
            vs_zero = steps("cat_vs_zero")
            sc1, red = steps("cat_sc1", 3), steps("cat_red", 3)
            mt, nm, mp = steps("cat_mt"), steps("cat_nm", 4), steps("cat_mp", 1)
            mdma = [steps(f"cat_mdma{g}") for g in range(2)]
            sc2, ex = steps("cat_sc2", 2), steps("cat_ex", 2)
            vs, pv, os_, ox, st = (steps("cat_" + n) for n in ("vs", "pv", "os", "ox", "store"))
            rc = steps("cat_rec")

            def quad(b, hh, k=0):
                b, c = back(b, hh // QH, k, H2 // QH)
                return S[:, bass.ds(b * TB, TB), QH * D2 * c:QH * D2 * (c + 1)].rearrange("p i (h d) -> p i h d", d=D2)

            def run(eng, first, second, last=None, late=3):
                def heads(b, ub, do1, do2):
                    for hh in range(H2):
                        if do1:
                            first(b, ub, hh)
                        if do2:
                            second(b - 1, 1 - ub, hh)
                        if last and hh == late and do2:
                            last(b - 1, 1 - ub, 1)
                        if last and hh == GH + late and do1:
                            last(b, ub, 0)
                heads(0, 0, True, False)
                heads(1, 1, True, True)
                with eng.Fori(1, NB // 2) as bp:
                    for ub in range(2):
                        heads(bp * 2 + ub, ub, True, True)
                heads(NB, 0, False, True)

            def at_least(n, low):
                return not isinstance(n, int) or n >= low

            with nc.Block() as block:
                @block.sync
                def _(sp):
                    def maxima(b, ub, g):
                        sp.wait_ge(mp.sem, mp.at(b * 2 + g))
                        settle(sp, ready)
                        for c in range(3):
                            sp.dma_start(QS[ub][MAXR + c:MAXR + c + 1, g * GH:(g + 1) * GH, :]
                                         .rearrange("p h s -> p (h s)"), MP[g][:, c, :]).then_inc(mdma[g].sem, 16)

                    def load(b, ub, g):
                        sp.wait_ge(sc2.sem, sc2.at((b - 2) * H2 + (g + 1) * GH - 1))
                        settle(sp, ready)
                        load_stacks(sp, b, ub, g)
                    env["load_moe"](sp)
                    maxima(0, 0, 0)
                    with sp.Fori(0, NB // 2 - 1) as j:
                        for k in range(2):
                            b, ub = j * 2 + 1 + k, 1 - k
                            maxima(b - 1, 1 - ub, 1)
                            load(b + 1, 1 - ub, 0)
                            maxima(b, ub, 0)
                            load(b + 1, 1 - ub, 1)
                    maxima(NB - 2, 0, 1)
                    for g in range(2):
                        maxima(NB - 1, 1, g)

                @block.gpsimd
                def _(pool):
                    for u in range(2):
                        last = pool.memset(VS[u][:, :, :, :], 0.0)
                    last.then_inc(vs_zero.sem, 1)
                    pool.wait_ge(vs_zero.sem, 1)
                    for u in range(2):
                        last = pool.memset(VS[u][:, :, :, D2:D2 + 1], 1.0)
                    last.then_inc(vs_zero.sem, 1)
                    pool.wait_ge(vs_zero.sem, 2)

                    def second(b, ub, hh):
                        if hh % QH == 0:
                            n = b * (H2 // QH) + hh // QH
                            if at_least(n, 2):
                                pool.wait_ge(pv.sem, pv.at(n - 2))
                                settle(pool, ready)
                            pool.tensor_copy(VS[(hh // QH) % 2][:, :, :, 0:D2], quad(b, hh))\
                                .then_inc(vs.sem, 1)
                    run(pool, lambda *a: None, second)

                @block.tensor
                def _(pe):
                    def first(b, ub, hh):
                        m = b * H2 + hh
                        q, k = QS[ub], KS[ub]
                        if hh % GH == 0:
                            pe.wait_ge(loaded[ub][hh // GH].sem, ((b - ub) * 8 + 16) * 6)
                        for s, tiles in enumerate(([3], [1], [0, 2])):
                            if at_least(m, 1):
                                pe.wait_ge(red.sem, red.at(m - 1, s + 1))
                            for i in tiles:
                                o = A[:, OFF[i]:OFF[i] + (i + 1) * P]
                                pe.matmul(o, q[0:MAXR, hh, i * P:(i + 1) * P], k[0:MAXR, hh, 0:(i + 1) * P],
                                          start=True, stop=False, skip_group_check=True)
                                last = pe.matmul(o[:, i * P:], mk[:, 4, :], mk[:, 2, :], start=False, stop=True,
                                                 skip_group_check=True)
                            last.then_inc(sc1.sem, 1)

                    def values(n, u, pieces):
                        if 0 in pieces:
                            pe.wait_ge(ex.sem, ex.at(n * QH + QH - 1))
                            pe.wait_ge(vs.sem, vs.at(n))
                            if at_least(n, 1):
                                pe.wait_ge(os_.sem, os_.at(n - 1))
                        for j in pieces:
                            for c in range(QH):
                                last = pe.matmul(OP[CW * c:CW * (c + 1), j * P:], VS[u][:, j, c, :],
                                                 PT[u][c][:, OFT[j]:OFT[j] + (TB - j) * P],
                                                 start=(j == 0), stop=(j == TB - 1), skip_group_check=True)
                            if j == TB - 1:
                                last.then_inc(pv.sem, 1)

                    def turn(n):
                        pe.wait_ge(os_.sem, os_.at(n))
                        if at_least(n, 1):
                            pe.wait_ge(st.sem, st.at(n - 1))
                        for i in range(TB):
                            last = pe.transpose(OX[:, i, :, :].rearrange("p c w -> p (c w)"), OS[:, i * P:(i + 1) * P],
                                                ident[:, :])
                        last.then_inc(ox.sem, 1)

                    def second(b, ub, hh):
                        m = b * H2 + hh
                        n, c = b * (H2 // QH) + hh // QH, hh % QH
                        q, k = QS[ub], KS[ub]
                        if at_least(n, 1) and PIECES[c]:
                            values(n - 1, (hh // QH - 1) % 2, PIECES[c])
                        if c == 1 and at_least(n, 2):
                            went = (b + 1) * 2 - 2 + (hh > 3) + (hh > GH + 3 and not (isinstance(b, int) and b == NB - 1))
                            pe.wait_ge(nm.sem, nm.at(went, 1))
                            turn(n - 2)
                        if hh % GH == 0:
                            pe.wait_ge(mdma[hh // GH].sem, (b + 1) * 48)
                        for s, tiles in enumerate(([0, 1, 3], [2])):
                            if at_least(m, 1):
                                pe.wait_ge(ex.sem, ex.at(m - 1, s + 1))
                            for j in tiles:
                                o = B[:, OFT[j]:OFT[j] + (TB - j) * P]
                                pe.matmul(o, k[0:FULL, hh, j * P:(j + 1) * P], q[0:FULL, hh, j * P:],
                                          start=True, stop=False, skip_group_check=True)
                                last = pe.matmul(o[:, 0:P], mk[:, 4, :], mk[:, 3, :], start=False, stop=True,
                                                 skip_group_check=True)
                            last.then_inc(sc2.sem, 1)

                    def last(b, ub, g):
                        n = b * 2 + g
                        pe.wait_ge(red.sem, red.at(b * H2 + g * GH + GH - 1))
                        if at_least(n, 1):
                            pe.wait_ge(nm.sem, nm.at(n - 1, 1))
                        done = b * (H2 // QH) - 4 + (2 * g + 2) - 2
                        if at_least(done, 0):
                            pe.wait_ge(st.sem, st.at(done))
                        pe.transpose(MT, MX[g][:, :, :].rearrange("p h i -> p (h i)"), ident[:, :]).then_inc(mt.sem, 1)
                    run(pe, first, second, last)
                    values(NQ - 1, 1, [0, 1, 2, 3])
                    turn(NQ - 2)
                    turn(NQ - 1)

                @block.scalar
                def _(act):
                    def out(n):
                        act.wait_ge(pv.sem, pv.at(n))
                        if at_least(n, 1):
                            act.wait_ge(ox.sem, ox.at(n - 1))
                        act.activation(OS[:, :], OP[:, :], ACT.Copy).then_inc(os_.sem, 1)

                    def second(b, ub, hh):
                        m = b * H2 + hh
                        n, c = b * (H2 // QH) + hh // QH, hh % QH
                        u = (hh // QH) % 2
                        if c == 0 and at_least(n, 2):
                            out(n - 2)
                        act.wait_ge(sc2.sem, sc2.at(m, 1))
                        act.activation(PT[u][c][:, 0:1024], B[:, 0:1024], ACT.Exp).then_inc(ex.sem, 1)
                        act.wait_ge(sc2.sem, sc2.at(m, 2))
                        act.activation(PT[u][c][:, 1024:1280], B[:, 1024:1280], ACT.Exp).then_inc(ex.sem, 1)

                    def last(b, ub, g):
                        act.wait_ge(mt.sem, mt.at(b * 2 + g))
                        act.activation(NM[:, :], MT, ACT.Copy, scale=-1.0).then_inc(nm.sem, 1)
                    run(act, lambda *a: None, second, last)
                    out(NQ - 2)
                    out(NQ - 1)

                @block.vector
                def _(dve):
                    def first(b, ub, hh):
                        m, g = b * H2 + hh, hh // GH
                        if hh % GH == 0 and at_least(b, 1):
                            dve.wait_ge(mt.sem, mt.at(b * 2 + g - 2))
                        for s, tiles in enumerate(([3], [1], [0, 2])):
                            dve.wait_ge(sc1.sem, sc1.at(m, s + 1))
                            for i in tiles:
                                last = dve.tensor_reduce(MX[g][:, hh % GH, i:i + 1], A[:, OFF[i]:OFF[i] + (i + 1) * P],
                                                         AX, ALU.max)
                            last.then_inc(red.sem, 1)

                    def store(n, place):
                        dve.wait_ge(ox.sem, ox.at(n))
                        dve.reciprocal(rec[:, :, :], OX[:, :, :, D2]).then_inc(rc.sem, 1)
                        dve.wait_ge(rc.sem, rc.at(n))
                        dve.tensor_tensor(place, OX[:, :, :, 0:D2],
                                          rec[:, :, :].unsqueeze(3).to_broadcast([P, TB, QH, D2]), ALU.mult)\
                            .then_inc(st.sem, 1)

                    def second(b, ub, hh):
                        n, c = b * (H2 // QH) + hh // QH, hh % QH
                        if c == 1 and at_least(n, 2):
                            store(n - 2, quad(b, hh, 2))

                    def last(b, ub, g):
                        n = b * 2 + g
                        dve.wait_ge(nm.sem, nm.at(n, 1))
                        if at_least(b, 1):
                            dve.wait_ge(mdma[g].sem, (b - 1) * 48 + 48)
                        dve.tensor_copy(MP[g][:, 0, :], NM[:, :]).then_inc(nm.sem, 1)
                        dve.wait_ge(nm.sem, nm.at(n, 2))
                        dve.tensor_tensor(MR[:, :], NM[:, :], MP[g][:, 0, :], ALU.subtract).then_inc(nm.sem, 1)
                        dve.wait_ge(nm.sem, nm.at(n, 3))
                        dve.tensor_copy(MP[g][:, 1, :], MR[:, :]).then_inc(nm.sem, 1)
                        dve.wait_ge(nm.sem, nm.at(n, 4))
                        dve.tensor_tensor(MP[g][:, 2, :], MR[:, :], MP[g][:, 1, :], ALU.subtract).then_inc(mp.sem, 1)
                    run(dve, first, second, last, 4)
                    store(NQ - 2, quad(NB - 1, H2 - 1, 1))
                    store(NQ - 1, quad(NB - 1, H2 - 1))
    return ln1, ln2


def experts(nc, sb, ps, steps, Norm, before, env):
    NB, X, S, ident, out, NE, ready = (env[k] for k in ("NB", "X", "S", "ident", "out", "NE", "ready"))
    br, bs, NS = (env[k] for k in ("br", "bs", "NS"))
    EB = 4
    with ExitStack() as ctx:
        wp, bp_, cen, eb, wr, ws = (env["moe"][k] for k in ("wp", "bp_", "cen", "eb", "wr", "ws"))
        wss = sb("w_shared_mean", [P, D], ctx=ctx)
        brs = sb("biases", [P, D], ctx=ctx)
        GT = sb("gates_t", [P, SEQ], ctx=ctx)
        iot = sb("iota", [P, NE], ctx=ctx)
        iot_i = sb("iota_i", [P, NE], mybir.dt.int32, ctx=ctx)
        AO = [sb(f"attn_out{u}", [P, TB, D], ctx=ctx) for u in range(2)]
        AT = sb("attn_out_t", [P, SEQ], ctx=ctx)
        PO = sb("proj", [P, TB, D], ctx=ctx)
        T = sb("proj_normed", [P, TB, D], ctx=ctx)
        U = [sb(f"u{u}", [P, TB, D], ctx=ctx) for u in range(2)]
        UT = [sb(f"u_t{u}", [P, SEQ], ctx=ctx) for u in range(2)]
        sc = sb("route", [P, TB, NE], ctx=ctx)
        se = sb("route_exp", [P, TB, NE], ctx=ctx)
        sp_ = sb("route_p", [P, TB, NE], ctx=ctx)
        sm = sb("route_stat", [P, 3, TB], ctx=ctx)
        top = sb("top8", [P, TB, 8], ctx=ctx)
        tix = sb("top8_index", [P, TB, 8], mybir.dt.uint32, ctx=ctx)
        tif = sb("top2_index", [P, TB, 2], ctx=ctx)
        eq = sb("chosen", [P, TB, 2, NE], ctx=ctx)
        g2 = sb("gate_parts", [P, TB, 2, NE], ctx=ctx)
        gt = [sb(f"gates{u}", [P, TB, NE], ctx=ctx) for u in range(2)]
        ACC = sb("acc", [P, TB, D], ctx=ctx)
        PR = sb("products", [P, TB, EB, D], ctx=ctx)
        H = sb("products_half", [P, TB, 2, D], ctx=ctx)
        Q = sb("products_sum", [P, TB, D], ctx=ctx)
        Z = sb("mixture", [P, TB, D], ctx=ctx)
        OUT = [sb(f"out{u}", [P, TB, D], ctx=ctx) for u in range(2)]
        TN = sb("out_normed", [P, TB, D], ctx=ctx)
        R = [ps(f"e_ring{k}", [P, SEQ], ctx) for k in range(2)]
        BP = ps("base_ps", [P, TB, D], ctx)
        E = [ps(f"experts{k}", [P, EB, D], ctx) for k in range(4)]
        EA = ps("experts_act", [P, EB, D], ctx)
        ln1, ln2, ln3 = (Norm(f"eln{k}", ctx, on_act=True, after=q) for k, q in enumerate(before))
        (w_in, init, ao, at_ps, at, po_ps, po, t_ok, x_ok, u_ok, ut_ps, ut, sc_ps, gt_ok, gtt_ps, gtt, bp_ps, fin) = (
            steps("exp_" + n) for n in ("w_in", "init", "ao", "at_ps", "at", "po_ps", "po", "t_ok", "x_ok", "u_ok",
                                        "ut_ps", "ut", "sc_ps", "gates", "gtt_ps", "gtt", "bp_ps", "fin"))
        rt, rex = steps("exp_route", 6), steps("exp_rex")
        KD = NE // EB - 1
        eps_, chain, total = steps("exp_e", 4 * KD), steps("exp_chain", 4 * KD * EB), steps("exp_total", 2)
        ea_ps, ea, pool_sum = steps("exp_ea_ps", TB), steps("exp_ea", TB), steps("exp_pool_sum", 2)
        n_ok, o_ok = steps("exp_norm"), steps("exp_out")
        shared_w = steps("exp_shared_w")
        tk = steps("exp_topk", 5)
        stored = [steps(f"exp_stored{u}") for u in range(2)]
        OV = out.rearrange("b (t p) d -> b p t d", p=P)
        PIECES = [(p, k) for p in range(2) for k in range(KD)]

        def run(eng, slot, extra=2):
            def one(g, u, n=None):
                has = lambda k: n is None or 0 <= n - k < NB
                slot(g * 2 + u, u, has)
            for n in range(4):
                one(n // 2, n % 2, n)
            with eng.Fori(2, NB // 2) as g:
                for u in range(2):
                    one(g, u)
            for n in range(extra):
                one(NB // 2, n, NB + n)

        with nc.Block() as block:
            @block.sync
            def _(sp):
                sp.wait_ge(init.sem, 2)
                for dst, src in ((brs[0:NE, :], br), (brs[32:32 + NS, :], bs)):
                    sp.dma_start(dst, src).then_inc(w_in.sem, 16)

                def slot(b, u, has):
                    if has(2):
                        sp.wait_ge(o_ok.sem, o_ok.at(b - 2))
                        settle(sp, ready)
                        sp.dma_start(OV[b - 2], OUT[u][:, :, :]).then_inc(stored[u].sem, 16)
                run(sp, slot)
                for u in range(2):
                    sp.wait_ge(stored[u].sem, 16 * (NB // 2))

            @block.gpsimd
            def _(pool):
                pool.memset(brs[:, :], 0.0).then_inc(init.sem, 1)
                pool.memset(GT[:, :], 0.0).then_inc(init.sem, 1)
                pool.wait_ge(init.sem, 2)
                pool.memset(GT[32:32 + NS, :], 1.0 / NS).then_inc(init.sem, 1)
                pool.wait_ge(init.sem, 3)
                pool.iota(iot_i[:, :], pattern=[[1, NE]], base=0, channel_multiplier=0).then_inc(init.sem, 1)
                pool.wait_ge(init.sem, 4)
                pool.tensor_copy(iot[:, :], iot_i[:, :]).then_inc(init.sem, 1)
                pool.wait_ge(init.sem, 5)

                def slot(b, u, has):
                    if has(0):
                        if has(2):
                            pool.wait_ge(at_ps.sem, at_ps.at(b - 2))
                        if has(2):
                            pool.wait_ge(pool_sum.sem, pool_sum.at(b - 2))
                        elif has(1):
                            pool.wait_ge(ln2.rstd.sem, ln2.rstd.at(b - 1))
                        settle(pool, ready)
                        pool.tensor_copy(AO[u][:, :, :], S[:, bass.ds(b * TB, TB), :]).then_inc(ao.sem, 1)
                        pool.wait_ge(ao.sem, ao.at(b))
                    elif has(2):
                        pool.wait_ge(pool_sum.sem, pool_sum.at(b - 2))
                    if has(2):
                        ln3.power(pool, b - 2)
                        pool.wait_ge(ln3.rstd.sem, ln3.rstd.at(b - 2))
                    if has(0):
                        ln1.power(pool, b)
                        pool.wait_ge(ln1.rstd.sem, ln1.rstd.at(b))
                    if has(0):
                        pool.wait_ge(t_ok.sem, t_ok.at(b))
                        xb = X[:, bass.ds(b * TB, TB), :]
                        pool.tensor_tensor(xb, xb, T[:, :, :], ALU.add).then_inc(x_ok.sem, 1)
                        pool.wait_ge(x_ok.sem, x_ok.at(b))
                    if has(2):
                        pool.wait_ge(n_ok.sem, n_ok.at(b - 2))
                        if has(4):
                            pool.wait_ge(stored[u].sem, (b - 4 - u) * 8 + 16)
                        pool.tensor_tensor(OUT[u][:, :, :], X[:, bass.ds((b - 2) * TB, TB), :], TN[:, :, :], ALU.add)\
                            .then_inc(o_ok.sem, 1)
                        pool.wait_ge(o_ok.sem, o_ok.at(b - 2))
                    if has(0):
                        ln2.power(pool, b)
                    if has(1):
                        if has(0):
                            pool.wait_ge(ln2.rstd.sem, ln2.rstd.at(b))
                        pool.wait_ge(ea.sem, ea.at(b - 1))
                        pool.tensor_tensor(H[:, :, :, :], PR[:, :, 0:2, :], PR[:, :, 2:4, :], ALU.add)\
                            .then_inc(pool_sum.sem, 1)
                        pool.wait_ge(pool_sum.sem, pool_sum.at(b - 1, 1))
                        if has(2):
                            pool.wait_ge(total.sem, total.at(b - 2))
                        pool.tensor_tensor(Q[:, :, :], H[:, :, 0, :], H[:, :, 1, :], ALU.add).then_inc(pool_sum.sem, 1)
                run(pool, slot)

            @block.tensor
            def _(pe):
                pe.wait_ge(env["moe_in"].sem, 16 * 6)
                pe.wait_ge(w_in.sem, 16 * 2)
                pe.wait_ge(init.sem, 5)
                pe.wait_ge(shared_w.sem, 2)

                def fill(n, u, has, j):
                    if not has(1):
                        return
                    p, k = PIECES[j]
                    for tt in range(2):
                        f = 2 * j + tt
                        if f >= 4:
                            pe.wait_ge(chain.sem, chain.at(n, (f - 4) // 2 * 8 + 7 + tt))
                        elif has(2):
                            pe.wait_ge(chain.sem, chain.at(n - 1, (f + 4 * KD - 4) // 2 * 8 + 7 + tt))
                        t = 2 * p + tt
                        pe.matmul(E[f % 4][:, :, :], UT[u][:, t * P:(t + 1) * P], wr[:, EB * k:EB * (k + 1), :],
                                  start=True, stop=True).then_inc(eps_.sem, 1)

                def fill_act(n, u, has, t):
                    if not has(1):
                        return
                    if t > 0:
                        pe.wait_ge(ea.sem, ea.at(n, t))
                    elif has(2):
                        pe.wait_ge(ea.sem, ea.at(n - 1))
                    pe.matmul(EA[:, :, :], UT[u][:, t * P:(t + 1) * P], wr[:, EB * KD:, :], start=True, stop=True)\
                      .then_inc(ea_ps.sem, 1)

                def slot(b, u, has):
                    n, v = b - 1, 1 - u
                    if has(0):
                        pe.wait_ge(ao.sem, ao.at(b))
                        if has(1):
                            pe.wait_ge(ut.sem, ut.at(b - 1))
                        for t in range(TB):
                            last = pe.transpose(R[0][:, t * P:(t + 1) * P], AO[u][:, t, :], ident[:, :])
                        last.then_inc(at_ps.sem, 1)
                    fill(n, v, has, 0)
                    if has(0):
                        pe.wait_ge(at.sem, at.at(b))
                        if has(1):
                            pe.wait_ge(rt.sem, rt.at(b - 1, 1))
                        for t in range(TB):
                            last = pe.matmul(R[1][:, t * P:(t + 1) * P], AT[:, t * P:(t + 1) * P], wp[:, :],
                                             start=True, stop=True)
                        last.then_inc(po_ps.sem, 1)
                    fill(n, v, has, 1)
                    fill_act(n, v, has, 0)
                    if has(1):
                        pe.wait_ge(gt_ok.sem, gt_ok.at(n))
                        if not has(0):
                            pe.wait_ge(ut.sem, ut.at(n))
                        for t in range(TB):
                            last = pe.transpose(R[0][0:NE, t * P:(t + 1) * P], gt[v][:, t, :], ident[:, :])
                        last.then_inc(gtt_ps.sem, 1)
                    fill(n, v, has, 2)
                    fill_act(n, v, has, 1)
                    if has(1):
                        pe.wait_ge(gtt.sem, gtt.at(n))
                        if has(2):
                            pe.wait_ge(total.sem, total.at(n - 1))
                        for t in range(TB):
                            pe.matmul(BP[:, t, :], GT[:, t * P:(t + 1) * P], brs[:, :], start=True, stop=False,
                                      skip_group_check=True)
                            last = pe.matmul(BP[:, t, :], UT[v][:, t * P:(t + 1) * P], wss[:, :], start=False, stop=True,
                                             skip_group_check=True)
                        last.then_inc(bp_ps.sem, 1)
                    fill(n, v, has, 3)
                    fill_act(n, v, has, 2)
                    fill(n, v, has, 4)
                    fill_act(n, v, has, 3)
                    fill(n, v, has, 5)
                    if has(0):
                        pe.wait_ge(u_ok.sem, u_ok.at(b))
                        if has(1):
                            pe.wait_ge(gtt.sem, gtt.at(n))
                        for t in range(TB):
                            last = pe.transpose(R[0][:, t * P:(t + 1) * P], U[u][:, t, :], ident[:, :])
                        last.then_inc(ut_ps.sem, 1)
                    if has(0):
                        pe.wait_ge(ut.sem, ut.at(b))
                        pe.wait_ge(po.sem, po.at(b))
                        for t in range(TB):
                            last = pe.matmul(R[1][:, t * NE:(t + 1) * NE], UT[u][:, t * P:(t + 1) * P], cen[:, :],
                                             start=True, stop=True)
                        last.then_inc(sc_ps.sem, 1)
                run(pe, slot, 1)

            @block.scalar
            def _(act):
                def products(n, u, has, t):
                    if not has(1):
                        return
                    act.wait_ge(ea_ps.sem, ea_ps.at(n, t + 1))
                    if has(2) and t == 0:
                        act.wait_ge(pool_sum.sem, pool_sum.at(n - 1, 1))
                    if t == 0:
                        act.wait_ge(gt_ok.sem, gt_ok.at(n))
                    for e in range(EB):
                        i = EB * KD + e
                        last = act.activation(PR[:, t, e, :], EA[:, e, :], ACT.Copy, scale=gt[u][:, t, i:i + 1])
                    last.then_inc(ea.sem, 1)

                def slot(b, u, has):
                    n, v = b - 1, 1 - u
                    if has(0):
                        act.wait_ge(at_ps.sem, at_ps.at(b))
                        if has(1):
                            act.wait_ge(po_ps.sem, po_ps.at(b - 1))
                        act.activation(AT[:, :], R[0][:, :], ACT.Copy).then_inc(at.sem, 1)
                    products(n, v, has, 0)
                    if has(1):
                        act.wait_ge(gtt_ps.sem, gtt_ps.at(n))
                        if has(2):
                            act.wait_ge(bp_ps.sem, bp_ps.at(n - 1))
                        act.activation(GT[0:NE, :], R[0][0:NE, :], ACT.Copy).then_inc(gtt.sem, 1)
                    products(n, v, has, 1)
                    if has(0):
                        if has(1):
                            act.wait_ge(x_ok.sem, x_ok.at(n))
                        ln1.apply_act(act, b, lambda t: [T[:, t, :]], lambda t: [PO[:, t, :]]).then_inc(t_ok.sem, 1)
                    if has(2):
                        if has(3):
                            act.wait_ge(o_ok.sem, o_ok.at(b - 3))
                        ln3.apply_act(act, b - 2, lambda t: [TN[:, t, :]], lambda t: [Z[:, t, :]]).then_inc(n_ok.sem, 1)
                    products(n, v, has, 2)
                    products(n, v, has, 3)
                    if has(0):
                        ln2.apply_act(act, b, lambda t: [U[u][:, t, :]], lambda t: [X[:, b * TB + t, :]])\
                           .then_inc(u_ok.sem, 1)
                        act.wait_ge(ut_ps.sem, ut_ps.at(b))
                        act.activation(UT[u][:, :], R[0][:, :], ACT.Copy).then_inc(ut.sem, 1)
                        act.wait_ge(rt.sem, rt.at(b, 3))
                        act.activation(se[:, :, :], sc[:, :, :], ACT.Exp).then_inc(rex.sem, 1)
                run(act, slot)

            @block.vector
            def _(dve):
                dve.wait_ge(env["moe_in"].sem, 16 * 6)
                assert NS == 2
                dve.tensor_tensor(wss[:, :], ws[:, 0, :], ws[:, 1, :], ALU.add).then_inc(shared_w.sem, 1)
                dve.wait_ge(shared_w.sem, 1)
                dve.tensor_scalar(wss[:, :], wss[:, :], 1.0 / NS, None, ALU.mult).then_inc(shared_w.sem, 1)
                dve.wait_ge(init.sem, 5)

                def piece(n, u, has, j):
                    if not has(1):
                        return
                    p, k = PIECES[j]
                    for e in range(EB):
                        for tt in range(2):
                            i, t, f = EB * k + e, 2 * p + tt, 2 * j + tt
                            step = j * 8 + e * 2 + tt
                            if e == 0:
                                dve.wait_ge(eps_.sem, eps_.at(n, f + 1))
                            if i > 0:
                                dve.wait_ge(chain.sem, chain.at(n, step - 1))
                            base = U[u][:, t, :] if i == 0 else ACC[:, t, :]
                            dve.scalar_tensor_tensor(ACC[:, t, :], E[f % 4][:, e, :], gt[u][:, t, i:i + 1], base,
                                                     ALU.mult, ALU.add).then_inc(chain.sem, 1)

                def slot(b, u, has):
                    n, v = b - 1, 1 - u
                    xt = lambda t: [X[:, b * TB + t, :]]
                    if has(0):
                        dve.wait_ge(po_ps.sem, po_ps.at(b))
                        dve.tensor_tensor(PO[:, :, :], R[1][:, :].rearrange("p (t d) -> p t d", d=D),
                                          bp_[:, :].unsqueeze(1).to_broadcast([P, TB, D]), ALU.add).then_inc(po.sem, 1)
                    if has(1):
                        dve.wait_ge(gt_ok.sem, gt_ok.at(n))
                    piece(n, v, has, 0)
                    if has(0):
                        dve.wait_ge(po.sem, po.at(b))
                        ln1.stats(dve, b, lambda t: [PO[:, t, :]])
                    if has(2):
                        ln3.shift(dve, b - 2)
                    piece(n, v, has, 1)
                    if has(0):
                        ln1.shift(dve, b)
                    piece(n, v, has, 2)
                    piece(n, v, has, 3)
                    if has(0):
                        dve.wait_ge(x_ok.sem, x_ok.at(b))
                        ln2.stats(dve, b, xt)
                    piece(n, v, has, 4)
                    if has(0):
                        ln2.shift(dve, b)
                    piece(n, v, has, 5)
                    if has(1):
                        dve.wait_ge(bp_ps.sem, bp_ps.at(n))
                        dve.wait_ge(chain.sem, chain.at(n))
                        if has(2):
                            dve.wait_ge(n_ok.sem, n_ok.at(n - 1))
                        dve.tensor_tensor(Z[:, :, :], ACC[:, :, :], BP[:, :, :], ALU.add).then_inc(total.sem, 1)
                        dve.wait_ge(pool_sum.sem, pool_sum.at(n))
                        dve.wait_ge(total.sem, total.at(n, 1))
                        dve.tensor_tensor(Z[:, :, :], Z[:, :, :], Q[:, :, :], ALU.add).then_inc(total.sem, 1)
                    if has(0):
                        dve.wait_ge(sc_ps.sem, sc_ps.at(b))
                        ebb = eb[:, :].unsqueeze(1).to_broadcast([P, TB, NE])
                        dve.tensor_tensor(sc[:, :, :], R[1][:, 0:TB * NE].rearrange("p (t e) -> p t e", e=NE), ebb, ALU.add)\
                            .then_inc(rt.sem, 1)
                    if has(1):
                        dve.wait_ge(total.sem, total.at(n))
                        ln3.pieces_stats(dve, lambda t: [Z[:, t, :]])
                    if has(0):
                        dve.wait_ge(rt.sem, rt.at(b, 1))
                        dve.tensor_reduce(sm[:, 0, :], sc[:, :, :], AX, ALU.max).then_inc(rt.sem, 1)
                        dve.wait_ge(rt.sem, rt.at(b, 2))
                        bc = lambda k: sm[:, k, :].unsqueeze(2).to_broadcast([P, TB, NE])
                        dve.tensor_tensor(sc[:, :, :], sc[:, :, :], bc(0), ALU.subtract).then_inc(rt.sem, 1)
                    if has(1):
                        ln3.aggregate(dve, n)
                        ln3.variance(dve, n)
                    if has(0):
                        dve.wait_ge(rex.sem, rex.at(b))
                        dve.tensor_reduce(sm[:, 1, :], se[:, :, :], AX, ALU.add).then_inc(rt.sem, 1)
                        dve.wait_ge(rt.sem, rt.at(b, 4))
                        dve.reciprocal(sm[:, 2, :], sm[:, 1, :]).then_inc(rt.sem, 1)
                        dve.wait_ge(rt.sem, rt.at(b, 5))
                        dve.tensor_tensor(sp_[:, :, :], se[:, :, :], bc(2), ALU.mult).then_inc(rt.sem, 1)
                        dve.wait_ge(rt.sem, rt.at(b, 6))
                        settle(dve, ready)
                        for t in range(TB):
                            last = dve.max(top[:, t, :], sp_[:, t, :])
                        last.then_inc(tk.sem, 1)
                        dve.wait_ge(tk.sem, tk.at(b, 1))
                        settle(dve, ready)
                        for t in range(TB):
                            last = dve.max_index(tix[:, t, :], top[:, t, :], sp_[:, t, :])
                        last.then_inc(tk.sem, 1)
                        dve.wait_ge(tk.sem, tk.at(b, 2))
                        dve.tensor_copy(tif[:, :, :], tix[:, :, 0:2]).then_inc(tk.sem, 1)
                        dve.wait_ge(tk.sem, tk.at(b, 3))
                        pairs = [P, TB, 2, NE]
                        dve.tensor_tensor(eq[:, :, :, :], iot[:, :].unsqueeze(1).unsqueeze(1).to_broadcast(pairs),
                                          tif[:, :, :].unsqueeze(3).to_broadcast(pairs), ALU.is_equal).then_inc(tk.sem, 1)
                        dve.wait_ge(tk.sem, tk.at(b, 4))
                        dve.tensor_tensor(g2[:, :, :, :], eq[:, :, :, :],
                                          sp_[:, :, :].unsqueeze(2).to_broadcast(pairs), ALU.mult).then_inc(tk.sem, 1)
                        dve.wait_ge(tk.sem, tk.at(b, 5))
                        dve.tensor_tensor(gt[u][:, :, :], g2[:, :, 0, :], g2[:, :, 1, :], ALU.add).then_inc(gt_ok.sem, 1)
                run(dve, slot)


def constants():
    half = np.arange(0, 64, 2, dtype=np.float32)
    inv = (np.float32(1.0) / np.float32(10000.0) ** (half / np.float32(64))).astype(np.float32)
    t = np.arange(SEQ, dtype=np.float32)
    fr = (t[:, None] * inv[None, :]).astype(np.float32)
    fr = np.concatenate([fr, fr], -1)
    base = ((half + np.float32(0.4 * 64)) / np.float32(1.4 * 64)).astype(np.float32)
    power = ((t - SEQ // 2) / np.float32(32.0)).astype(np.float32)
    sc = (base[None, :] ** power[:, None]).astype(np.float32)
    sc = np.concatenate([sc, sc], -1)
    cos, sin = np.cos(fr), np.sin(fr)
    sgn = np.concatenate([-np.ones(32, np.float32), np.ones(32, np.float32)])
    tabs = np.stack([cos * sc * 8, cos / sc, sgn * sin * sc * 8, sgn * sin / sc], 1).astype(np.float32)
    rot = np.ascontiguousarray(tabs.reshape(TB, P, 4, 64).transpose(1, 0, 2, 3))
    r, c = np.arange(P)[:, None], np.arange(P)[None, :]
    rr, cc = r % 64, c % 64
    cur, prev = cc <= rr, cc >= rr
    loc = np.where(r < 64, np.where(c < 64, cur, prev), np.where(c < 64, prev, cur))
    loc0 = loc & ~((r < 64) & (c >= 64))
    neg = lambda ok: np.where(ok, 0.0, MASKED)
    eye = np.eye(P)
    mk = np.stack([neg(loc), neg(loc0), neg(c <= r), neg(r <= c), eye], 1).astype(np.float32)
    shift = (c == r + 1).astype(np.float32)
    carry = ((r == P - 1) & (c == 0)).astype(np.float32)
    return {"rot": rot, "mk": mk, "ident": eye.astype(np.float32), "shift": shift, "carry": carry}


ORDER = ["L0_attn_x", "L0_attn_filt", "L0_ffn_wqkv", "L0_ffn_q_scale", "L0_ffn_k_scale", "L0_ffn_wo", "L0_ffn_ln_g",
         "L0_ffn_ln_b", "L0_ffn_w1", "L0_ffn_b1", "L0_ffn_w2", "L0_ffn_b2", "L1_attn_w_attn", "L1_attn_b_attn",
         "L1_attn_w_proj", "L1_attn_b_proj", "L1_ffn_centroids", "L1_ffn_expert_biases", "L1_ffn_Wr", "L1_ffn_br",
         "L1_ffn_Ws", "L1_ffn_bs"]


def build(nc, inputs):
    arrays = {}

    def give(name, a):
        arrays[name] = np.ascontiguousarray(a)
        return nc.dram_tensor(name, a.shape, mybir.dt.from_np(arrays[name].dtype), kind="ExternalInput").ap()

    args = []
    for name in ORDER:
        a = np.asarray(inputs[name])
        if name == "L1_ffn_centroids":
            a = a.T
        if name in ("L1_ffn_Wr", "L1_ffn_Ws"):
            a = a.transpose(2, 0, 1)
        args.append(give("in_" + name, a))
    k = constants()
    rot = give("c_rot", k["rot"])
    masks = [give("c_" + n, k[n]) for n in ("mk", "ident", "shift", "carry")]
    shape = np.asarray(inputs["L0_attn_x"]).shape
    out = nc.dram_tensor("out_dram", shape, F32, kind="ExternalOutput").ap()
    program(nc, *args, rot, masks, out)
    return arrays


def kernel(**inputs):
    import concourse.bacc as bacc
    from concourse.bass_utils import run_bass_kernel_spmd

    nc = bacc.Bacc("TRN2", target_bir_lowering=False, num_devices=1)
    arrays = build(nc, inputs)
    r = run_bass_kernel_spmd(nc, [arrays], core_ids=[0])
    return r.results[0]["out_dram"]
```
